# Optimizing a Trainium2 kernel written in Bass

```python
import numpy as np
import jax
import jax.numpy as jnp

def _softmax(x, axis=-1):
    return jax.nn.softmax(x, axis=axis)

def _gelu(x):
    return jax.nn.gelu(x, approximate=True)

def _silu(x):
    return jax.nn.silu(x)

def _sigmoid(x):
    return jax.nn.sigmoid(x)

def _layernorm(x, axis=-1, eps=1e-05):
    m = jnp.mean(x, axis=axis, keepdims=True)
    v = jnp.var(x, axis=axis, keepdims=True)
    return (x - m) / jnp.sqrt(v + eps)

def _scatter_add(tgt, idx, src, axis=0):
    return tgt.at[idx].add(src)

def _segment_sum(src, seg, n):
    return jax.ops.segment_sum(src, seg, n)
kernel_name = 'mk_recurrent_d2_jaxref_r4_34e7bc'

def setup_inputs(seed: int=0):
    np.random.seed(seed)
    _w = jnp.asarray

    def _L0_attn_setup():
        import jax, jax.numpy as jnp
        import numpy as np
        B, L, H, N = (4, 1024, 256, 64)
        LN_EPS = 1e-05

        def _s4d_kernel(log_A_real, A_imag, C_re, C_im, log_dt, length):
            A = -jnp.exp(log_A_real) + 1j * A_imag
            dt = jnp.exp(log_dt)[:, None]
            dtA = dt * A
            C = C_re + 1j * C_im
            Ct = C * (jnp.exp(dtA) - 1.0) / A
            l = jnp.arange(length, dtype=jnp.float32)
            V = jnp.exp(dtA[:, :, None] * l[None, None, :])
            K = 2.0 * jnp.real(jnp.einsum('hn,hnl->hl', Ct, V))
            return K
        key = jax.random.key(seed)
        ks = jax.random.split(key, 6)
        x = jax.random.normal(ks[0], (B, L, H), dtype=jnp.float32)
        log_A_real = jnp.log(0.5 * jnp.ones((H, N), dtype=jnp.float32))
        A_imag = jnp.broadcast_to(jnp.pi * jnp.arange(N, dtype=jnp.float32), (H, N))
        C_re = jax.random.normal(ks[1], (H, N), dtype=jnp.float32) * 0.5
        C_im = jax.random.normal(ks[2], (H, N), dtype=jnp.float32) * 0.5
        u = jax.random.uniform(ks[3], (H,), dtype=jnp.float32)
        log_dt = u * (jnp.log(0.1) - jnp.log(0.001)) + jnp.log(0.001)
        D = jax.random.normal(ks[4], (H,), dtype=jnp.float32)
        ln_w = jnp.ones((H,), dtype=jnp.float32)
        ln_b = jnp.zeros((H,), dtype=jnp.float32)
        return {'x': x, 'log_A_real': log_A_real, 'A_imag': A_imag, 'C_re': C_re, 'C_im': C_im, 'log_dt': log_dt, 'D': D, 'ln_w': ln_w, 'ln_b': ln_b}
    _L0_attn_in = _L0_attn_setup()

    def _L0_ffn_setup():
        import jax, jax.numpy as jnp
        import numpy as np
        R = 64
        key = jax.random.key(seed)
        k1, k2, k3 = jax.random.split(key, 3)
        B, S, D_IN, D_OUT = (8, 1024, 256, 256)
        x = jax.random.normal(k1, (B, S, D_IN), dtype=jnp.float32)
        weight = jax.random.normal(k2, (D_OUT, D_IN), dtype=jnp.float32) * (1.0 / np.sqrt(D_IN))
        disha = jax.random.normal(k3, (R, D_OUT), dtype=jnp.float32) * 0.01
        return {'x': x, 'weight': weight, 'disha': disha}
    _L0_ffn_in = _L0_ffn_setup()

    def _L1_attn_setup():
        import jax, jax.numpy as jnp
        import numpy as np
        B, S, C, H = (2, 1024, 256, 8)
        D = C // H
        KCONV = 7

        def _ripple(x, Wqkv, Wo, conv_w):
            b, s, c = x.shape
            d = c // H
            qkv = x @ Wqkv
            q, k, v = jnp.split(qkv, 3, axis=-1)

            def heads(t):
                return t.reshape(b, s, H, d).transpose(0, 2, 1, 3)
            qh, kh, vh = (heads(q), heads(k), heads(v))
            n_pow = int(np.floor(np.log2(s))) + 1
            offsets = jnp.concatenate([jnp.zeros((1,), jnp.int32), (2 ** jnp.arange(n_pow)).astype(jnp.int32)])
            pos = jnp.arange(s, dtype=jnp.int32)[:, None] - offsets[None, :]
            valid = pos >= 0
            posc = jnp.clip(pos, 0)
            kg = kh[:, :, posc]
            vg = vh[:, :, posc]
            sc = jnp.einsum('bhsd,bhskd->bhsk', qh, kg) / np.sqrt(d)
            sc = jnp.where(valid[None, None], sc, -jnp.inf)
            w = jax.nn.softmax(sc, axis=-1)
            tele = jnp.einsum('bhsk,bhskd->bhsd', w, vg)
            vpad = jnp.pad(v, ((0, 0), (KCONV - 1, 0), (0, 0)))
            conv = jax.lax.conv_general_dilated(vpad.transpose(0, 2, 1), conv_w[:, None, :], window_strides=(1,), padding='VALID', feature_group_count=c, dimension_numbers=('NCH', 'OIH', 'NCH')).transpose(0, 2, 1)
            conv_h = conv.reshape(b, s, H, d).transpose(0, 2, 1, 3)
            fq = jax.nn.elu(qh) + 1.0
            fk = jax.nn.elu(kh) + 1.0
            kv = jnp.einsum('bhsd,bhse->bhde', fk, vh)
            z = jnp.einsum('bhsd,bhd->bhs', fq, fk.sum(2))
            low = jnp.einsum('bhsd,bhde->bhse', fq, kv) / (z[..., None] + 1e-06)
            h = (tele + conv_h + low).transpose(0, 2, 1, 3).reshape(b, s, c)
            return h @ Wo
        key = jax.random.key(seed)
        k1, k2, k3, k4 = jax.random.split(key, 4)
        x = jax.random.normal(k1, (B, S, C), jnp.float32)
        Wqkv = jax.random.normal(k2, (C, 3 * C), jnp.float32) * (1.0 / np.sqrt(C))
        Wo = jax.random.normal(k3, (C, C), jnp.float32) * (1.0 / np.sqrt(C))
        conv_w = jax.random.normal(k4, (C, KCONV), jnp.float32) * (1.0 / np.sqrt(KCONV))
        return {'x': x, 'Wqkv': Wqkv, 'Wo': Wo, 'conv_w': conv_w}
    _L1_attn_in = _L1_attn_setup()

    def _L1_ffn_setup():
        import jax, jax.numpy as jnp
        import numpy as np
        TOP_K = 4
        CAP_FACTOR = 4

        def swiglu(x, w1, w2, w3):
            return jax.nn.silu(x @ w1) * (x @ w3) @ w2
        key = jax.random.key(seed)
        ks = jax.random.split(key, 8)
        B, S, D, H, E = (2, 512, 256, 128, 32)
        Hs = 2 * H
        sd = lambda *sh: 1.0 / np.sqrt(sh[-2])
        x = jax.random.normal(ks[0], (B, S, D), dtype=jnp.float32)
        Wg = jax.random.normal(ks[1], (D, E), dtype=jnp.float32) * (1.0 / np.sqrt(D))
        W1 = jax.random.normal(ks[2], (E, D, H), dtype=jnp.float32) * (1.0 / np.sqrt(D))
        W3 = jax.random.normal(ks[3], (E, D, H), dtype=jnp.float32) * (1.0 / np.sqrt(D))
        W2 = jax.random.normal(ks[4], (E, H, D), dtype=jnp.float32) * (1.0 / np.sqrt(H))
        Ws1 = jax.random.normal(ks[5], (D, Hs), dtype=jnp.float32) * (1.0 / np.sqrt(D))
        Ws3 = jax.random.normal(ks[6], (D, Hs), dtype=jnp.float32) * (1.0 / np.sqrt(D))
        Ws2 = jax.random.normal(ks[7], (Hs, D), dtype=jnp.float32) * (1.0 / np.sqrt(Hs))
        return {'x': x, 'Wg': Wg, 'W1': W1, 'W2': W2, 'W3': W3, 'Ws1': Ws1, 'Ws2': Ws2, 'Ws3': Ws3}
    _L1_ffn_in = _L1_ffn_setup()
    _d = {'L0_attn_x': _L0_attn_in['x'], 'L0_attn_log_A_real': _L0_attn_in['log_A_real'], 'L0_attn_A_imag': _L0_attn_in['A_imag'], 'L0_attn_C_re': _L0_attn_in['C_re'], 'L0_attn_C_im': _L0_attn_in['C_im'], 'L0_attn_log_dt': _L0_attn_in['log_dt'], 'L0_attn_D': _L0_attn_in['D'], 'L0_attn_ln_w': _L0_attn_in['ln_w'], 'L0_attn_ln_b': _L0_attn_in['ln_b'], 'L0_ffn_weight': _L0_ffn_in['weight'], 'L0_ffn_disha': _L0_ffn_in['disha'], 'L1_attn_Wqkv': _L1_attn_in['Wqkv'], 'L1_attn_Wo': _L1_attn_in['Wo'], 'L1_attn_conv_w': _L1_attn_in['conv_w'], 'L1_ffn_Wg': _L1_ffn_in['Wg'], 'L1_ffn_W1': _L1_ffn_in['W1'], 'L1_ffn_W2': _L1_ffn_in['W2'], 'L1_ffn_W3': _L1_ffn_in['W3'], 'L1_ffn_Ws1': _L1_ffn_in['Ws1'], 'L1_ffn_Ws2': _L1_ffn_in['Ws2'], 'L1_ffn_Ws3': _L1_ffn_in['Ws3']}
    _x0 = _d['L0_attn_x']
    _d['L0_attn_x'] = jax.random.normal(jax.random.fold_in(jax.random.key(seed), 1), (1, 4096, 256), dtype=_x0.dtype)
    del _x0
    return _d

def reference(L0_attn_x, L0_attn_log_A_real, L0_attn_A_imag, L0_attn_C_re, L0_attn_C_im, L0_attn_log_dt, L0_attn_D, L0_attn_ln_w, L0_attn_ln_b, L0_ffn_weight, L0_ffn_disha, L1_attn_Wqkv, L1_attn_Wo, L1_attn_conv_w, L1_ffn_Wg, L1_ffn_W1, L1_ffn_W2, L1_ffn_W3, L1_ffn_Ws1, L1_ffn_Ws2, L1_ffn_Ws3):

    def _L0_attn_ref(x, log_A_real, A_imag, C_re, C_im, log_dt, D, ln_w, ln_b):
        import jax, jax.numpy as jnp
        import numpy as np
        B, L, H, N = (4, 1024, 256, 64)
        LN_EPS = 1e-05

        def _s4d_kernel(log_A_real, A_imag, C_re, C_im, log_dt, length):
            A = -jnp.exp(log_A_real) + 1j * A_imag
            dt = jnp.exp(log_dt)[:, None]
            dtA = dt * A
            C = C_re + 1j * C_im
            Ct = C * (jnp.exp(dtA) - 1.0) / A
            l = jnp.arange(length, dtype=jnp.float32)
            V = jnp.exp(dtA[:, :, None] * l[None, None, :])
            K = 2.0 * jnp.real(jnp.einsum('hn,hnl->hl', Ct, V))
            return K
        b, length, h = x.shape
        K = _s4d_kernel(log_A_real, A_imag, C_re, C_im, log_dt, length)
        n = 2 * length
        Xf = jnp.fft.rfft(x, n=n, axis=1)
        Kf = jnp.fft.rfft(K, n=n, axis=1)
        y = jnp.fft.irfft(Xf * Kf.T[None, :, :], n=n, axis=1)[:, :length, :]
        z = y + x * D[None, None, :]
        r = x + z
        mu = jnp.mean(r, axis=-1, keepdims=True)
        var = jnp.var(r, axis=-1, keepdims=True)
        out = (r - mu) * jax.lax.rsqrt(var + LN_EPS) * ln_w + ln_b
        return out

    def _L0_ffn_ref(x, weight, disha):
        import jax, jax.numpy as jnp
        import numpy as np
        R = 64
        result = jnp.einsum('bsd,od->bso', x, weight)
        r = disha.shape[0]
        pooled = x.reshape(*x.shape[:-1], x.shape[-1] // r, r).sum(axis=-2)
        return result + pooled @ disha

    def _L1_attn_ref(x, Wqkv, Wo, conv_w):
        import jax, jax.numpy as jnp
        import numpy as np
        B, S, C, H = (2, 1024, 256, 8)
        D = C // H
        KCONV = 7

        def _ripple(x, Wqkv, Wo, conv_w):
            b, s, c = x.shape
            d = c // H
            qkv = x @ Wqkv
            q, k, v = jnp.split(qkv, 3, axis=-1)

            def heads(t):
                return t.reshape(b, s, H, d).transpose(0, 2, 1, 3)
            qh, kh, vh = (heads(q), heads(k), heads(v))
            n_pow = int(np.floor(np.log2(s))) + 1
            offsets = jnp.concatenate([jnp.zeros((1,), jnp.int32), (2 ** jnp.arange(n_pow)).astype(jnp.int32)])
            pos = jnp.arange(s, dtype=jnp.int32)[:, None] - offsets[None, :]
            valid = pos >= 0
            posc = jnp.clip(pos, 0)
            kg = kh[:, :, posc]
            vg = vh[:, :, posc]
            sc = jnp.einsum('bhsd,bhskd->bhsk', qh, kg) / np.sqrt(d)
            sc = jnp.where(valid[None, None], sc, -jnp.inf)
            w = jax.nn.softmax(sc, axis=-1)
            tele = jnp.einsum('bhsk,bhskd->bhsd', w, vg)
            vpad = jnp.pad(v, ((0, 0), (KCONV - 1, 0), (0, 0)))
            conv = jax.lax.conv_general_dilated(vpad.transpose(0, 2, 1), conv_w[:, None, :], window_strides=(1,), padding='VALID', feature_group_count=c, dimension_numbers=('NCH', 'OIH', 'NCH')).transpose(0, 2, 1)
            conv_h = conv.reshape(b, s, H, d).transpose(0, 2, 1, 3)
            fq = jax.nn.elu(qh) + 1.0
            fk = jax.nn.elu(kh) + 1.0
            kv = jnp.einsum('bhsd,bhse->bhde', fk, vh)
            z = jnp.einsum('bhsd,bhd->bhs', fq, fk.sum(2))
            low = jnp.einsum('bhsd,bhde->bhse', fq, kv) / (z[..., None] + 1e-06)
            h = (tele + conv_h + low).transpose(0, 2, 1, 3).reshape(b, s, c)
            return h @ Wo
        return x + _ripple(x, Wqkv, Wo, conv_w)

    def _L1_ffn_ref(x, Wg, W1, W2, W3, Ws1, Ws2, Ws3):
        import jax, jax.numpy as jnp
        import numpy as np
        TOP_K = 4
        CAP_FACTOR = 4

        def swiglu(x, w1, w2, w3):
            return jax.nn.silu(x @ w1) * (x @ w3) @ w2
        B, S, D = x.shape
        E = Wg.shape[1]
        T = B * S
        xf = x.reshape(T, D)
        scores = jax.nn.softmax(xf @ Wg, axis=-1)
        weights, indices = jax.lax.top_k(scores, TOP_K)
        P = T * TOP_K
        pair_expert = indices.reshape(-1)
        pair_token = jnp.repeat(jnp.arange(T), TOP_K)
        pair_weight = weights.reshape(-1).astype(xf.dtype)
        C = CAP_FACTOR * P // E
        y = jnp.zeros_like(xf)
        for e in range(E):
            pos = jnp.nonzero(pair_expert == e, size=C, fill_value=P)[0]
            valid = pos < P
            safe = jnp.minimum(pos, P - 1)
            tok = jnp.where(valid, pair_token[safe], 0)
            w = jnp.where(valid, pair_weight[safe], 0.0)
            xg = xf[tok]
            out = swiglu(xg, W1[e], W2[e], W3[e]) * w[:, None]
            y = y.at[tok].add(out)
        z = swiglu(xf, Ws1, Ws2, Ws3)
        return (y + z).reshape(B, S, D)
    x = L0_attn_x
    xn = _layernorm(x, axis=-1)
    s = _L0_attn_ref(xn, L0_attn_log_A_real, L0_attn_A_imag, L0_attn_C_re, L0_attn_C_im, L0_attn_log_dt, L0_attn_D, L0_attn_ln_w, L0_attn_ln_b)
    g = _silu(_L0_ffn_ref(xn, L0_ffn_weight, L0_ffn_disha))
    x = x + s * g
    xn = _layernorm(x, axis=-1)
    s = _L1_attn_ref(xn, L1_attn_Wqkv, L1_attn_Wo, L1_attn_conv_w)
    g = _silu(_L1_ffn_ref(xn, L1_ffn_Wg, L1_ffn_W1, L1_ffn_W2, L1_ffn_W3, L1_ffn_Ws1, L1_ffn_Ws2, L1_ffn_Ws3))
    x = x + s * g
    return x

_drawn_inputs = setup_inputs


def setup_inputs(seed=0):
    import zlib

    import numpy as np

    out = dict(_drawn_inputs(seed))
    spreads = {'L0_attn_log_A_real': (-0.6931471824645996, 0.577),
     'L0_attn_ln_w': (1.0, 0.2),
     'L0_attn_ln_b': (0.0, 0.1)}
    factors = {}
    for name, (base, spread) in spreads.items():
        noise = np.random.default_rng([zlib.crc32(name.encode()), seed]).standard_normal(out[name].shape)
        drawn = base * np.exp(spread * noise) if base else spread * noise
        out[name] = jnp.asarray(drawn.astype(out[name].dtype))
    for name, factor in factors.items():
        out[name] = (out[name] * factor).astype(out[name].dtype)
    return out
```

```python
from contextlib import ExitStack

import concourse.bass as bass
from concourse import mybir

F32 = mybir.dt.float32
BF16 = mybir.dt.bfloat16
I32 = mybir.dt.int32
U32 = mybir.dt.uint32
ALU = mybir.AluOpType
ACT = mybir.ActivationFunctionType
AX_X = mybir.AxisListType.X

P = 128
T, D = 4096, 256
NC = T // P
NST = 64
GH = 8
NG = P // GH
EPS = 1e-5
PI = 3.14159265358979
TWO_PI = 6.2831850
MAGIC = 12582912.0


class Chain:

    def __init__(self, eng, sem):
        self.eng, self.sem, self.n = eng, sem, 0

    def __call__(self, ins):
        self.n += 1
        ins.then_inc(self.sem, 1)
        self.eng.wait_ge(self.sem, self.n)


class Core:
    used = []

    def __init__(self, nc):
        self.nc, self.stack = nc, ExitStack()

    def __enter__(self):
        return self

    def __exit__(self, *a):
        self.stack.close()

    def sb(self, name, shape, dt=F32):
        return self.stack.enter_context(self.nc.sbuf_tensor(name, shape, dt))

    def ps(self, name, shape, dt=F32):
        return self.stack.enter_context(self.nc.psum_tensor(name, shape, dt))

    def sem(self, name):
        Core.used.append(self.nc.alloc_semaphore(name=name))
        return Core.used[-1]

    def recycle(self):
        self.nc.clear_and_free_semaphores(Core.used)
        self.nc.all_engine_barrier()
        Core.used = []


def moments_to_scale(ve, link, stats, mean, rstd, tmp):
    me, mo = stats[:, :, 1], stats[:, :, 4]
    link(ve.tensor_tensor(mean, me, mo, ALU.add))
    link(ve.tensor_tensor(tmp, me, mo, ALU.subtract))
    link(ve.tensor_scalar(mean, mean, 0.5, None, ALU.mult))
    link(ve.tensor_tensor(tmp, tmp, tmp, ALU.mult))
    link(ve.tensor_tensor(rstd, stats[:, :, 2], stats[:, :, 5], ALU.add))
    link(ve.tensor_scalar(rstd, rstd, 1.0 / D, EPS, ALU.mult, ALU.add))
    link(ve.scalar_tensor_tensor(rstd, tmp, 0.25, rstd, ALU.mult, ALU.add))


def make_identity(pool, link, tile, base=0, step=-1):
    link(pool.memset(tile, 0.0))
    link(pool.affine_select(out=tile, in_=tile, compare_op=ALU.not_equal, fill=1.0, base=base,
                            pattern=[[step, P]], channel_multiplier=1))


def stage_norm_gate0(nc, x, weight, disha, ident, anti, XN, G0, xs_dram):
    ROWS = 1024
    KD = D // P
    with Core(nc) as k:
        X = k.sb("a_x", [P, NC, D])
        wraw = k.sb("a_wraw", [P, KD, D])
        drep = k.sb("a_drep", [P, D])
        weff = k.sb("a_weff", [P, KD, D])
        stats = k.sb("a_stats", [P, NC, 6])
        zero = k.sb("a_zero", [P, ROWS // P * D])
        zeroed, cleared = k.sem("a_zeroed"), k.sem("a_cleared")
        mean = k.sb("a_mean", [P, NC])
        rstd = k.sb("a_rstd", [P, NC])
        tmp = k.sb("a_tmp", [P, NC])
        xf = [k.sb(f"a_xf{b}", [P, D]) for b in range(2)]
        xT = [k.sb(f"a_xT{b}", [P, KD, P]) for b in range(2)]
        tp = [k.ps(f"a_tp{b}", [P, KD, P]) for b in range(2)]
        gp = [k.ps(f"a_gp{b}", [P, D]) for b in range(2)]
        wt = k.ps("a_wt", [P, KD, D])
        x_in = [k.sem(f"a_x_in{i}") for i in range(4)]
        w_in = k.sem("a_w_in")
        pool_link, dve_link = k.sem("a_pool"), k.sem("a_dve")
        ident_ready = k.sem("a_ident_ready")
        wt_ready, weff_ready = k.sem("a_wt_ready"), k.sem("a_weff_ready")
        var_ready, std_ready = k.sem("a_var_ready"), k.sem("a_std_ready")
        xf_ready = k.sem("a_xf_ready")
        tp_ready, xT_ready = k.sem("a_tp_ready"), k.sem("a_xT_ready")
        gp_ready, g_ready = k.sem("a_gp_ready"), k.sem("a_g_ready")
        with nc.Block() as block:

            @block.sync
            def _(sp):
                for i in range(4):
                    c0 = i * NC // 4
                    sp.dma_start(X[:, c0:c0 + NC // 4, :],
                                 x[0, c0 * P:(c0 + NC // 4) * P, :].rearrange("(c s) d -> s c d", s=P)
                                 ).then_inc(x_in[i], 16)
                sp.wait_ge(zeroed, 1)
                for i in range(SLOTS // ROWS):
                    sp.dma_start(xs_dram[i * ROWS:(i + 1) * ROWS, :].rearrange("(p r) d -> p (r d)", p=P), zero[:]
                                 ).then_inc(cleared, 16)
                sp.wait_ge(cleared, 16 * (SLOTS // ROWS))

            @block.gpsimd
            def _(pool):
                link = Chain(pool, pool_link)
                pool.memset(zero[:], 0.0).then_inc(zeroed, 1)
                make_identity(pool, link, ident[:])
                make_identity(pool, link, anti[:], base=-(P - 1), step=1)
                pool.sem_inc(ident_ready, 1)

            @block.vector
            def _(ve):
                link = Chain(ve, dve_link)
                for i in range(4):
                    ve.wait_ge(x_in[i], 16)
                    with ve.Fori(i * NC // 4, (i + 1) * NC // 4) as c:
                        last = ve.bn_stats(stats[:, c, :], X[:, c, :])
                ve.drain()
                moments_to_scale(ve, link, stats, mean[:], rstd[:], tmp[:])
                ve.sem_inc(var_ready, 1)
                ve.wait_ge(std_ready, 1)
                link(ve.reciprocal(rstd[:], rstd[:]))
                ve.wait_ge(w_in, 48)
                ve.wait_ge(wt_ready, 1)
                for j in range(KD):
                    ve.tensor_tensor(weff[:, j, :], wt[:, j, :], drep[:], ALU.add).then_inc(weff_ready, 1)
                for b in range(2):
                    ve.tensor_scalar(xf[b][:], X[:, b, :], mean[:, b:b + 1], rstd[:, b:b + 1],
                                     ALU.subtract, ALU.mult).then_inc(xf_ready, 1)
                    ve.tensor_scalar(XN[:, b, :], X[:, b, :], mean[:, b:b + 1], rstd[:, b:b + 1],
                                     ALU.subtract, ALU.mult)
                with ve.Fori(1, NC // 2) as i:
                    for b in range(2):
                        c = 2 * i + b
                        ve.wait_ge(tp_ready, 2 * i + b - 1)
                        ve.tensor_scalar(xf[b][:], X[:, c, :], mean[:, bass.ds(c, 1)], rstd[:, bass.ds(c, 1)],
                                         ALU.subtract, ALU.mult).then_inc(xf_ready, 1)
                        ve.tensor_scalar(XN[:, c, :], X[:, c, :], mean[:, bass.ds(c, 1)], rstd[:, bass.ds(c, 1)],
                                         ALU.subtract, ALU.mult)

            @block.scalar
            def _(act):
                act.dma_start(wraw[:], weight.rearrange("(j o) d -> o j d", o=P)).then_inc(w_in, 16)
                for j in range(2):
                    act.dma_start(drep[64 * j:64 * j + 64, :], disha).then_inc(w_in, 16)
                act.wait_ge(var_ready, 1)
                act.activation(rstd[:], rstd[:], ACT.Sqrt).then_inc(std_ready, 1)
                act.preload_act_table(ACT.Silu)
                with act.Fori(0, NC // 2) as i:
                    for b in range(2):
                        act.wait_ge(tp_ready, 2 * i + b + 1)
                        act.copy(xT[b][:], tp[b][:]).then_inc(xT_ready, 1)
                    for b in range(2):
                        act.wait_ge(gp_ready, 2 * i + b + 1)
                        act.activation(G0[:, 2 * i + b, :], gp[b][:], ACT.Silu).then_inc(g_ready, 1)

            @block.tensor
            def _(pe):
                pe.wait_ge(ident_ready, 1)
                pe.wait_ge(w_in, 48)
                for j in range(KD):
                    for d in range(KD):
                        last = pe.transpose(wt[:, d, j * P:(j + 1) * P], wraw[:, j, d * P:(d + 1) * P], ident[:])
                last.then_inc(wt_ready, 1)
                pe.wait_ge(weff_ready, KD)
                with pe.Fori(0, NC // 2) as i:
                    for b in range(2):
                        pe.wait_ge(xf_ready, 2 * i + b + 1)
                        for d in range(KD):
                            last = pe.transpose(tp[b][:, d, :], xf[b][:, d * P:(d + 1) * P], ident[:])
                        last.then_inc(tp_ready, 1)
                    for b in range(2):
                        pe.wait_ge(xT_ready, 2 * i + b + 1)
                        for d in range(KD):
                            last = pe.matmul(gp[b][:], xT[b][:, d, :], weff[:, d, :],
                                             start=(d == 0), stop=(d == KD - 1))
                        last.then_inc(gp_ready, 1)




def frac_turns(ve, link, out, turns, tmp):
    link(ve.tensor_scalar(tmp, turns, MAGIC, MAGIC, ALU.add, ALU.subtract))
    link(ve.tensor_tensor(out, turns, tmp, ALU.subtract))


def stage_s4d_constants(nc, log_a_re, a_im, c_re, c_im, log_dt, ident, turns, DP, CMH, CML, MR, MRN, MI, WR, WQ):
    with Core(nc) as k:
        raw = [k.sb(f"b_raw{i}", [P, 2, NST]) for i in range(4)]
        names = ["e1", "ai", "cr", "ci", "dt", "th", "em", "den", "f", "t1", "t2", "t3", "sh", "ch", "re", "im",
                 "xr", "xi", "ctr", "cti", "mag", "decay", "hpi"]
        v = {n: k.sb(f"b_{n}", [P, P])[:] for n in names}
        CM = k.sb("b_cm", [P, P, 2, 2])
        tp = k.ps("b_tp", [P, 4, P])
        raw_in, dt_in = k.sem("b_raw_in"), k.sem("b_dt_in")
        tp_ready, ve_link, act_link = k.sem("b_tp_ready"), k.sem("b_dve"), k.sem("b_act")
        asked, act_done = k.sem("b_asked"), k.sem("b_act_done")
        with nc.Block() as block:

            @block.sync
            def _(sp):
                for i, a in enumerate((log_a_re, a_im, c_re, c_im)):
                    sp.dma_start(raw[i][:], a.rearrange("(g p) n -> p g n", g=2)).then_inc(raw_in, 16)
                for g in range(2):
                    sp.dma_start(v["dt"][g * NST:(g + 1) * NST, :],
                                 log_dt[g * P:(g + 1) * P].partition_broadcast(NST)).then_inc(dt_in, 16)

            @block.tensor
            def _(pe):
                pe.wait_ge(raw_in, 64)
                for i in range(4):
                    last = pe.transpose(tp[:, i, :], raw[i][:].rearrange("p g n -> p (g n)"), ident[:])
                last.then_inc(tp_ready, 1)

            @block.scalar
            def _(act):
                act.wait_ge(tp_ready, 1)
                act.wait_ge(dt_in, 32)
                act.activation(v["e1"], tp[:, 0, :], ACT.Exp).then_inc(act_done, 1)
                act.activation(v["dt"], v["dt"], ACT.Exp).then_inc(act_done, 1)
                act.wait_ge(asked, 1)
                act.activation(v["em"], v["decay"], ACT.Tanh, scale=0.5).then_inc(act_done, 1)
                act.wait_ge(asked, 2)
                act.activation(v["sh"], v["f"], ACT.Sin, scale=TWO_PI).then_inc(act_done, 1)
                act.activation(v["t3"], v["f"], ACT.Abs).then_inc(act_link, 1)
                act.wait_ge(act_link, 1)
                act.activation(v["ch"], v["t3"], ACT.Sin, scale=-TWO_PI, bias=v["hpi"][:, 0:1]).then_inc(act_done, 1)
                act.wait_ge(asked, 3)
                act.activation(v["xi"], v["f"], ACT.Sin, scale=TWO_PI).then_inc(act_done, 1)
                act.activation(v["t3"], v["f"], ACT.Abs).then_inc(act_link, 1)
                act.wait_ge(act_link, 2)
                act.activation(v["xr"], v["t3"], ACT.Sin, scale=-TWO_PI, bias=v["hpi"][:, 0:1]).then_inc(act_done, 1)

            @block.vector
            def _(ve):
                link = Chain(ve, ve_link)
                mul, add, sub = ALU.mult, ALU.add, ALU.subtract

                def tt(o, a, b, op):
                    link(ve.tensor_tensor(o, a, b, op))

                def ts(o, a, s1, s2, op0, op1=ALU.bypass):
                    link(ve.tensor_scalar(o, a, s1, s2, op0, op1))

                link(ve.memset(v["hpi"], PI / 2))
                ve.wait_ge(act_done, 2)
                link(ve.tensor_copy(v["ai"], tp[:, 1, :]))
                link(ve.tensor_copy(v["cr"], tp[:, 2, :]))
                link(ve.tensor_copy(v["ci"], tp[:, 3, :]))
                link(ve.scalar_tensor_tensor(v["decay"], v["e1"], -1.0, v["dt"], mul, mul))
                tt(v["th"], v["ai"], v["dt"], mul)
                ts(turns[:], v["th"], 0.15915494309189535, None, mul)
                ve.sem_inc(asked, 1)
                ts(v["t1"], turns[:], 0.5, None, mul)
                frac_turns(ve, link, v["f"], v["t1"], v["t2"])
                ve.sem_inc(asked, 1)
                ve.wait_ge(act_done, 3)
                ts(v["t1"], v["em"], -1.0, 1.0, mul, add)
                link(ve.reciprocal(v["t1"], v["t1"]))
                link(ve.scalar_tensor_tensor(v["em"], v["em"], 2.0, v["t1"], mul, mul))
                tt(v["t1"], v["e1"], v["e1"], mul)
                tt(v["t2"], v["ai"], v["ai"], mul)
                tt(v["den"], v["t1"], v["t2"], add)
                link(ve.reciprocal(v["den"], v["den"]))
                ve.wait_ge(act_done, 5)
                ts(v["t1"], v["em"], 1.0, None, add)
                tt(v["t2"], v["sh"], v["sh"], mul)
                tt(v["t2"], v["t2"], v["t1"], mul)
                link(ve.scalar_tensor_tensor(v["re"], v["t2"], -2.0, v["em"], mul, add))
                tt(v["t2"], v["sh"], v["ch"], mul)
                link(ve.scalar_tensor_tensor(v["im"], v["t2"], 2.0, v["t1"], mul, mul))
                ts(v["t1"], turns[:], float(P), None, mul)
                frac_turns(ve, link, v["f"], v["t1"], v["t2"])
                ve.sem_inc(asked, 1)
                ve.wait_ge(act_done, 7)
                ts(DP[:, 0, :], v["em"], 1.0, None, add)
                for i in range(6):
                    tt(DP[:, i + 1, :], DP[:, i, :], DP[:, i, :], mul)
                tt(v["mag"], DP[:, 6, :], DP[:, 6, :], mul)
                for r in range(2):
                    tt(WR[:, r, :], v["mag"], v["xr"], mul)
                tt(WQ[:, 0, :], v["mag"], v["xi"], mul)
                ts(WQ[:, 1, :], WQ[:, 0, :], -1.0, None, mul)
                tt(v["t1"], v["re"], v["e1"], mul)
                tt(v["t2"], v["im"], v["ai"], mul)
                tt(v["xr"], v["t2"], v["t1"], sub)
                tt(v["t1"], v["im"], v["e1"], mul)
                tt(v["t2"], v["re"], v["ai"], mul)
                link(ve.scalar_tensor_tensor(v["xi"], v["t1"], -1.0, v["t2"], mul, sub))
                tt(v["xr"], v["xr"], v["den"], mul)
                tt(v["xi"], v["xi"], v["den"], mul)
                tt(v["t1"], v["cr"], v["xr"], mul)
                tt(v["t2"], v["ci"], v["xi"], mul)
                tt(v["t3"], v["t1"], v["t2"], sub)
                ts(v["ctr"], v["t3"], 2.0, None, mul)
                tt(v["t1"], v["cr"], v["xi"], mul)
                tt(v["t2"], v["ci"], v["xr"], mul)
                tt(v["t3"], v["t1"], v["t2"], add)
                ts(v["cti"], v["t3"], 2.0, None, mul)
                tt(v["t1"], v["ctr"], v["re"], mul)
                tt(v["t2"], v["cti"], v["im"], mul)
                tt(v["t3"], v["t1"], v["t2"], sub)
                tt(MR[:], v["t3"], v["ctr"], add)
                ts(MRN[:], MR[:], -1.0, None, mul)
                tt(v["t1"], v["ctr"], v["im"], mul)
                tt(v["t2"], v["cti"], v["re"], mul)
                tt(v["t3"], v["t1"], v["t2"], add)
                tt(MI[:], v["t3"], v["cti"], add)
                link(ve.memset(CM[:], 0.0))
                for g in range(2):
                    q = slice(g * NST, (g + 1) * NST)
                    link(ve.tensor_copy(CM[q, :, 0, g], v["ctr"][q, :]))
                    ts(CM[q, :, 1, g], v["cti"][q, :], -1.0, None, mul)
                link(ve.tensor_copy(CMH[:], CM[:]))
                tt(CML[:], CM[:], CMH[:], sub)


def stage_s4d_states(nc, turns, DP, CMH, CML, MR, MRN, MI, ident, anti, XN, KT, S, v_dram):
    KP = 7
    with Core(nc) as k:
        lag = k.sb("c_lag", [P, P])
        hpi = k.sb("c_hpi", [P, 1])
        ea = [k.sb(f"c_ea{b}", [P, GH, P]) for b in range(2)]
        fr = [k.sb(f"c_fr{b}", [P, GH, P]) for b in range(2)]
        co = [k.sb(f"c_co{b}", [P, GH, P]) for b in range(2)]
        si = [k.sb(f"c_si{b}", [P, GH, P]) for b in range(2)]
        rn = k.sb("c_rn", [P, GH, P])
        V = [k.sb(f"c_v{b}", [P, 2, GH, P]) for b in range(2)]
        VP = [k.sb(f"c_vp{b}", [P, 2, 2, GH, P], BF16) for b in range(2)]
        VT = k.sb("c_vt", [P, 4, 4, P])
        xg = k.sb("c_xg", [P, NC, 2, GH])
        t1, t2 = k.sb("c_t1", [P, GH, NC]), k.sb("c_t2", [P, GH, NC])
        xp = k.ps("c_xp", [P, NC, 2, GH])
        vtp = k.ps("c_vtp", [P, 4, 4, P])
        ktp = k.ps("c_ktp", [P, GH, 2])
        bp = [k.ps(f"c_bp{b}", [P, 2, GH, NC]) for b in range(2)]
        pool_link, ve_link, act_link = k.sem("c_pool"), k.sem("c_dve"), k.sem("c_act")
        st_link, v_half, kt_taken = k.sem("c_sums"), k.sem("c_v_half"), k.sem("c_kt_taken")
        lag_ready, ea_ready = k.sem("c_lag_ready"), k.sem("c_ea_ready")
        fr_ready, trig_ready = k.sem("c_fr_ready"), k.sem("c_trig_ready")
        v_ready, v_stored = k.sem("c_v_ready"), [k.sem(f"c_v_stored{b}") for b in range(2)]
        xp_ready, xg_ready = k.sem("c_xp_ready"), k.sem("c_xg_ready")
        vtp_ready, vt_ready = k.sem("c_vtp_ready"), k.sem("c_vt_ready")
        vh_ready, vl_ready = k.sem("c_vh_ready"), k.sem("c_vl_ready")
        kt_ready, bp_ready, s_ready = k.sem("c_kt_ready"), k.sem("c_bp_ready"), k.sem("c_s_ready")
        lags = lag[:].unsqueeze(1).to_broadcast([P, GH, P])

        def columns(a, g, n):
            return a[:, bass.ds(g * GH, GH)].unsqueeze(2).to_broadcast([P, GH, n])

        def groups(eng, step):
            step(0, 0, 0)
            step(1, 1, 1)
            with eng.Fori(1, NG // 2 - 1) as i:
                for b in range(2):
                    step(2 * i + b, b, 2)
            step(NG - 2, 0, 2)
            step(NG - 1, 1, NG - 1)

        with nc.Block() as block:

            @block.gpsimd
            def _(pool):
                link = Chain(pool, pool_link)
                link(pool.iota(lag[:], pattern=[[1, P]], base=0, channel_multiplier=0,
                               allow_small_or_imprecise_dtypes=True))
                link(pool.memset(hpi[:], PI / 2))
                pool.sem_inc(lag_ready, 1)
                for b in range(2):
                    link(pool.memset(ea[b][:, :, 0:1], 1.0))

                def magnitudes(g, b, wait):
                    if wait:
                        pool.wait_ge(v_ready, g - 1)
                    for m in range(KP):
                        n = 1 << m
                        ins = pool.tensor_tensor(ea[b][:, :, n:2 * n], ea[b][:, :, 0:n],
                                                 columns(DP[:, m, :], g, n), ALU.mult)
                        if m < KP - 1:
                            ins.then_inc(pool_link, 1)
                            pool.wait_ge(pool_link, link.n + (KP - 1) * g + m + 1)
                        else:
                            ins.then_inc(ea_ready, 1)

                def step(g, b, at):
                    if at != NG - 1:
                        magnitudes(g + 1, 1 - b, at >= 1)
                    if at >= 2:
                        pool.wait_ge(v_stored[b], 8 * (g - b) if at == 2 else 8 * (NG - 2))
                        pool.wait_ge(kt_ready, g - 1)
                    pool.wait_ge(vh_ready, g + 1)
                    pool.tensor_tensor(VP[b][:, 1], V[b][:], VP[b][:, 0], ALU.subtract).then_inc(vl_ready, 1)
                magnitudes(0, 0, False)
                groups(pool, step)

            @block.vector
            def _(ve):
                ve.wait_ge(lag_ready, 1)

                def phase(g, b):
                    ve.tensor_tensor(fr[b][:], columns(turns, g, P), lags, ALU.mult).then_inc(ve_link, 1)
                    ve.wait_ge(ve_link, 2 * g + 1)
                    ve.tensor_scalar(rn[:], fr[b][:], MAGIC, MAGIC, ALU.add, ALU.subtract).then_inc(ve_link, 1)
                    ve.wait_ge(ve_link, 2 * g + 2)
                    ve.tensor_tensor(fr[b][:], fr[b][:], rn[:], ALU.subtract).then_inc(fr_ready, 1)

                def add_to_states(g, b):
                    ve.wait_ge(bp_ready, g + 1)
                    br, bi = bp[b][:, 0, :, :], bp[b][:, 1, :, :]
                    for r, (m1, m2) in enumerate(((MR, MI), (MI, MRN))):
                        ve.tensor_tensor(t1[:], br, columns(m1, g, NC), ALU.mult).then_inc(st_link, 1)
                        ve.tensor_tensor(t2[:], bi, columns(m2, g, NC), ALU.mult).then_inc(st_link, 1)
                        ve.wait_ge(st_link, 6 * g + 3 * r + 2)
                        o = S[:, :, r, bass.ds(g * GH, GH)].rearrange("p c h -> p h c")
                        if r == 0:
                            ins = ve.tensor_tensor(o, t1[:], t2[:], ALU.subtract)
                        else:
                            ins = ve.tensor_tensor(o, t2[:], t1[:], ALU.subtract)
                        ins.then_inc(st_link, 1)
                        ve.wait_ge(st_link, 6 * g + 3 * r + 3)
                    ve.sem_inc(s_ready, 1)

                def step(g, b, at):
                    if at != NG - 1:
                        phase(g + 1, 1 - b)
                    ve.wait_ge(ea_ready, g + 1)
                    ve.wait_ge(trig_ready, g + 1)
                    if at >= 2:
                        ve.wait_ge(vl_ready, g - 1)
                    ve.tensor_tensor(V[b][:, 0, :, :], ea[b][:], co[b][:], ALU.mult).then_inc(v_half, 1)
                    ve.tensor_tensor(V[b][:, 1, :, :], ea[b][:], si[b][:], ALU.mult).then_inc(v_ready, 1)
                    if at >= 1:
                        add_to_states(g - 1, 1 - b)
                phase(0, 0)
                groups(ve, step)
                add_to_states(NG - 1, 1)

            @block.scalar
            def _(act):
                act.preload_act_table(ACT.Sin)
                act.wait_ge(lag_ready, 1)

                def trig(g, b, wait):
                    act.wait_ge(fr_ready, g + 1)
                    if wait:
                        act.wait_ge(v_ready, g - 1)
                    act.activation(si[b][:], fr[b][:], ACT.Sin, scale=TWO_PI).then_inc(act_link, 1)
                    act.wait_ge(act_link, 2 * g + 1)
                    act.activation(fr[b][:], fr[b][:], ACT.Abs).then_inc(act_link, 1)
                    act.wait_ge(act_link, 2 * g + 2)
                    act.activation(co[b][:], fr[b][:], ACT.Sin, scale=-TWO_PI, bias=hpi[:]).then_inc(trig_ready, 1)

                def take_taps(g):
                    act.wait_ge(kt_ready, g + 1)
                    act.copy(KT[:, :, bass.ds(g * GH, GH)], ktp[:].rearrange("p h g -> p g h")
                             ).then_inc(kt_taken, 1)

                def step(g, b, at):
                    act.wait_ge(v_ready, g + 1)
                    if at >= 2:
                        act.wait_ge(v_stored[b], 8 * (g - b) if at == 2 else 8 * (NG - 2))
                    act.copy(VP[b][:, 0], V[b][:]).then_inc(vh_ready, 1)
                    if at != NG - 1:
                        trig(g + 1, 1 - b, at >= 1)
                    if at >= 1:
                        act.wait_ge(bp_ready, g)
                    act.wait_ge(xp_ready, g + 1)
                    act.copy(xg[:], xp[:]).then_inc(xg_ready, 1)
                    act.wait_ge(vtp_ready, g + 1)
                    for q in range(4):
                        ins = act.copy(VT[:, q, :, :], vtp[:, q, :, :])
                    ins.then_inc(vt_ready, 1)
                    if at >= 1:
                        take_taps(g - 1)
                trig(0, 0, False)
                groups(act, step)
                take_taps(NG - 1)

            @block.tensor
            def _(pe):
                def taps(g, b, wait):
                    pe.wait_ge(vl_ready, g + 1)
                    if wait:
                        pe.wait_ge(kt_taken, g)
                    for h in range(GH):
                        for n, (r, part, c) in enumerate((r, part, c) for r in range(2)
                                                         for part, c in ((0, CMH), (0, CML), (1, CMH))):
                            last = pe.matmul(ktp[:, h, :], VP[b][:, part, r, h, :], c[:, g * GH + h, r, :],
                                             start=(n == 0), stop=(n == 5))
                    last.then_inc(kt_ready, 1)

                def step(g, b, at):
                    pe.matmul(xp[:], anti[:], XN4[:, :, :, bass.ds(g * GH, GH)],
                              start=True, stop=True).then_inc(xp_ready, 1)
                    pe.wait_ge(v_ready, g + 1)
                    for m in range(2 * GH):
                        last = pe.transpose(vtp[:, m // 4, m % 4, :], V[b][:, m // GH, m % GH, :], ident[:])
                    last.then_inc(vtp_ready, 1)
                    if at >= 1:
                        taps(g - 1, 1 - b, at >= 2)
                    pe.wait_ge(xg_ready, g + 1)
                    pe.wait_ge(vt_ready, g + 1)
                    if at >= 2:
                        pe.wait_ge(s_ready, g - 1)
                    for m in range(2 * GH):
                        for q in range(2):
                            half = slice(q * NST, (q + 1) * NST)
                            last = pe.matmul(bp[b][half, m // GH, m % GH, :], VT[:, m // 4, m % 4, half],
                                             xg[:, :, q, m % GH], start=True, stop=True)
                    last.then_inc(bp_ready, 1)
                XN4 = XN[:].rearrange("p c (g h) -> p c g h", g=2)
                groups(pe, step)
                taps(NG - 1, 1, True)

            @block.sync
            def _(sp):
                def store(g, b, at):
                    sp.wait_ge(vl_ready, g + 1)
                    sp.dma_start(v_dram[g], VP[b][:].rearrange("p t r h l -> p (t r h l)")).then_inc(v_stored[b], 16)
                groups(sp, store)
                for b in range(2):
                    sp.wait_ge(v_stored[b], 8 * NG)


def stage_s4d_scan(nc, WR, WQ, S, KT, ident, kp_dram):
    with Core(nc) as k:
        a, q = k.sb("d_a", [P, 2, P]), k.sb("d_q", [P, 2, P])
        kp = k.sb("d_kp", [P, 2, 2 * P, 2], BF16)
        ktt = k.ps("d_ktt", [P, 2, P])
        link, zeroed, turned = k.sem("d_link"), k.sem("d_zeroed"), k.sem("d_turned")
        kph_ready = k.sem("d_kph_ready")
        kp_ready, kp_stored = k.sem("d_kp_ready"), k.sem("d_kp_stored")
        with nc.Block() as block:

            @block.vector
            def _(ve):
                ve.wait_ge(kph_ready, 1)
                taps = kp[:, :, P - 1:2 * P - 1, :]
                ve.tensor_tensor(taps[:, :, :, 1], ktt[:], taps[:, :, :, 0], ALU.subtract).then_inc(kp_ready, 1)
                with ve.Fori(1, NC - 1) as c:
                    before, here = S[:, c - 1, :, :], S[:, c, :, :]
                    n = 4 * c - 4
                    ve.tensor_tensor(a[:], before, WR[:], ALU.mult).then_inc(link, 1)
                    for r in range(2):
                        ins = ve.tensor_tensor(q[:, r, :], S[:, c - 1, 1 - r, :], WQ[:, r, :], ALU.mult)
                    ins.then_inc(link, 1)
                    ve.wait_ge(link, n + 1)
                    ve.tensor_tensor(a[:], a[:], here, ALU.add).then_inc(link, 1)
                    ve.wait_ge(link, n + 3)
                    ve.tensor_tensor(here, a[:], q[:], ALU.add).then_inc(link, 1)
                    ve.wait_ge(link, n + 4)

            @block.gpsimd
            def _(pool):
                pool.memset(kp[:], 0.0).then_inc(zeroed, 1)

            @block.tensor
            def _(pe):
                for g in range(2):
                    last = pe.transpose(ktt[:, g, :], KT[:, g, :], ident[:])
                last.then_inc(turned, 1)

            @block.scalar
            def _(act):
                act.wait_ge(zeroed, 1)
                act.wait_ge(turned, 1)
                act.copy(kp[:, :, P - 1:2 * P - 1, 0], ktt[:]).then_inc(kph_ready, 1)

            @block.sync
            def _(sp):
                sp.wait_ge(kp_ready, 1)
                sp.dma_start(kp_dram.rearrange("(g h) m -> h g m", g=2),
                             kp[:].rearrange("p g m t -> p g (m t)").bitcast(F32)).then_inc(kp_stored, 16)
                sp.wait_ge(kp_stored, 16)


def stage_s4d_outputs(nc, S, XN, anti, v_dram, kp_dram, Y):
    with Core(nc) as k:
        V = [k.sb(f"e_v{b}", [P, 2, 2, GH, P], BF16) for b in range(2)]
        tz = [k.sb(f"e_tz{b}", [P, 2, GH, P]) for b in range(2)]
        sg = [k.sb(f"e_sg{b}", [P, 2, GH, 2, NC], BF16) for b in range(2)]
        xg = [k.sb(f"e_xg{b}", [P, 2, NC, 2, GH], BF16) for b in range(2)]
        xp = [k.ps(f"e_xp{b}", [P, NC, 2, GH]) for b in range(2)]
        yp = [[k.ps(f"e_yp{b}{q}", [P, GH * 2, NC]) for q in range(2)] for b in range(2)]
        loaded = [k.sem(f"e_loaded{b}") for b in range(2)]
        xp_ready, xh_ready, sh_ready = k.sem("e_xp_ready"), k.sem("e_xh_ready"), k.sem("e_sh_ready")
        xl_ready, sl_ready = k.sem("e_xl_ready"), k.sem("e_sl_ready")
        yp_ready, y_ready = k.sem("e_yp_ready"), k.sem("e_y_ready")
        PARTS = ((0, 0), (0, 1), (1, 0))

        def groups(eng, step):
            for b in range(2):
                step(b, b, True)
            with eng.Fori(1, NG // 2) as i:
                for b in range(2):
                    step(2 * i + b, b, False)

        def states_of(g):
            return S[:, :, :, bass.ds(g * GH, GH)].rearrange("p c r h -> p h r c")

        with nc.Block() as block:

            @block.sync
            def _(sp):
                def load(g, b, first):
                    if not first:
                        sp.wait_ge(yp_ready, g - 1)
                    sp.dma_start(V[b][:].rearrange("p t r h l -> p (t r h l)"), v_dram[g]).then_inc(loaded[b], 16)
                    for q in range(2):
                        rows = bass.AP(kp_dram.tensor, (q * P + g * GH) * 2 * P, [[1, P], [2 * P, GH], [1, P]])
                        sp.dma_start(tz[b][:, q, :, :], rows).then_inc(loaded[b], 16)
                groups(sp, load)

            @block.scalar
            def _(act):
                def step(g, b, first):
                    if not first:
                        act.wait_ge(yp_ready, g - 1)
                    act.wait_ge(xp_ready, g + 1)
                    act.copy(xg[b][:, 0], xp[b][:]).then_inc(xh_ready, 1)
                    act.copy(sg[b][:, 0], states_of(g)).then_inc(sh_ready, 1)
                groups(act, step)

            @block.gpsimd
            def _(pool):
                def step(g, b, first):
                    pool.wait_ge(sh_ready, g + 1)
                    pool.tensor_tensor(sg[b][:, 1], states_of(g), sg[b][:, 0], ALU.subtract).then_inc(sl_ready, 1)
                groups(pool, step)

            @block.tensor
            def _(pe):
                XN4 = XN[:].rearrange("p c (g h) -> p c g h", g=2)

                def turn(g, b):
                    pe.matmul(xp[b][:], anti[:], XN4[:, :, :, bass.ds(g * GH, GH)],
                              start=True, stop=True).then_inc(xp_ready, 1)

                def outputs(g, b, first):
                    pe.wait_ge(xl_ready, g + 1)
                    pe.wait_ge(sl_ready, g + 1)
                    pe.wait_ge(loaded[b], 24 * (g - b) + 48)
                    if not first:
                        pe.wait_ge(y_ready, g - 1)
                    for h in range(GH):
                        for q in range(2):
                            rows = slice(q * NST, (q + 1) * NST)
                            o = yp[b][q][:, h, :]
                            taps = tz[b][:, q, h, :].bitcast(BF16).rearrange("p (l t) -> p t l", t=2)
                            for n, (i, j) in enumerate(PARTS):
                                pe.matmul(o, taps[:, i, :], xg[b][:, j, :, q, h], start=(n == 0), stop=False)
                            for n, (r, i, j) in enumerate((r, i, j) for r in range(2) for i, j in PARTS):
                                last = pe.matmul(o[:, 1:NC], V[b][rows, i, r, h, :], sg[b][rows, j, h, r, 0:NC - 1],
                                                 start=False, stop=(n == 5))
                    last.then_inc(yp_ready, 1)

                turn(0, 0)
                turn(1, 1)
                for b in range(2):
                    outputs(b, b, True)
                    turn(2 + b, b)
                with pe.Fori(1, NG // 2 - 1) as i:
                    for b in range(2):
                        outputs(2 * i + b, b, False)
                        turn(2 * i + b + 2, b)
                outputs(NG - 2, 0, False)
                outputs(NG - 1, 1, False)

            @block.vector
            def _(ve):
                Y4 = Y[:].rearrange("p c (g h) -> p g h c", g=2)

                def part(g, b):
                    ve.wait_ge(xh_ready, g + 1)
                    ve.tensor_tensor(xg[b][:, 1], xp[b][:], xg[b][:, 0], ALU.subtract).then_inc(xl_ready, 1)

                def take(g, b):
                    ve.wait_ge(yp_ready, g + 1)
                    for q in range(2):
                        ins = ve.tensor_copy(Y4[:, q, bass.ds(g * GH, GH), :], yp[b][q][:, 0:GH, :])
                    ins.then_inc(y_ready, 1)

                part(0, 0)
                part(1, 1)
                with ve.Fori(0, NG // 2 - 1) as i:
                    for b in range(2):
                        take(2 * i + b, b)
                        part(2 * i + b + 2, b)
                take(NG - 2, 0)
                take(NG - 1, 1)


def stage_mix0(nc, x, d_skip, ln_w, ln_b, XN, G0, Y, x1_dram, xn1_dram):
    BC = 4
    NBK = NC // BC
    with Core(nc) as k:
        d1, lw, lb = k.sb("f_d1", [P, D]), k.sb("f_lw", [P, D]), k.sb("f_lb", [P, D])
        xr = [k.sb(f"f_xr{b}", [P, BC, D]) for b in range(2)]
        stats = k.sb("f_stats", [P, NC, 6])
        mean, rstd, tmp = k.sb("f_mean", [P, NC]), k.sb("f_rstd", [P, NC]), k.sb("f_tmp", [P, NC])
        shift = k.sb("f_shift", [P, NC])
        rows_in = k.sem("f_rows_in")
        x_in = [k.sem(f"f_x_in{b}") for b in range(2)]
        ve_link, d1_ready = k.sem("f_dve"), k.sem("f_d1_ready")
        skip_ready, var_ready, std_ready = k.sem("f_skip_ready"), k.sem("f_var_ready"), k.sem("f_std_ready")
        scale_ready, norm_ready, lnw_ready = k.sem("f_scale_ready"), k.sem("f_norm_ready"), k.sem("f_lnw_ready")
        x1_ready, xn1_ready, stored = k.sem("f_x1_ready"), k.sem("f_xn1_ready"), k.sem("f_stored")
        out_link = k.sem("f_out_link")

        def rows(a):
            return a[:].unsqueeze(1).to_broadcast([P, BC, D])

        def block_of(a, i):
            return a[:, bass.ds(i * BC, BC), :]

        def dram_block(a, i):
            return a[bass.ds(i * BC * P, BC * P), :].rearrange("(c s) d -> s c d", s=P)

        with nc.Block() as block:

            @block.sync
            def _(sp):
                for dst, src in ((d1, d_skip), (lw, ln_w), (lb, ln_b)):
                    sp.dma_start(dst[:], src.partition_broadcast(P)).then_inc(rows_in, 16)
                for b in range(2):
                    sp.dma_start(xr[b][:], dram_block(x[0], b)).then_inc(x_in[b], 16)
                with sp.Fori(1, NBK // 2) as i:
                    for b in range(2):
                        sp.wait_ge(x1_ready, 2 * i + b - 1)
                        sp.dma_start(xr[b][:], dram_block(x[0], 2 * i + b)).then_inc(x_in[b], 16)

            @block.gpsimd
            def _(pool):
                pool.wait_ge(d1_ready, 1)
                with pool.Fori(0, NBK) as i:
                    pool.tensor_tensor(block_of(XN, i), block_of(XN, i), rows(d1), ALU.mult).then_inc(skip_ready, 1)
                with pool.Fori(0, NBK) as i:
                    pool.wait_ge(norm_ready, i + 1)
                    pool.tensor_tensor(block_of(Y, i), block_of(Y, i), rows(lw), ALU.mult).then_inc(lnw_ready, 1)

            @block.scalar
            def _(act):
                act.preload_act_table(ACT.Sqrt)
                act.wait_ge(var_ready, 1)
                act.activation(rstd[:], rstd[:], ACT.Sqrt).then_inc(std_ready, 1)
                act.wait_ge(scale_ready, 1)
                with act.Fori(0, NBK) as i:
                    for j in range(BC):
                        c = i * BC + j
                        ins = act.activation(Y[:, c, :], Y[:, c, :], ACT.Identity, bias=shift[:, bass.ds(c, 1)],
                                             scale=rstd[:, bass.ds(c, 1)])
                    ins.then_inc(norm_ready, 1)
                with act.Fori(0, NBK) as i:
                    act.wait_ge(x1_ready, i + 1)
                    act.dma_start(dram_block(x1_dram, i), block_of(Y, i)).then_inc(stored, 16)
                act.wait_ge(var_ready, 2)
                act.activation(rstd[:], rstd[:], ACT.Sqrt).then_inc(std_ready, 1)
                with act.Fori(0, NBK) as i:
                    act.wait_ge(xn1_ready, i + 1)
                    act.dma_start(dram_block(xn1_dram, i), block_of(XN, i)).then_inc(stored, 16)
                act.wait_ge(stored, 32 * NBK)

            @block.vector
            def _(ve):
                link = Chain(ve, ve_link)
                ve.wait_ge(rows_in, 48)
                ve.tensor_scalar(d1[:], d1[:], 1.0, None, ALU.add).then_inc(d1_ready, 1)

                def statistics(src, i):
                    for j in range(BC):
                        ve.bn_stats(stats[:, i * BC + j, :], src[:, i * BC + j, :])

                def scales(n):
                    ve.drain()
                    moments_to_scale(ve, link, stats, mean[:], rstd[:], tmp[:])
                    ve.sem_inc(var_ready, 1)
                    ve.wait_ge(std_ready, n)
                    link(ve.reciprocal(rstd[:], rstd[:]))
                    link(ve.scalar_tensor_tensor(shift[:], mean[:], -1.0, rstd[:], ALU.mult, ALU.mult))

                with ve.Fori(0, NBK) as i:
                    ve.wait_ge(skip_ready, i + 1)
                    ve.tensor_tensor(block_of(Y, i), block_of(Y, i), block_of(XN, i), ALU.add).then_inc(out_link, 1)
                    ve.wait_ge(out_link, i + 1)
                    statistics(Y, i)
                scales(1)
                ve.sem_inc(scale_ready, 1)
                with ve.Fori(0, NBK // 2) as i:
                    for b in range(2):
                        n = 2 * i + b
                        y = block_of(Y, n)
                        ve.wait_ge(lnw_ready, n + 1)
                        ve.tensor_tensor(y, y, rows(lb), ALU.add).then_inc(out_link, 1)
                        ve.wait_ge(out_link, 2 * n + NBK + 1)
                        ve.tensor_tensor(y, y, block_of(G0, n), ALU.mult).then_inc(out_link, 1)
                        ve.wait_ge(out_link, 2 * n + NBK + 2)
                        ve.wait_ge(x_in[b], 16 * i + 16)
                        ve.tensor_tensor(y, y, xr[b][:], ALU.add).then_inc(x1_ready, 1)
                        ve.wait_ge(x1_ready, n + 1)
                        statistics(Y, n)
                scales(2)
                with ve.Fori(0, NBK) as i:
                    for j in range(BC):
                        c = i * BC + j
                        ins = ve.tensor_scalar(XN[:, c, :], Y[:, c, :], mean[:, bass.ds(c, 1)],
                                               rstd[:, bass.ds(c, 1)], ALU.subtract, ALU.mult)
                    ins.then_inc(xn1_ready, 1)

NJ = T // P
NH, DH = 8, 32
NE, TOPK = 32, 4
HM, HS = 128, 256
CAP = 4 * T * TOPK // NE
GT = 256
NGR = T * TOPK // GT + NE
SLOTS = NGR * GT
SHIFTS = [64, 32, 16, 8, 4, 2, 1, 0]
OFFSETS = [0] + [1 << i for i in range(12)]
KCONV = 7
FAR = 1.0e30


def token_rows(a, j):
    return a.rearrange("(p j) d -> p j d", j=NJ)[:, bass.ds(j, 1), :].rearrange("p a d -> p (a d)")


def by_twos(eng, n, step):
    for b in range(2):
        step(b, b, True)
    with eng.Fori(1, n // 2) as i:
        for b in range(2):
            step(2 * i + b, b, False)


def stage_projections(nc, w_qkv, w_gate, ws1, ws2, ws3, xn1_dram, z_dram, ident, Q, K, V, L, KVB):
    KD = D // P
    with Core(nc) as k:
        wqv, wkg = k.sb("g_wqv", [P, KD, 2 * D]), k.sb("g_wkg", [P, KD, D + NE])
        w1s, w3s, w2s = k.sb("g_w1", [P, KD, HS]), k.sb("g_w3", [P, KD, HS]), k.sb("g_w2", [P, KD, D])
        xf = [k.sb(f"g_xf{b}", [P, D]) for b in range(2)]
        xT = [k.sb(f"g_xT{b}", [P, KD, P]) for b in range(2)]
        low = [k.sb(f"g_low{b}", [P, D]) for b in range(2)]
        fk = [k.sb(f"g_fk{b}", [P, D]) for b in range(2)]
        vs = [k.sb(f"g_vs{b}", [P, D + 1]) for b in range(2)]
        th = [k.sb(f"g_th{b}", [P, KD, P]) for b in range(2)]
        gate = [k.sb(f"g_gate{b}", [P, KD, P]) for b in range(2)]
        zs = [k.sb(f"g_zs{b}", [P, D]) for b in range(2)]
        tp = k.ps("g_tp", [P, KD, P])
        qvp = [k.ps(f"g_qvp{b}", [P, 2 * D]) for b in range(2)]
        kgp = k.ps("g_kgp", [P, D + NE])
        hp = k.ps("g_hp", [P, 2, KD, P])
        zp = k.ps("g_zp", [P, D])
        kv = [k.ps(f"g_kv{m}", [P, 2 * D]) for m in range(KD)]
        w_in, x_in = k.sem("g_w_in"), [k.sem(f"g_x_in{b}") for b in range(2)]
        ones_ready = k.sem("g_ones_ready")
        tp_ready, xT_ready, qv_ready, kg_ready = (k.sem(f"g_{n}_ready") for n in ("tp", "xT", "qv", "kg"))
        h_ready, th_ready, gate_ready, z_ready = (k.sem(f"g_{n}_ready") for n in ("h", "th", "gate", "z"))
        low_ready, ex_ready, fk_ready, vs_ready = (k.sem(f"g_{n}_ready") for n in ("low", "ex", "fk", "vs"))
        zs_ready, z_stored = k.sem("g_zs_ready"), [k.sem(f"g_z_stored{b}") for b in range(2)]
        kv_done, half_gate, v_copied = k.sem("g_kv_done"), k.sem("g_half_gate"), k.sem("g_v_copied")
        q_taken = k.sem("g_q_taken")

        def heads(a, j):
            return a[:, :, bass.ds(j, 1), :].rearrange("p h a d -> p h (a d)")

        with nc.Block() as block:

            @block.sync
            def _(sp):
                def step(j, b, first):
                    if not first:
                        sp.wait_ge(tp_ready, j - 1)
                    sp.dma_start(xf[b][:], token_rows(xn1_dram, j)).then_inc(x_in[b], 16)
                    if not first:
                        sp.wait_ge(zs_ready, j - 1)
                        sp.dma_start(token_rows(z_dram, j - 2), zs[b][:]).then_inc(z_stored[b], 16)
                for i in range(2):
                    sp.dma_start(wqv[:, :, i * D:(i + 1) * D],
                                 w_qkv[:, 2 * i * D:2 * i * D + D].rearrange("(k p) n -> p k n", p=P)
                                 ).then_inc(w_in, 16)
                by_twos(sp, NJ, step)
                for b in range(2):
                    sp.wait_ge(zs_ready, NJ - 1 + b)
                    sp.dma_start(token_rows(z_dram, NJ - 2 + b), zs[b][:]).then_inc(z_stored[b], 16)
                for b in range(2):
                    sp.wait_ge(z_stored[b], 8 * NJ)

            @block.gpsimd
            def _(pool):
                for b in range(2):
                    pool.memset(vs[b][:, D:D + 1], 1.0)
                pool.memset(KVB[:], 0.0).then_inc(ones_ready, 1)

                def step(j, b, first):
                    pool.wait_ge(vs_ready, j + 1)
                    pool.tensor_copy(heads(V, j), vs[b][:, 0:D].rearrange("p (h d) -> p h d", h=NH)
                                     ).then_inc(v_copied, 1)
                by_twos(pool, NJ, step)

            @block.tensor
            def _(pe):
                pe.wait_ge(w_in, 112)
                pe.wait_ge(ones_ready, 1)

                def transposes(j, b):
                    pe.wait_ge(x_in[b], 8 * (j - b) + 16)
                    for d in range(KD):
                        last = pe.transpose(tp[:, d, :], xf[b][:, d * P:(d + 1) * P], ident[:])
                    last.then_inc(tp_ready, 1)

                def products(j, b, first):
                    pe.wait_ge(xT_ready, j + 1)
                    if first < 2:
                        pe.wait_ge(q_taken, j - 1)
                    for d in range(KD):
                        last = pe.matmul(qvp[b][:], xT[b][:, d, :], wqv[:, d, :], start=(d == 0), stop=(d == KD - 1))
                    last.then_inc(qv_ready, 1)
                    if first < 3:
                        pe.wait_ge(fk_ready, j)
                    for d in range(KD):
                        last = pe.matmul(kgp[:], xT[b][:, d, :], wkg[:, d, :], start=(d == 0), stop=(d == KD - 1))
                    last.then_inc(kg_ready, 1)
                    if first < 3:
                        pe.wait_ge(gate_ready, j)
                    for s, w in enumerate((w1s, w3s)):
                        for m in range(KD):
                            for d in range(KD):
                                last = pe.matmul(hp[:, s, m, :], w[:, d, m * P:(m + 1) * P], xT[b][:, d, :],
                                                 start=(d == 0), stop=(d == KD - 1))
                    last.then_inc(h_ready, 1)

                def sums(j, b, at):
                    pe.wait_ge(fk_ready, j + 1)
                    pe.wait_ge(vs_ready, j + 1)
                    for m in range(KD):
                        last = pe.matmul(kv[m][:, 0:D + 1], fk[b][:, m * P:(m + 1) * P], vs[b][:],
                                         start=(at == 0), stop=(at == 2), skip_group_check=True)
                    last.then_inc(kv_done, 1)
                    pe.wait_ge(gate_ready, j + 1)
                    if at:
                        pe.wait_ge(zs_ready, j)
                    for m in range(KD):
                        last = pe.matmul(zp[:], gate[b][:, m, :], w2s[:, m, :], start=(m == 0), stop=(m == KD - 1))
                    last.then_inc(z_ready, 1)

                transposes(0, 0)
                products(0, 0, 3)
                transposes(1, 1)
                products(1, 1, 2)
                sums(0, 0, 0)
                with pe.Fori(1, NJ // 2) as i:
                    for b in range(2):
                        j = 2 * i + b
                        transposes(j, b)
                        products(j, b, 0)
                        sums(j - 1, 1 - b, 1)
                sums(NJ - 1, 1, 2)

            @block.scalar
            def _(act):
                act.dma_start(wkg[:, :, 0:D], w_qkv[:, D:2 * D].rearrange("(k p) n -> p k n", p=P)
                              ).then_inc(w_in, 16)
                act.dma_start(wkg[:, :, D:D + NE], w_gate.rearrange("(k p) n -> p k n", p=P)).then_inc(w_in, 16)
                for dst, src in ((w1s, ws1), (w3s, ws3), (w2s, ws2)):
                    act.dma_start(dst[:], src.rearrange("(k p) n -> p k n", p=P)).then_inc(w_in, 16)
                act.preload_act_table(ACT.Exp)

                def store_z(j, b, wait):
                    act.wait_ge(z_ready, j + 1)
                    if wait:
                        act.wait_ge(z_stored[b], 8 * (j - b))
                    act.mul(zs[b][:], zp[:], 0.5).then_inc(zs_ready, 1)

                def step(j, b, first):
                    act.wait_ge(tp_ready, j + 1)
                    act.copy(xT[b][:], tp[:]).then_inc(xT_ready, 1)
                    act.wait_ge(qv_ready, j + 1)
                    if not first:
                        act.wait_ge(v_copied, j - 1)
                        act.wait_ge(kv_done, j - 1)
                    act.copy(vs[b][:, 0:D], qvp[b][:, D:2 * D]).then_inc(vs_ready, 1)
                    act.copy(heads(Q, j), qvp[b][:, 0:D].rearrange("p (h d) -> p h d", h=NH)).then_inc(q_taken, 1)
                    act.wait_ge(low_ready, j + 1)
                    act.activation(low[b][:], low[b][:], ACT.Exp).then_inc(ex_ready, 1)
                    act.wait_ge(h_ready, j + 1)
                    act.activation(th[b][:], hp[:, 0, :, :], ACT.Tanh, scale=0.5).then_inc(th_ready, 1)

                for b in range(2):
                    step(b, b, True)
                store_z(0, 0, False)
                step(2, 0, False)
                store_z(1, 1, False)
                step(3, 1, False)
                with act.Fori(2, NJ // 2) as i:
                    for b in range(2):
                        j = 2 * i + b
                        store_z(j - 2, b, True)
                        step(j, b, False)
                store_z(NJ - 2, 0, True)
                store_z(NJ - 1, 1, True)

            @block.vector
            def _(ve):
                def step(j, b, first):
                    ve.wait_ge(kg_ready, j + 1)
                    kj = kgp[:, 0:D]
                    ve.tensor_scalar(low[b][:], kj, 0.0, None, ALU.min).then_inc(low_ready, 1)
                    ve.tensor_copy(heads(K, j), kj.rearrange("p (h d) -> p h d", h=NH))
                    ve.tensor_copy(L[:, bass.ds(j, 1), :].rearrange("p a e -> p (a e)"), kgp[:, D:D + NE])
                    ve.wait_ge(ex_ready, j + 1)
                    if not first:
                        ve.wait_ge(kv_done, j - 1)
                    ve.scalar_tensor_tensor(fk[b][:], kj, 0.0, low[b][:], ALU.max, ALU.add).then_inc(fk_ready, 1)
                    ve.wait_ge(th_ready, j + 1)
                    ve.scalar_tensor_tensor(th[b][:], th[b][:], 1.0, hp[:, 0, :, :], ALU.add, ALU.mult
                                            ).then_inc(half_gate, 1)
                    ve.wait_ge(half_gate, j + 1)
                    if not first:
                        ve.wait_ge(z_ready, j - 1)
                    ve.tensor_tensor(gate[b][:], th[b][:], hp[:, 1, :, :], ALU.mult).then_inc(gate_ready, 1)
                by_twos(ve, NJ, step)
                ve.wait_ge(kv_done, NJ)
                ve.wait_ge(ones_ready, 1)
                for h in range(NH):
                    m, q = h // 4, slice(DH * (h % 4), DH * (h % 4) + DH)
                    ve.tensor_copy(KVB[q, m, q], kv[m][q, h * DH:(h + 1) * DH])
                    ve.tensor_copy(KVB[q, m, P + h % 4:P + h % 4 + 1], kv[m][q, D:D + 1])


def stage_routing(nc, L, WK, SIDX, GIDX, EXP):
    with Core(nc) as k:
        one = [P, NJ, NE]
        E, A, B, OH = k.sb("h_e", one), k.sb("h_a", one), k.sb("h_b", one), k.sb("h_oh", one)
        SL, PR = k.sb("h_sl", one), k.sb("h_pr", one)
        G1 = k.sb("h_g1", [P, NGR, NE])
        M8, I8 = k.sb("h_m8", [P, NJ, 8]), k.sb("h_i8", [P, NJ, 8], U32)
        IF = k.sb("h_if", [P, NJ, 8])
        mx, POS, KEPT = k.sb("h_mx", [P, NJ]), k.sb("h_pos", [P, NJ, TOPK]), k.sb("h_kept", [P, NJ, TOPK])
        ie, ig = k.sb("h_ie", [P, NE]), k.sb("h_ig", [P, NGR])
        tri, ones = k.sb("h_tri", [P, P]), k.sb("h_ones", [P, P])
        ng, sa, sb_, ex = k.sb("h_ng", [P, NE]), k.sb("h_sa", [P, NE]), k.sb("h_sb", [P, NE]), k.sb("h_ex", [P, NGR])
        cnt = k.ps("h_cnt", [P, 2, NE])
        pl, vl, const_ready = k.sem("h_pl"), k.sem("h_vl"), k.sem("h_const")
        shifted, exped, tot_ready, cnt_ready = (k.sem(f"h_{n}") for n in ("shifted", "exped", "tot", "cnt"))
        with nc.Block() as block:

            @block.gpsimd
            def _(pool):
                link = Chain(pool, pl)
                link(pool.iota(ie[:], pattern=[[1, NE]], base=0, channel_multiplier=0,
                               allow_small_or_imprecise_dtypes=True))
                link(pool.iota(ig[:], pattern=[[1, NGR]], base=0, channel_multiplier=0,
                               allow_small_or_imprecise_dtypes=True))
                link(pool.memset(ones[:], 1.0))
                link(pool.affine_select(out=tri[:], in_=ones[:], compare_op=ALU.is_ge, fill=0.0, base=-1,
                                        pattern=[[1, P]], channel_multiplier=-1))
                pool.sem_inc(const_ready, 1)

            @block.scalar
            def _(act):
                act.wait_ge(shifted, 1)
                act.activation(E[:], E[:], ACT.Exp).then_inc(exped, 1)

            @block.tensor
            def _(pe):
                pe.wait_ge(const_ready, 1)
                pe.wait_ge(tot_ready, 1)
                pe.matmul(cnt[:, 0, :], tri[:], sa[:], start=True, stop=True)
                pe.matmul(cnt[:, 1, :], ones[:], sa[:], start=True, stop=True).then_inc(cnt_ready, 1)

            @block.vector
            def _(ve):
                link = Chain(ve, vl)

                def tt(o, a, b, op):
                    link(ve.tensor_tensor(o, a, b, op))

                def ts(o, a, s1, s2, op0, op1=ALU.bypass):
                    link(ve.tensor_scalar(o, a, s1, s2, op0, op1))

                def over_e(a):
                    return a.unsqueeze(2).to_broadcast(one)

                def over_j(a):
                    return a.unsqueeze(1).to_broadcast(one)

                link(ve.tensor_reduce(mx[:], L[:], AX_X, ALU.max))
                ve.tensor_tensor(E[:], L[:], over_e(mx[:]), ALU.subtract).then_inc(shifted, 1)
                ve.wait_ge(exped, 1)
                link(ve.tensor_reduce(mx[:], E[:], AX_X, ALU.add))
                link(ve.reciprocal(mx[:], mx[:]))
                tt(E[:], E[:], over_e(mx[:]), ALU.mult)
                for j in range(NJ):
                    ve.max(M8[:, j, :], E[:, j, :])
                ve.drain()
                for j in range(NJ):
                    ve.max_index(I8[:, j, :], M8[:, j, :], E[:, j, :])
                ve.drain()
                link(ve.tensor_copy(IF[:], I8[:]))
                ve.wait_ge(const_ready, 1)
                for n in range(TOPK):
                    tt(OH[:], over_j(ie[:]), over_e(IF[:, :, n]), ALU.is_equal)
                    if n == 0:
                        link(ve.tensor_copy(A[:], OH[:]))
                    else:
                        tt(A[:], A[:], OH[:], ALU.add)
                link(ve.tensor_copy(SL[:], A[:]))
                a, b, s = A, B, 1
                while s < NJ:
                    link(ve.tensor_copy(b[:, 0:s, :], a[:, 0:s, :]))
                    tt(b[:, s:NJ, :], a[:, s:NJ, :], a[:, 0:NJ - s, :], ALU.add)
                    a, b, s = b, a, 2 * s
                link(ve.tensor_copy(sa[:], a[:, NJ - 1, :]))
                ve.sem_inc(tot_ready, 1)
                ve.wait_ge(cnt_ready, 1)
                tt(a[:], a[:], SL[:], ALU.subtract)
                tt(a[:], a[:], over_j(cnt[:, 0, :]), ALU.add)
                ts(ng[:], cnt[:, 1, :], float(CAP), None, ALU.min)
                ts(ng[:], ng[:], 1.0 / GT, (GT - 1.0) / GT - 0.5 + 0.5 / GT, ALU.mult, ALU.add)
                ts(ng[:], ng[:], MAGIC, MAGIC, ALU.add, ALU.subtract)
                link(ve.tensor_copy(sa[:], ng[:]))
                c, d, s = sa, sb_, 1
                while s < NE:
                    link(ve.tensor_copy(d[:, 0:s], c[:, 0:s]))
                    tt(d[:, s:NE], c[:, s:NE], c[:, 0:NE - s], ALU.add)
                    c, d, s = d, c, 2 * s
                tt(G1[:], c[:].unsqueeze(1).to_broadcast([P, NGR, NE]), ig[:].unsqueeze(2).to_broadcast([P, NGR, NE]),
                   ALU.is_le)
                link(ve.tensor_reduce(ex[:], G1[:], AX_X, ALU.add))
                ts(ex[:], ex[:], NE - 1.0, None, ALU.min)
                link(ve.tensor_copy(EXP[:], ex[:]))
                tt(d[:], c[:], ng[:], ALU.subtract)
                ts(d[:], d[:], float(GT), None, ALU.mult)
                ts(SL[:], a[:], float(CAP), 4.0 * SLOTS, ALU.is_ge, ALU.mult)
                tt(SL[:], SL[:], a[:], ALU.add)
                tt(SL[:], SL[:], over_j(d[:]), ALU.add)
                for n in range(TOPK):
                    tt(OH[:], over_j(ie[:]), over_e(IF[:, :, n]), ALU.is_equal)
                    tt(PR[:], OH[:], SL[:], ALU.mult)
                    link(ve.tensor_reduce(POS[:, :, n], PR[:], AX_X, ALU.add))
                link(ve.tensor_copy(SIDX[:], POS[:]))
                ts(KEPT[:], POS[:], float(SLOTS), None, ALU.is_lt)
                tt(WK[:], M8[:, :, 0:TOPK], KEPT[:], ALU.mult)
                tt(POS[:], POS[:], KEPT[:], ALU.mult)
                link(ve.tensor_copy(GIDX[:], POS[:]))


def stage_scatter(nc, xn1_dram, xs_dram, SIDX):
    with Core(nc) as k:
        xr = [k.sb(f"i_x{b}", [P, D]) for b in range(2)]
        ix = [k.sb(f"i_ix{b}", [P, TOPK], U32) for b in range(2)]
        x_in = [k.sem(f"i_x_in{b}") for b in range(2)]
        ix_ready, sent = k.sem("i_ix_ready"), [k.sem(f"i_sent{b}") for b in range(2)]
        waited = k.sem("i_waited")
        with nc.Block() as block:

            @block.sync
            def _(sp):
                def step(j, b, first):
                    if not first:
                        sp.wait_ge(sent[b], 8 * TOPK * (j - b))
                    sp.dma_start(xr[b][:], token_rows(xn1_dram, j)).then_inc(x_in[b], 16)
                by_twos(sp, NJ, step)

            @block.gpsimd
            def _(pool):
                def step(j, b, first):
                    if not first:
                        pool.wait_ge(sent[b], 8 * TOPK * (j - b))
                        pool.sem_inc(waited, 1)
                    pool.tensor_copy(ix[b][:], SIDX[:, bass.ds(j, 1), :].rearrange("p a n -> p (a n)")
                                     ).then_inc(ix_ready, 1)
                    pool.wait_ge(ix_ready, j + 1)
                    pool.sem_inc(waited, 1)
                    pool.wait_ge(x_in[b], 8 * (j - b) + 16)
                    pool.sem_inc(waited, 1)
                    for n in range(TOPK):
                        pool.indirect_dma_start(xs_dram, bass.IndirectOffsetOnAxis(ix[b][:, n:n + 1], 0), xr[b][:],
                                                None, bounds_check=SLOTS - 1, oob_is_err=False
                                                ).then_inc(sent[b], 16)
                by_twos(pool, NJ, step)
                for b in range(2):
                    pool.wait_ge(sent[b], 8 * TOPK * NJ)


def stage_experts_and_attention(nc, w1, w2, w3, conv_w, xs_dram, o_dram, ident, EXP, Q, K, V):
    KD = D // P
    PER = NGR // NH
    SCALE = float(DH) ** -0.5
    with Core(nc) as k:
        KC, VC = k.sb("j_kc", [P, 8, NJ, DH]), k.sb("j_vc", [P, 8, NJ, DH])
        prod, acc = k.sb("j_prod", [P, NJ, DH]), k.sb("j_acc", [P, NJ, DH])
        cprod, cacc = k.sb("j_cprod", [P, NJ, DH]), k.sb("j_cacc", [P, NJ, DH])
        SC, MASK = k.sb("j_sc", [P, len(OFFSETS), NJ]), k.sb("j_mask", [P, len(OFFSETS), NJ])
        mx = k.sb("j_mx", [P, NJ])
        cw = k.sb("j_cw", [P, DH, KCONV])
        WA = [k.sb(f"j_wa{b}", [P, 2, KD, HM]) for b in range(2)]
        WB = [k.sb(f"j_wb{b}", [P, D]) for b in range(2)]
        xs = [k.sb(f"j_xs{b}", [P, 2, D]) for b in range(2)]
        xT = [k.sb(f"j_xT{b}", [P, KD, GT]) for b in range(2)]
        th = [k.sb(f"j_th{b}", [P, GT]) for b in range(2)]
        gate = [k.sb(f"j_gate{b}", [P, GT]) for b in range(2)]
        ob = [k.sb(f"j_ob{b}", [P, 2, D]) for b in range(2)]
        tp = [k.ps(f"j_tp{b}", [P, KD, GT]) for b in range(2)]
        hp = [k.ps(f"j_hp{b}", [P, 2, GT]) for b in range(2)]
        op = [k.ps(f"j_op{b}", [P, 2, D]) for b in range(2)]
        w_in, x_in = [k.sem(f"j_w_in{b}") for b in range(2)], [k.sem(f"j_x_in{b}") for b in range(2)]
        tp_ready, xT_ready, h_ready, th_ready = (k.sem(f"j_{n}_ready") for n in ("tp", "xT", "h", "th"))
        half_gate, gate_ready, o_ready, ob_ready = (k.sem(f"j_{n}") for n in ("half", "gated", "o", "ob"))
        stored = [k.sem(f"j_stored{b}") for b in range(2)]
        pl, vl, zeroed = k.sem("j_pl"), k.sem("j_vl"), k.sem("j_zeroed")
        k_in, v_in, cw_in = k.sem("j_k_in"), k.sem("j_v_in"), k.sem("j_cw_in")
        scored, weighed, shifted, exped = (k.sem(f"j_{n}") for n in ("scored", "weighed", "shifted", "exped"))
        convolved, summed = k.sem("j_convolved"), k.sem("j_summed")
        waited = k.sem("j_waited")

        def heads(eng, body):
            body(0, 0)
            with eng.Fori(1, NH - 1) as h:
                body(h, 1)
            body(NH - 1, 2)

        def head(a, h):
            return a[:, bass.ds(h, 1), :, :].rearrange("p a j d -> p (a j) d")

        def back(a, o):
            if o < NJ:
                return a[:, 6:8, :, :].rearrange("p m j d -> p (m j) d")[:, NJ - o:2 * NJ - o, :]
            return a[:, SHIFTS.index(o // NJ), :, :]

        class HeadChain:

            def __init__(self, eng, sem, before=0):
                self.eng, self.sem, self.before, self.per, self.n, self.h = eng, sem, before, None, 0, 0

            def start(self, h, which):
                if which == 1:
                    self.per = self.n
                self.h, self.n = h, 0

            def __call__(self, ins):
                self.n += 1
                ins.then_inc(self.sem, 1)
                done = self.before + self.n if self.per is None else self.before + self.per * self.h + self.n
                self.eng.wait_ge(self.sem, done)

        with nc.Block() as block:

            @block.sync
            def _(sp):
                def step(g, b, first):
                    if not first:
                        sp.wait_ge(tp_ready, g - 1)
                    sp.dma_start(xs[b][:], xs_dram[bass.ds(g * GT, GT), :].rearrange("(t p) d -> p t d", p=P)
                                 ).then_inc(x_in[b], 16)
                    e = sp.value_load(EXP[0:1, bass.ds(g, 1)], min_val=0, max_val=NE - 1)
                    if not first:
                        sp.wait_ge(h_ready, g - 1)
                    for i, w in enumerate((w1, w3)):
                        sp.dma_start(WA[b][:, i, :, :], w[bass.ds(e, 1)].rearrange("e (k p) n -> p (e k) n", p=P)
                                     ).then_inc(w_in[b], 16)
                    if not first:
                        sp.wait_ge(o_ready, g - 1)
                    sp.dma_start(WB[b][:], w2[bass.ds(e, 1)].rearrange("e p n -> p (e n)")).then_inc(w_in[b], 16)
                    if not first:
                        sp.wait_ge(ob_ready, g - 1)
                        sp.dma_start(o_dram[bass.ds(g * GT - 2 * GT, GT), :].rearrange("(t p) d -> p t d", p=P),
                                     ob[b][:]).then_inc(stored[b], 16)
                by_twos(sp, NGR, step)
                for b in range(2):
                    sp.wait_ge(ob_ready, NGR - 1 + b)
                    g = NGR - 2 + b
                    sp.dma_start(o_dram[g * GT:(g + 1) * GT, :].rearrange("(t p) d -> p t d", p=P),
                                 ob[b][:]).then_inc(stored[b], 16)
                for b in range(2):
                    sp.wait_ge(stored[b], 8 * NGR)

            @block.tensor
            def _(pe):
                def transposes(g, b):
                    pe.wait_ge(x_in[b], 8 * (g - b) + 16)
                    for t in range(2):
                        for d in range(KD):
                            last = pe.transpose(tp[b][:, d, t * P:(t + 1) * P], xs[b][:, t, d * P:(d + 1) * P],
                                                ident[:])
                    last.then_inc(tp_ready, 1)

                def hidden(g, b):
                    pe.wait_ge(xT_ready, g + 1)
                    pe.wait_ge(w_in[b], 24 * (g - b) + 48)
                    for i in range(2):
                        for d in range(KD):
                            last = pe.matmul(hp[b][:, i, :], WA[b][:, i, d, :], xT[b][:, d, :],
                                             start=(d == 0), stop=(d == KD - 1))
                    last.then_inc(h_ready, 1)

                def outputs(g, b, first):
                    pe.wait_ge(gate_ready, g + 1)
                    if not first:
                        pe.wait_ge(ob_ready, g - 1)
                    for t in range(2):
                        last = pe.matmul(op[b][:, t, :], gate[b][:, t * P:(t + 1) * P], WB[b][:],
                                         start=True, stop=True)
                    last.then_inc(o_ready, 1)

                def step(g, b, first):
                    hidden(g + 1, 1 - b)
                    outputs(g, b, first)
                    transposes(g + 2, b)

                transposes(0, 0)
                transposes(1, 1)
                hidden(0, 0)
                by_twos(pe, NGR - 2, step)
                hidden(NGR - 1, 1)
                outputs(NGR - 2, 0, False)
                outputs(NGR - 1, 1, False)

            @block.scalar
            def _(act):
                act.preload_act_table(ACT.Exp)

                def move_xT(g, b, wait):
                    act.wait_ge(tp_ready, g + 1)
                    if wait:
                        act.wait_ge(h_ready, g - 1)
                    act.copy(xT[b][:], tp[b][:]).then_inc(xT_ready, 1)

                def tanh(g, b, wait):
                    act.wait_ge(h_ready, g + 1)
                    if wait:
                        act.wait_ge(gate_ready, g - 1)
                    act.activation(th[b][:], hp[b][:, 0, :], ACT.Tanh, scale=0.5).then_inc(th_ready, 1)

                def move_out(g, b, wait):
                    act.wait_ge(o_ready, g + 1)
                    if wait:
                        act.wait_ge(stored[b], 8 * (g - b))
                    act.mul(ob[b][:], op[b][:], 0.5).then_inc(ob_ready, 1)

                def body(h, which):
                    for n in range(PER):
                        g, b, end = h * PER + n, n % 2, which == 2 and n >= PER - 2
                        if not (end and n == PER - 1):
                            tanh(g + 1, 1 - b, which > 0 or n > 0)
                        move_out(g, b, which > 0 or n > 1)
                        if not end:
                            move_xT(g + 2, b, True)
                        if n == 4:
                            act.wait_ge(shifted, h + 1)
                            act.activation(SC[:], SC[:], ACT.Exp, scale=SCALE).then_inc(exped, 1)

                move_xT(0, 0, False)
                move_xT(1, 1, False)
                tanh(0, 0, False)
                heads(act, body)

            @block.gpsimd
            def _(pool):
                link = Chain(pool, pl)
                link(pool.memset(KC[:], 0.0))
                link(pool.memset(VC[:], 0.0))
                link(pool.memset(MASK[:], 0.0))
                for s, o in enumerate(OFFSETS):
                    link(pool.affine_select(out=MASK[:, s, :], in_=MASK[:, s, :], compare_op=ALU.is_ge, fill=-FAR,
                                            base=-o, pattern=[[1, NJ]], channel_multiplier=NJ))
                pool.sem_inc(zeroed, 1)

                def shifted_copies(dst, src, h, sem):
                    for i, m in enumerate(SHIFTS):
                        pool.dma_start(dst[m:P, i, :, :], head(src, h)[0:P - m]).then_inc(sem, 16)

                def taps(h):
                    pool.dma_start(cw[:], conv_w[bass.ds(h * DH, DH), :].partition_broadcast(P)).then_inc(cw_in, 16)

                shifted_copies(KC, K, 0, k_in)
                shifted_copies(VC, V, 0, v_in)
                taps(0)
                hlink = HeadChain(pool, pl, link.n)

                def body(h, which):
                    hlink.start(h, which)
                    pool.wait_ge(v_in, 128 * h + 128)
                    pool.sem_inc(waited, 1)
                    pool.wait_ge(cw_in, 16 * h + 16)
                    pool.sem_inc(waited, 1)
                    for o in range(KCONV):
                        t = KCONV - 1 - o
                        w = cw[:, :, t:t + 1].rearrange("p d a -> p a d").to_broadcast([P, NJ, DH])
                        dst = cacc if o == 0 else cprod
                        hlink(pool.tensor_tensor(dst[:], back(VC, o), w, ALU.mult))
                        if o:
                            hlink(pool.tensor_tensor(cacc[:], cacc[:], cprod[:], ALU.add))
                    pool.sem_inc(convolved, 1)
                    if which < 2:
                        pool.wait_ge(scored, h + 1)
                        pool.sem_inc(waited, 1)
                        shifted_copies(KC, K, h + 1, k_in)
                        pool.wait_ge(summed, h + 1)
                        pool.sem_inc(waited, 1)
                        shifted_copies(VC, V, h + 1, v_in)
                        taps(h + 1)
                heads(pool, body)

            @block.vector
            def _(ve):
                hlink = HeadChain(ve, vl)
                ve.wait_ge(zeroed, 1)

                def gated(g, b, wait):
                    ve.wait_ge(th_ready, g + 1)
                    hlink(ve.scalar_tensor_tensor(th[b][:], th[b][:], 1.0, hp[b][:, 0, :], ALU.add, ALU.mult))
                    if wait:
                        ve.wait_ge(o_ready, g - 1)
                    ve.tensor_tensor(gate[b][:], th[b][:], hp[b][:, 1, :], ALU.mult).then_inc(gate_ready, 1)

                def body(h, which):
                    hlink.start(h, which)
                    ve.wait_ge(k_in, 128 * h + 128)
                    n = 0
                    for s, o in enumerate(OFFSETS):
                        hlink(ve.tensor_tensor(prod[:], head(Q, h), back(KC, o), ALU.mult))
                        hlink(ve.tensor_reduce(SC[:, s, :], prod[:], AX_X, ALU.add))
                        if s % 2:
                            gated(h * PER + n, n % 2, which > 0 or n > 1)
                            n += 1
                    ve.sem_inc(scored, 1)
                    by_token = SC[:].rearrange("p s j -> p j s")
                    every = mx[:].unsqueeze(1).to_broadcast([P, len(OFFSETS), NJ])
                    hlink(ve.tensor_tensor(SC[:], SC[:], MASK[:], ALU.add))
                    hlink(ve.tensor_reduce(mx[:], by_token, AX_X, ALU.max))
                    ve.tensor_tensor(SC[:], SC[:], every, ALU.subtract).then_inc(shifted, 1)
                    ve.wait_ge(exped, h + 1)
                    hlink(ve.tensor_reduce(mx[:], by_token, AX_X, ALU.add))
                    hlink(ve.reciprocal(mx[:], mx[:]))
                    hlink(ve.tensor_tensor(SC[:], SC[:], every, ALU.mult))
                    ve.wait_ge(v_in, 128 * h + 128)
                    for s, o in enumerate(OFFSETS):
                        w = SC[:, s, :].unsqueeze(2).to_broadcast([P, NJ, DH])
                        dst = prod if s else acc
                        hlink(ve.tensor_tensor(dst[:], back(VC, o), w, ALU.mult))
                        if s:
                            hlink(ve.tensor_tensor(acc[:], acc[:], prod[:], ALU.add))
                        if s % 2:
                            gated(h * PER + n, n % 2, True)
                            n += 1
                    ve.wait_ge(convolved, h + 1)
                    ve.tensor_tensor(head(K, h), acc[:], cacc[:], ALU.add).then_inc(summed, 1)
                heads(ve, body)


def stage_mix1(nc, w_o, xn1_dram, x1_dram, z_dram, o_dram, ident, Q, K, KVB, WK, GIDX, out):
    KD = D // P
    LW = P + 4
    with Core(nc) as k:
        wo = k.sb("m_wo", [P, KD, D])
        two = range(2)
        xr = [k.sb(f"m_xn{b}", [P, D]) for b in two]
        x1 = [k.sb(f"m_x1{b}", [P, D]) for b in two]
        zr = [k.sb(f"m_z{b}", [P, D]) for b in two]
        ix = [k.sb(f"m_ix{b}", [P, TOPK], U32) for b in two]
        gt = [k.sb(f"m_gt{b}", [P, TOPK, D]) for b in two]
        ex = [k.sb(f"m_ex{b}", [P, D]) for b in two]
        fq = [k.sb(f"m_fq{b}", [P, D]) for b in two]
        fqT = [k.sb(f"m_fqT{b}", [P, KD, P]) for b in two]
        rz = [k.sb(f"m_rz{b}", [P, KD, 4]) for b in two]
        hs = [k.sb(f"m_h{b}", [P, D]) for b in two]
        hT = [k.sb(f"m_hT{b}", [P, KD, P]) for b in two]
        s1 = [k.sb(f"m_s1{b}", [P, D]) for b in two]
        th = [k.sb(f"m_th{b}", [P, D]) for b in two]
        res = [k.sb(f"m_res{b}", [P, D]) for b in two]
        qp = [k.ps(f"m_qp{b}", [P, KD, P]) for b in two]
        lp = [k.ps(f"m_lp{b}", [P, KD, LW]) for b in two]
        hp = [k.ps(f"m_hp{b}", [P, KD, P]) for b in two]
        ap = [k.ps(f"m_ap{b}", [P, D]) for b in two]
        wo_in = k.sem("m_wo_in")
        rows_in, got = [k.sem(f"m_rows_in{b}") for b in two], [k.sem(f"m_got{b}") for b in two]
        ix_ready, vl, stored = k.sem("m_ix_ready"), k.sem("m_vl"), [k.sem(f"m_stored{b}") for b in two]
        min_ready, ex_ready, fq_ready, qp_ready = (k.sem(f"m_{n}_ready") for n in ("min", "ex", "fq", "qp"))
        fqT_ready, lp_ready, hs_ready, hp_ready = (k.sem(f"m_{n}_ready") for n in ("fqT", "lp", "hs", "hp"))
        hT_ready, ap_ready, f_ready, th_ready = (k.sem(f"m_{n}_ready") for n in ("hT", "ap", "f", "th"))
        res_ready = k.sem("m_res_ready")
        waited = k.sem("m_waited")

        def heads(a, j):
            return a[:, :, bass.ds(j, 1), :].rearrange("p h a d -> p h (a d)")

        with nc.Block() as block:

            @block.sync
            def _(sp):
                sp.dma_start(wo[:], w_o.rearrange("(k p) n -> p k n", p=P)).then_inc(wo_in, 16)
                for b in two:
                    sp.sem_inc(stored[b], 16)

                def step(j, b, first):
                    if not first:
                        sp.wait_ge(res_ready, j - 1)
                        sp.dma_start(token_rows(out[0], j - 2), res[b][:]).then_inc(stored[b], 16)
                    for dst, src in ((xr, xn1_dram), (x1, x1_dram), (zr, z_dram)):
                        sp.dma_start(dst[b][:], token_rows(src, j)).then_inc(rows_in[b], 16)
                by_twos(sp, NJ, step)
                for b in two:
                    sp.wait_ge(res_ready, NJ - 1 + b)
                    sp.dma_start(token_rows(out[0], NJ - 2 + b), res[b][:]).then_inc(stored[b], 16)
                for b in two:
                    sp.wait_ge(stored[b], 8 * NJ + 16)

            @block.gpsimd
            def _(pool):
                def step(j, b, first):
                    if not first:
                        pool.wait_ge(got[b], 8 * TOPK * (j - b))
                        pool.sem_inc(waited, 1)
                        pool.wait_ge(f_ready, j - 1)
                        pool.sem_inc(waited, 1)
                    pool.tensor_copy(ix[b][:], GIDX[:, bass.ds(j, 1), :].rearrange("p a n -> p (a n)")
                                     ).then_inc(ix_ready, 1)
                    pool.wait_ge(ix_ready, j + 1)
                    pool.sem_inc(waited, 1)
                    for n in range(TOPK):
                        pool.indirect_dma_start(gt[b][:, n, :], None, o_dram,
                                                bass.IndirectOffsetOnAxis(ix[b][:, n:n + 1], 0)).then_inc(got[b], 16)
                by_twos(pool, NJ, step)

            @block.tensor
            def _(pe):
                pe.wait_ge(wo_in, 16)

                def low(j, b):
                    pe.wait_ge(fq_ready, j + 1)
                    for d in range(KD):
                        last = pe.transpose(qp[b][:, d, :], fq[b][:, d * P:(d + 1) * P], ident[:])
                    last.then_inc(qp_ready, 1)
                    pe.wait_ge(fqT_ready, j + 1)
                    for m in range(KD):
                        last = pe.matmul(lp[b][:, m, :], fqT[b][:, m, :], KVB[:, m, :], start=True, stop=True)
                    last.then_inc(lp_ready, 1)

                def project(j, b):
                    pe.wait_ge(hs_ready, j + 1)
                    for d in range(KD):
                        last = pe.transpose(hp[b][:, d, :], hs[b][:, d * P:(d + 1) * P], ident[:])
                    last.then_inc(hp_ready, 1)
                    pe.wait_ge(hT_ready, j + 1)
                    for d in range(KD):
                        last = pe.matmul(ap[b][:], hT[b][:, d, :], wo[:, d, :], start=(d == 0), stop=(d == KD - 1))
                    last.then_inc(ap_ready, 1)

                with pe.Fori(0, NJ // 2) as i:
                    for b in two:
                        low(2 * i + b, b)
                    for b in two:
                        project(2 * i + b, b)

            @block.scalar
            def _(act):
                act.preload_act_table(ACT.Exp)
                with act.Fori(0, NJ // 2) as i:
                    for b in two:
                        act.wait_ge(min_ready, 2 * i + b + 1)
                        act.activation(ex[b][:], ex[b][:], ACT.Exp).then_inc(ex_ready, 1)
                    for b in two:
                        act.wait_ge(qp_ready, 2 * i + b + 1)
                        act.copy(fqT[b][:], qp[b][:]).then_inc(fqT_ready, 1)
                    for b in two:
                        act.wait_ge(hp_ready, 2 * i + b + 1)
                        act.copy(hT[b][:], hp[b][:]).then_inc(hT_ready, 1)
                    for b in two:
                        act.wait_ge(f_ready, 2 * i + b + 1)
                        act.activation(th[b][:], zr[b][:], ACT.Tanh, scale=0.5).then_inc(th_ready, 1)

            @block.vector
            def _(ve):
                count = [0]

                def turn(i, per):
                    count[0] = 0

                    def link(ins):
                        count[0] += 1
                        ins.then_inc(vl, 1)
                        ve.wait_ge(vl, per * i + count[0])
                    return link

                PER_TURN = 2 * (4 + TOPK - 1 + 3)
                with ve.Fori(0, NJ // 2) as i:
                    link = turn(i, PER_TURN)
                    for b in two:
                        ve.tensor_scalar(ex[b][:].rearrange("p (h d) -> p h d", h=NH), heads(Q, 2 * i + b), 0.0, None,
                                         ALU.min).then_inc(min_ready, 1)
                    for b in two:
                        ve.wait_ge(ex_ready, 2 * i + b + 1)
                        ve.scalar_tensor_tensor(fq[b][:].rearrange("p (h d) -> p h d", h=NH), heads(Q, 2 * i + b),
                                                0.0, ex[b][:].rearrange("p (h d) -> p h d", h=NH), ALU.max, ALU.add
                                                ).then_inc(fq_ready, 1)
                    for b in two:
                        ve.wait_ge(lp_ready, 2 * i + b + 1)
                        link(ve.tensor_scalar(rz[b][:], lp[b][:, :, P:LW], 1e-6, None, ALU.add))
                        link(ve.reciprocal(rz[b][:], rz[b][:]))
                        h4 = hs[b][:].rearrange("p (m h d) -> p m h d", m=KD, h=4)
                        for m in range(KD):
                            ins = ve.tensor_tensor(h4[:, m, :, :], lp[b][:, m, 0:P].rearrange("p (h d) -> p h d", h=4),
                                                   rz[b][:, m, :].unsqueeze(2).to_broadcast([P, 4, DH]), ALU.mult)
                            link(ins)
                        ve.tensor_tensor(hs[b][:].rearrange("p (h d) -> p h d", h=NH), heads(K, 2 * i + b),
                                         hs[b][:].rearrange("p (h d) -> p h d", h=NH), ALU.add).then_inc(hs_ready, 1)
                    for b in two:
                        j = 2 * i + b
                        ve.wait_ge(rows_in[b], 48 * i + 48)
                        ve.wait_ge(got[b], 16 * TOPK * i + 16 * TOPK)
                        for n in range(TOPK):
                            wn = WK[:, bass.ds(j, 1), n]
                            ins = ve.scalar_tensor_tensor(zr[b][:], gt[b][:, n, :], wn, zr[b][:], ALU.mult, ALU.add)
                            if n < TOPK - 1:
                                link(ins)
                            else:
                                ins.then_inc(f_ready, 1)
                    for b in two:
                        ve.wait_ge(ap_ready, 2 * i + b + 1)
                        link(ve.tensor_tensor(s1[b][:], ap[b][:], xr[b][:], ALU.add))
                        ve.wait_ge(th_ready, 2 * i + b + 1)
                        link(ve.scalar_tensor_tensor(th[b][:], th[b][:], 1.0, zr[b][:], ALU.add, ALU.mult))
                        link(ve.scalar_tensor_tensor(th[b][:], th[b][:], 0.5, s1[b][:], ALU.mult, ALU.mult))
                        ve.wait_ge(stored[b], 16 * i + 16)
                        ve.tensor_tensor(res[b][:], th[b][:], x1[b][:], ALU.add).then_inc(res_ready, 1)


def gated_s4d_then_ripple_moe(nc, x, log_a_re, a_im, c_re, c_im, log_dt, d_skip, ln_w, ln_b, ffn_w, disha,
                              w_qkv, w_o, conv_w, w_gate, w1, w2, w3, ws1, ws2, ws3, out):
    v_dram = nc.dram_tensor("v_powers", (NG, P, 4 * GH * P), BF16, kind="Internal").ap()
    kp_dram = nc.dram_tensor("padded_taps", (D, 2 * P), F32, kind="Internal").ap()
    x1_dram = nc.dram_tensor("x1", (T, D), F32, kind="Internal").ap()
    xn1_dram = nc.dram_tensor("xn1", (T, D), F32, kind="Internal").ap()
    z_dram = nc.dram_tensor("shared_out", (T, D), F32, kind="Internal").ap()
    xs_dram = nc.dram_tensor("slots_in", (SLOTS, D), F32, kind="Internal").ap()
    o_dram = nc.dram_tensor("slots_out", (SLOTS, D), F32, kind="Internal").ap()
    Core.used = []
    with Core(nc) as k:
        ident = k.sb("ident", [P, P])
        with Core(nc) as l0:
            anti = l0.sb("anti", [P, P])
            XN, G0 = l0.sb("XN", [P, NC, D]), l0.sb("G0", [P, NC, D])
            stage_norm_gate0(nc, x, ffn_w, disha, ident, anti, XN, G0, xs_dram)
            with Core(nc) as s4d:
                S = s4d.sb("S", [P, NC, 2, P])
                with Core(nc) as c:
                    turns, KT = c.sb("turns", [P, P]), c.sb("KT", [P, 2, P])
                    WR, WQ = c.sb("WR", [P, 2, P]), c.sb("WQ", [P, 2, P])
                    with Core(nc) as m:
                        DP = m.sb("DP", [P, 7, P])
                        CMH, CML = (m.sb(n, [P, P, 2, 2], BF16) for n in ("CMH", "CML"))
                        MR, MRN, MI = m.sb("MR", [P, P]), m.sb("MRN", [P, P]), m.sb("MI", [P, P])
                        stage_s4d_constants(nc, log_a_re, a_im, c_re, c_im, log_dt, ident, turns, DP, CMH, CML, MR, MRN,
                                            MI, WR, WQ)
                        stage_s4d_states(nc, turns, DP, CMH, CML, MR, MRN, MI, ident, anti, XN, KT, S, v_dram)
                    stage_s4d_scan(nc, WR, WQ, S, KT, ident, kp_dram)
                with Core(nc) as o:
                    Y = o.sb("Y", [P, NC, D])
                    stage_s4d_outputs(nc, S, XN, anti, v_dram, kp_dram, Y)
                    stage_mix0(nc, x, d_skip, ln_w, ln_b, XN, G0, Y, x1_dram, xn1_dram)
        k.recycle()
        with Core(nc) as l1:
            WK = l1.sb("WK", [P, NJ, TOPK])
            SIDX, GIDX = l1.sb("SIDX", [P, NJ, TOPK], U32), l1.sb("GIDX", [P, NJ, TOPK], U32)
            EXP = l1.sb("EXP", [P, NGR], I32)
            KVB = l1.sb("KVB", [P, 2, P + 4])
            Q, K, V = (l1.sb(n, [P, NH, NJ, DH]) for n in "QKV")
            with Core(nc) as g:
                L = g.sb("L", [P, NJ, NE])
                stage_projections(nc, w_qkv, w_gate, ws1, ws2, ws3, xn1_dram, z_dram, ident, Q, K, V, L, KVB)
                stage_routing(nc, L, WK, SIDX, GIDX, EXP)
            stage_scatter(nc, xn1_dram, xs_dram, SIDX)
            stage_experts_and_attention(nc, w1, w2, w3, conv_w, xs_dram, o_dram, ident, EXP, Q, K, V)
            stage_mix1(nc, w_o, xn1_dram, x1_dram, z_dram, o_dram, ident, Q, K, KVB, WK, GIDX, out)


_INS = ['L0_attn_x', 'L0_attn_log_A_real', 'L0_attn_A_imag', 'L0_attn_C_re', 'L0_attn_C_im', 'L0_attn_log_dt',
        'L0_attn_D', 'L0_attn_ln_w', 'L0_attn_ln_b', 'L0_ffn_weight', 'L0_ffn_disha', 'L1_attn_Wqkv', 'L1_attn_Wo',
        'L1_attn_conv_w', 'L1_ffn_Wg', 'L1_ffn_W1', 'L1_ffn_W2', 'L1_ffn_W3', 'L1_ffn_Ws1', 'L1_ffn_Ws2',
        'L1_ffn_Ws3']
_OUTS = [((1, 4096, 256), 'float32')]


def kernel(**inputs):
    import numpy as _np
    import concourse.bacc as _bacc
    from concourse import mybir as _mybir
    from concourse.bass_utils import run_bass_kernel_spmd as _run

    nc = _bacc.Bacc("TRN2", target_bir_lowering=False, num_devices=1)
    arrays, args = {}, []
    for name in _INS:
        a = _np.ascontiguousarray(inputs[name])
        arrays[f"in_{name}_dram"] = a
        args.append(nc.dram_tensor(f"in_{name}_dram", a.shape, _mybir.dt.from_np(a.dtype), kind="ExternalInput").ap())
    for i, (shape, dtype) in enumerate(_OUTS):
        dt = _mybir.dt.from_np(_np.dtype(dtype))
        args.append(nc.dram_tensor(f"out_{i}_dram", shape, dt, kind="ExternalOutput").ap())
    gated_s4d_then_ripple_moe(nc, *args)
    r = _run(nc, [arrays], core_ids=[0])
    return r.results[0]["out_0_dram"]
```

```python
from contextlib import ExitStack

import concourse.bass as bass
from concourse import mybir

F32 = mybir.dt.float32
BF16 = mybir.dt.bfloat16
I32 = mybir.dt.int32
U32 = mybir.dt.uint32
ALU = mybir.AluOpType
ACT = mybir.ActivationFunctionType
AX_X = mybir.AxisListType.X

P = 128
T, D = 4096, 256
NC = T // P
NST = 64
GH = 8
NG = P // GH
EPS = 1e-5
PI = 3.14159265358979
TWO_PI = 6.2831850
MAGIC = 12582912.0


class Chain:

    def __init__(self, eng, sem):
        self.eng, self.sem, self.n = eng, sem, 0

    def __call__(self, ins):
        self.n += 1
        ins.then_inc(self.sem, 1)
        self.eng.wait_ge(self.sem, self.n)


class Core:
    used = []

    def __init__(self, nc):
        self.nc, self.stack = nc, ExitStack()

    def __enter__(self):
        return self

    def __exit__(self, *a):
        self.stack.close()

    def sb(self, name, shape, dt=F32):
        return self.stack.enter_context(self.nc.sbuf_tensor(name, shape, dt))

    def ps(self, name, shape, dt=F32):
        return self.stack.enter_context(self.nc.psum_tensor(name, shape, dt))

    def sem(self, name):
        Core.used.append(self.nc.alloc_semaphore(name=name))
        return Core.used[-1]

    def recycle(self):
        self.nc.clear_and_free_semaphores(Core.used)
        self.nc.all_engine_barrier()
        Core.used = []


def moments_to_scale(ve, link, stats, mean, rstd, tmp):
    me, mo = stats[:, :, 1], stats[:, :, 4]
    link(ve.tensor_tensor(mean, me, mo, ALU.add))
    link(ve.tensor_tensor(tmp, me, mo, ALU.subtract))
    link(ve.tensor_scalar(mean, mean, 0.5, None, ALU.mult))
    link(ve.tensor_tensor(tmp, tmp, tmp, ALU.mult))
    link(ve.tensor_tensor(rstd, stats[:, :, 2], stats[:, :, 5], ALU.add))
    link(ve.tensor_scalar(rstd, rstd, 1.0 / D, EPS, ALU.mult, ALU.add))
    link(ve.scalar_tensor_tensor(rstd, tmp, 0.25, rstd, ALU.mult, ALU.add))


def make_identity(pool, link, tile, base=0, step=-1):
    link(pool.memset(tile, 0.0))
    link(pool.affine_select(out=tile, in_=tile, compare_op=ALU.not_equal, fill=1.0, base=base,
                            pattern=[[step, P]], channel_multiplier=1))


def stage_norm_gate0(nc, x, weight, disha, ident, anti, XN, G0, xs_dram):
    ROWS = 1024
    KD = D // P
    with Core(nc) as k:
        X = k.sb("a_x", [P, NC, D])
        wraw = k.sb("a_wraw", [P, KD, D])
        drep = k.sb("a_drep", [P, D])
        weff = k.sb("a_weff", [P, KD, D])
        stats = k.sb("a_stats", [P, NC, 6])
        zero = k.sb("a_zero", [P, ROWS // P * D])
        zeroed, cleared = k.sem("a_zeroed"), k.sem("a_cleared")
        mean = k.sb("a_mean", [P, NC])
        rstd = k.sb("a_rstd", [P, NC])
        tmp = k.sb("a_tmp", [P, NC])
        xf = [k.sb(f"a_xf{b}", [P, D]) for b in range(2)]
        xT = [k.sb(f"a_xT{b}", [P, KD, P]) for b in range(2)]
        tp = [k.ps(f"a_tp{b}", [P, KD, P]) for b in range(2)]
        gp = [k.ps(f"a_gp{b}", [P, D]) for b in range(2)]
        wt = k.ps("a_wt", [P, KD, D])
        x_in = [k.sem(f"a_x_in{i}") for i in range(4)]
        w_in = k.sem("a_w_in")
        pool_link, dve_link = k.sem("a_pool"), k.sem("a_dve")
        ident_ready = k.sem("a_ident_ready")
        wt_ready, weff_ready = k.sem("a_wt_ready"), k.sem("a_weff_ready")
        var_ready, std_ready = k.sem("a_var_ready"), k.sem("a_std_ready")
        xf_ready = k.sem("a_xf_ready")
        tp_ready, xT_ready = k.sem("a_tp_ready"), k.sem("a_xT_ready")
        gp_ready, g_ready = k.sem("a_gp_ready"), k.sem("a_g_ready")
        with nc.Block() as block:

            @block.sync
            def _(sp):
                for i in range(4):
                    c0 = i * NC // 4
                    sp.dma_start(X[:, c0:c0 + NC // 4, :],
                                 x[0, c0 * P:(c0 + NC // 4) * P, :].rearrange("(c s) d -> s c d", s=P)
                                 ).then_inc(x_in[i], 16)
                sp.wait_ge(zeroed, 1)
                for i in range(SLOTS // ROWS):
                    sp.dma_start(xs_dram[i * ROWS:(i + 1) * ROWS, :].rearrange("(p r) d -> p (r d)", p=P), zero[:]
                                 ).then_inc(cleared, 16)
                sp.wait_ge(cleared, 16 * (SLOTS // ROWS))

            @block.gpsimd
            def _(pool):
                link = Chain(pool, pool_link)
                pool.memset(zero[:], 0.0).then_inc(zeroed, 1)
                make_identity(pool, link, ident[:])
                make_identity(pool, link, anti[:], base=-(P - 1), step=1)
                pool.sem_inc(ident_ready, 1)

            @block.vector
            def _(ve):
                link = Chain(ve, dve_link)
                for i in range(4):
                    ve.wait_ge(x_in[i], 16)
                    with ve.Fori(i * NC // 4, (i + 1) * NC // 4) as c:
                        last = ve.bn_stats(stats[:, c, :], X[:, c, :])
                ve.drain()
                moments_to_scale(ve, link, stats, mean[:], rstd[:], tmp[:])
                ve.sem_inc(var_ready, 1)
                ve.wait_ge(std_ready, 1)
                link(ve.reciprocal(rstd[:], rstd[:]))
                ve.wait_ge(w_in, 48)
                ve.wait_ge(wt_ready, 1)
                for j in range(KD):
                    ve.tensor_tensor(weff[:, j, :], wt[:, j, :], drep[:], ALU.add).then_inc(weff_ready, 1)
                for b in range(2):
                    ve.tensor_scalar(xf[b][:], X[:, b, :], mean[:, b:b + 1], rstd[:, b:b + 1],
                                     ALU.subtract, ALU.mult).then_inc(xf_ready, 1)
                    ve.tensor_scalar(XN[:, b, :], X[:, b, :], mean[:, b:b + 1], rstd[:, b:b + 1],
                                     ALU.subtract, ALU.mult)
                with ve.Fori(1, NC // 2) as i:
                    for b in range(2):
                        c = 2 * i + b
                        ve.wait_ge(tp_ready, 2 * i + b - 1)
                        ve.tensor_scalar(xf[b][:], X[:, c, :], mean[:, bass.ds(c, 1)], rstd[:, bass.ds(c, 1)],
                                         ALU.subtract, ALU.mult).then_inc(xf_ready, 1)
                        ve.tensor_scalar(XN[:, c, :], X[:, c, :], mean[:, bass.ds(c, 1)], rstd[:, bass.ds(c, 1)],
                                         ALU.subtract, ALU.mult)

            @block.scalar
            def _(act):
                act.dma_start(wraw[:], weight.rearrange("(j o) d -> o j d", o=P)).then_inc(w_in, 16)
                for j in range(2):
                    act.dma_start(drep[64 * j:64 * j + 64, :], disha).then_inc(w_in, 16)
                act.wait_ge(var_ready, 1)
                act.activation(rstd[:], rstd[:], ACT.Sqrt).then_inc(std_ready, 1)
                act.preload_act_table(ACT.Silu)
                with act.Fori(0, NC // 2) as i:
                    for b in range(2):
                        act.wait_ge(tp_ready, 2 * i + b + 1)
                        act.copy(xT[b][:], tp[b][:]).then_inc(xT_ready, 1)
                    for b in range(2):
                        act.wait_ge(gp_ready, 2 * i + b + 1)
                        act.activation(G0[:, 2 * i + b, :], gp[b][:], ACT.Silu).then_inc(g_ready, 1)

            @block.tensor
            def _(pe):
                pe.wait_ge(ident_ready, 1)
                pe.wait_ge(w_in, 48)
                for j in range(KD):
                    for d in range(KD):
                        last = pe.transpose(wt[:, d, j * P:(j + 1) * P], wraw[:, j, d * P:(d + 1) * P], ident[:])
                last.then_inc(wt_ready, 1)
                pe.wait_ge(weff_ready, KD)
                with pe.Fori(0, NC // 2) as i:
                    for b in range(2):
                        pe.wait_ge(xf_ready, 2 * i + b + 1)
                        for d in range(KD):
                            last = pe.transpose(tp[b][:, d, :], xf[b][:, d * P:(d + 1) * P], ident[:])
                        last.then_inc(tp_ready, 1)
                    for b in range(2):
                        pe.wait_ge(xT_ready, 2 * i + b + 1)
                        for d in range(KD):
                            last = pe.matmul(gp[b][:], xT[b][:, d, :], weff[:, d, :],
                                             start=(d == 0), stop=(d == KD - 1))
                        last.then_inc(gp_ready, 1)




def frac_turns(ve, link, out, turns, tmp):
    link(ve.tensor_scalar(tmp, turns, MAGIC, MAGIC, ALU.add, ALU.subtract))
    link(ve.tensor_tensor(out, turns, tmp, ALU.subtract))


def stage_s4d_constants(nc, log_a_re, a_im, c_re, c_im, log_dt, ident, turns, DP, CMH, CML, MR, MRN, MI, WR, WQ):
    with Core(nc) as k:
        raw = [k.sb(f"b_raw{i}", [P, 2, NST]) for i in range(4)]
        names = ["e1", "ai", "cr", "ci", "dt", "th", "em", "den", "f", "t1", "t2", "t3", "sh", "ch", "re", "im",
                 "xr", "xi", "ctr", "cti", "mag", "decay", "hpi"]
        v = {n: k.sb(f"b_{n}", [P, P])[:] for n in names}
        CM = k.sb("b_cm", [P, P, 2, 2])
        tp = k.ps("b_tp", [P, 4, P])
        raw_in, dt_in = k.sem("b_raw_in"), k.sem("b_dt_in")
        tp_ready, ve_link, act_link = k.sem("b_tp_ready"), k.sem("b_dve"), k.sem("b_act")
        asked, act_done = k.sem("b_asked"), k.sem("b_act_done")
        with nc.Block() as block:

            @block.sync
            def _(sp):
                for i, a in enumerate((log_a_re, a_im, c_re, c_im)):
                    sp.dma_start(raw[i][:], a.rearrange("(g p) n -> p g n", g=2)).then_inc(raw_in, 16)
                for g in range(2):
                    sp.dma_start(v["dt"][g * NST:(g + 1) * NST, :],
                                 log_dt[g * P:(g + 1) * P].partition_broadcast(NST)).then_inc(dt_in, 16)

            @block.tensor
            def _(pe):
                pe.wait_ge(raw_in, 64)
                for i in range(4):
                    last = pe.transpose(tp[:, i, :], raw[i][:].rearrange("p g n -> p (g n)"), ident[:])
                last.then_inc(tp_ready, 1)

            @block.scalar
            def _(act):
                act.wait_ge(tp_ready, 1)
                act.wait_ge(dt_in, 32)
                act.activation(v["e1"], tp[:, 0, :], ACT.Exp).then_inc(act_done, 1)
                act.activation(v["dt"], v["dt"], ACT.Exp).then_inc(act_done, 1)
                act.wait_ge(asked, 1)
                act.activation(v["em"], v["decay"], ACT.Tanh, scale=0.5).then_inc(act_done, 1)
                act.wait_ge(asked, 2)
                act.activation(v["sh"], v["f"], ACT.Sin, scale=TWO_PI).then_inc(act_done, 1)
                act.activation(v["t3"], v["f"], ACT.Abs).then_inc(act_link, 1)
                act.wait_ge(act_link, 1)
                act.activation(v["ch"], v["t3"], ACT.Sin, scale=-TWO_PI, bias=v["hpi"][:, 0:1]).then_inc(act_done, 1)
                act.wait_ge(asked, 3)
                act.activation(v["xi"], v["f"], ACT.Sin, scale=TWO_PI).then_inc(act_done, 1)
                act.activation(v["t3"], v["f"], ACT.Abs).then_inc(act_link, 1)
                act.wait_ge(act_link, 2)
                act.activation(v["xr"], v["t3"], ACT.Sin, scale=-TWO_PI, bias=v["hpi"][:, 0:1]).then_inc(act_done, 1)

            @block.vector
            def _(ve):
                link = Chain(ve, ve_link)
                mul, add, sub = ALU.mult, ALU.add, ALU.subtract

                def tt(o, a, b, op):
                    link(ve.tensor_tensor(o, a, b, op))

                def ts(o, a, s1, s2, op0, op1=ALU.bypass):
                    link(ve.tensor_scalar(o, a, s1, s2, op0, op1))

                link(ve.memset(v["hpi"], PI / 2))
                ve.wait_ge(act_done, 2)
                link(ve.tensor_copy(v["ai"], tp[:, 1, :]))
                link(ve.tensor_copy(v["cr"], tp[:, 2, :]))
                link(ve.tensor_copy(v["ci"], tp[:, 3, :]))
                link(ve.scalar_tensor_tensor(v["decay"], v["e1"], -1.0, v["dt"], mul, mul))
                tt(v["th"], v["ai"], v["dt"], mul)
                ts(turns[:], v["th"], 0.15915494309189535, None, mul)
                ve.sem_inc(asked, 1)
                ts(v["t1"], turns[:], 0.5, None, mul)
                frac_turns(ve, link, v["f"], v["t1"], v["t2"])
                ve.sem_inc(asked, 1)
                ve.wait_ge(act_done, 3)
                ts(v["t1"], v["em"], -1.0, 1.0, mul, add)
                link(ve.reciprocal(v["t1"], v["t1"]))
                link(ve.scalar_tensor_tensor(v["em"], v["em"], 2.0, v["t1"], mul, mul))
                tt(v["t1"], v["e1"], v["e1"], mul)
                tt(v["t2"], v["ai"], v["ai"], mul)
                tt(v["den"], v["t1"], v["t2"], add)
                link(ve.reciprocal(v["den"], v["den"]))
                ve.wait_ge(act_done, 5)
                ts(v["t1"], v["em"], 1.0, None, add)
                tt(v["t2"], v["sh"], v["sh"], mul)
                tt(v["t2"], v["t2"], v["t1"], mul)
                link(ve.scalar_tensor_tensor(v["re"], v["t2"], -2.0, v["em"], mul, add))
                tt(v["t2"], v["sh"], v["ch"], mul)
                link(ve.scalar_tensor_tensor(v["im"], v["t2"], 2.0, v["t1"], mul, mul))
                ts(v["t1"], turns[:], float(P), None, mul)
                frac_turns(ve, link, v["f"], v["t1"], v["t2"])
                ve.sem_inc(asked, 1)
                ve.wait_ge(act_done, 7)
                ts(DP[:, 0, :], v["em"], 1.0, None, add)
                for i in range(6):
                    tt(DP[:, i + 1, :], DP[:, i, :], DP[:, i, :], mul)
                tt(v["mag"], DP[:, 6, :], DP[:, 6, :], mul)
                for r in range(2):
                    tt(WR[:, r, :], v["mag"], v["xr"], mul)
                tt(WQ[:, 0, :], v["mag"], v["xi"], mul)
                ts(WQ[:, 1, :], WQ[:, 0, :], -1.0, None, mul)
                tt(v["t1"], v["re"], v["e1"], mul)
                tt(v["t2"], v["im"], v["ai"], mul)
                tt(v["xr"], v["t2"], v["t1"], sub)
                tt(v["t1"], v["im"], v["e1"], mul)
                tt(v["t2"], v["re"], v["ai"], mul)
                link(ve.scalar_tensor_tensor(v["xi"], v["t1"], -1.0, v["t2"], mul, sub))
                tt(v["xr"], v["xr"], v["den"], mul)
                tt(v["xi"], v["xi"], v["den"], mul)
                tt(v["t1"], v["cr"], v["xr"], mul)
                tt(v["t2"], v["ci"], v["xi"], mul)
                tt(v["t3"], v["t1"], v["t2"], sub)
                ts(v["ctr"], v["t3"], 2.0, None, mul)
                tt(v["t1"], v["cr"], v["xi"], mul)
                tt(v["t2"], v["ci"], v["xr"], mul)
                tt(v["t3"], v["t1"], v["t2"], add)
                ts(v["cti"], v["t3"], 2.0, None, mul)
                tt(v["t1"], v["ctr"], v["re"], mul)
                tt(v["t2"], v["cti"], v["im"], mul)
                tt(v["t3"], v["t1"], v["t2"], sub)
                tt(MR[:], v["t3"], v["ctr"], add)
                ts(MRN[:], MR[:], -1.0, None, mul)
                tt(v["t1"], v["ctr"], v["im"], mul)
                tt(v["t2"], v["cti"], v["re"], mul)
                tt(v["t3"], v["t1"], v["t2"], add)
                tt(MI[:], v["t3"], v["cti"], add)
                link(ve.memset(CM[:], 0.0))
                for g in range(2):
                    q = slice(g * NST, (g + 1) * NST)
                    link(ve.tensor_copy(CM[q, :, 0, g], v["ctr"][q, :]))
                    ts(CM[q, :, 1, g], v["cti"][q, :], -1.0, None, mul)
                link(ve.tensor_copy(CMH[:], CM[:]))
                tt(CML[:], CM[:], CMH[:], sub)


def stage_s4d_states(nc, turns, DP, CMH, CML, MR, MRN, MI, ident, anti, XN, KT, S, v_dram):
    KP = 7
    with Core(nc) as k:
        lag = k.sb("c_lag", [P, P])
        hpi = k.sb("c_hpi", [P, 1])
        ea = [k.sb(f"c_ea{b}", [P, GH, P]) for b in range(2)]
        fr = [k.sb(f"c_fr{b}", [P, GH, P]) for b in range(2)]
        co = [k.sb(f"c_co{b}", [P, GH, P]) for b in range(2)]
        si = [k.sb(f"c_si{b}", [P, GH, P]) for b in range(2)]
        rn = k.sb("c_rn", [P, GH, P])
        V = [k.sb(f"c_v{b}", [P, 2, GH, P]) for b in range(2)]
        VP = [k.sb(f"c_vp{b}", [P, 2, 2, GH, P], BF16) for b in range(2)]
        VT = k.sb("c_vt", [P, 4, 4, P])
        xg = k.sb("c_xg", [P, NC, 2, GH])
        t1, t2 = k.sb("c_t1", [P, GH, NC]), k.sb("c_t2", [P, GH, NC])
        xp = k.ps("c_xp", [P, NC, 2, GH])
        vtp = k.ps("c_vtp", [P, 4, 4, P])
        ktp = k.ps("c_ktp", [P, GH, 2])
        bp = [k.ps(f"c_bp{b}", [P, 2, GH, NC]) for b in range(2)]
        pool_link, ve_link, act_link = k.sem("c_pool"), k.sem("c_dve"), k.sem("c_act")
        st_link, v_half, kt_taken = k.sem("c_sums"), k.sem("c_v_half"), k.sem("c_kt_taken")
        lag_ready, ea_ready = k.sem("c_lag_ready"), k.sem("c_ea_ready")
        fr_ready, trig_ready = k.sem("c_fr_ready"), k.sem("c_trig_ready")
        v_ready, v_stored = k.sem("c_v_ready"), [k.sem(f"c_v_stored{b}") for b in range(2)]
        xp_ready, xg_ready = k.sem("c_xp_ready"), k.sem("c_xg_ready")
        vtp_ready, vt_ready = k.sem("c_vtp_ready"), k.sem("c_vt_ready")
        vh_ready, vl_ready = k.sem("c_vh_ready"), k.sem("c_vl_ready")
        kt_ready, bp_ready, s_ready = k.sem("c_kt_ready"), k.sem("c_bp_ready"), k.sem("c_s_ready")
        lags = lag[:].unsqueeze(1).to_broadcast([P, GH, P])

        def columns(a, g, n):
            return a[:, bass.ds(g * GH, GH)].unsqueeze(2).to_broadcast([P, GH, n])

        def groups(eng, step):
            step(0, 0, 0)
            step(1, 1, 1)
            with eng.Fori(1, NG // 2 - 1) as i:
                for b in range(2):
                    step(2 * i + b, b, 2)
            step(NG - 2, 0, 2)
            step(NG - 1, 1, NG - 1)

        with nc.Block() as block:

            @block.gpsimd
            def _(pool):
                link = Chain(pool, pool_link)
                link(pool.iota(lag[:], pattern=[[1, P]], base=0, channel_multiplier=0,
                               allow_small_or_imprecise_dtypes=True))
                link(pool.memset(hpi[:], PI / 2))
                pool.sem_inc(lag_ready, 1)
                for b in range(2):
                    link(pool.memset(ea[b][:, :, 0:1], 1.0))

                def magnitudes(g, b, wait):
                    if wait:
                        pool.wait_ge(v_ready, g - 1)
                    for m in range(KP):
                        n = 1 << m
                        ins = pool.tensor_tensor(ea[b][:, :, n:2 * n], ea[b][:, :, 0:n],
                                                 columns(DP[:, m, :], g, n), ALU.mult)
                        if m < KP - 1:
                            ins.then_inc(pool_link, 1)
                            pool.wait_ge(pool_link, link.n + (KP - 1) * g + m + 1)
                        else:
                            ins.then_inc(ea_ready, 1)

                def step(g, b, at):
                    if at != NG - 1:
                        magnitudes(g + 1, 1 - b, at >= 1)
                    if at >= 2:
                        pool.wait_ge(v_stored[b], 8 * (g - b) if at == 2 else 8 * (NG - 2))
                        pool.wait_ge(kt_ready, g - 1)
                    pool.wait_ge(vh_ready, g + 1)
                    pool.tensor_tensor(VP[b][:, 1], V[b][:], VP[b][:, 0], ALU.subtract).then_inc(vl_ready, 1)
                magnitudes(0, 0, False)
                groups(pool, step)

            @block.vector
            def _(ve):
                ve.wait_ge(lag_ready, 1)

                def phase(g, b):
                    ve.tensor_tensor(fr[b][:], columns(turns, g, P), lags, ALU.mult).then_inc(ve_link, 1)
                    ve.wait_ge(ve_link, 2 * g + 1)
                    ve.tensor_scalar(rn[:], fr[b][:], MAGIC, MAGIC, ALU.add, ALU.subtract).then_inc(ve_link, 1)
                    ve.wait_ge(ve_link, 2 * g + 2)
                    ve.tensor_tensor(fr[b][:], fr[b][:], rn[:], ALU.subtract).then_inc(fr_ready, 1)

                def add_to_states(g, b):
                    ve.wait_ge(bp_ready, g + 1)
                    br, bi = bp[b][:, 0, :, :], bp[b][:, 1, :, :]
                    for r, (m1, m2) in enumerate(((MR, MI), (MI, MRN))):
                        ve.tensor_tensor(t1[:], br, columns(m1, g, NC), ALU.mult).then_inc(st_link, 1)
                        ve.tensor_tensor(t2[:], bi, columns(m2, g, NC), ALU.mult).then_inc(st_link, 1)
                        ve.wait_ge(st_link, 6 * g + 3 * r + 2)
                        o = S[:, :, r, bass.ds(g * GH, GH)].rearrange("p c h -> p h c")
                        if r == 0:
                            ins = ve.tensor_tensor(o, t1[:], t2[:], ALU.subtract)
                        else:
                            ins = ve.tensor_tensor(o, t2[:], t1[:], ALU.subtract)
                        ins.then_inc(st_link, 1)
                        ve.wait_ge(st_link, 6 * g + 3 * r + 3)
                    ve.sem_inc(s_ready, 1)

                def step(g, b, at):
                    if at != NG - 1:
                        phase(g + 1, 1 - b)
                    ve.wait_ge(ea_ready, g + 1)
                    ve.wait_ge(trig_ready, g + 1)
                    if at >= 2:
                        ve.wait_ge(vl_ready, g - 1)
                    ve.tensor_tensor(V[b][:, 0, :, :], ea[b][:], co[b][:], ALU.mult).then_inc(v_half, 1)
                    ve.tensor_tensor(V[b][:, 1, :, :], ea[b][:], si[b][:], ALU.mult).then_inc(v_ready, 1)
                    if at >= 1:
                        add_to_states(g - 1, 1 - b)
                phase(0, 0)
                groups(ve, step)
                add_to_states(NG - 1, 1)

            @block.scalar
            def _(act):
                act.preload_act_table(ACT.Sin)
                act.wait_ge(lag_ready, 1)

                def trig(g, b, wait):
                    act.wait_ge(fr_ready, g + 1)
                    if wait:
                        act.wait_ge(v_ready, g - 1)
                    act.activation(si[b][:], fr[b][:], ACT.Sin, scale=TWO_PI).then_inc(act_link, 1)
                    act.wait_ge(act_link, 2 * g + 1)
                    act.activation(fr[b][:], fr[b][:], ACT.Abs).then_inc(act_link, 1)
                    act.wait_ge(act_link, 2 * g + 2)
                    act.activation(co[b][:], fr[b][:], ACT.Sin, scale=-TWO_PI, bias=hpi[:]).then_inc(trig_ready, 1)

                def take_taps(g):
                    act.wait_ge(kt_ready, g + 1)
                    act.copy(KT[:, :, bass.ds(g * GH, GH)], ktp[:].rearrange("p h g -> p g h")
                             ).then_inc(kt_taken, 1)

                def step(g, b, at):
                    act.wait_ge(v_ready, g + 1)
                    if at >= 2:
                        act.wait_ge(v_stored[b], 8 * (g - b) if at == 2 else 8 * (NG - 2))
                    act.copy(VP[b][:, 0], V[b][:]).then_inc(vh_ready, 1)
                    if at != NG - 1:
                        trig(g + 1, 1 - b, at >= 1)
                    if at >= 1:
                        act.wait_ge(bp_ready, g)
                    act.wait_ge(xp_ready, g + 1)
                    act.copy(xg[:], xp[:]).then_inc(xg_ready, 1)
                    act.wait_ge(vtp_ready, g + 1)
                    for q in range(4):
                        ins = act.copy(VT[:, q, :, :], vtp[:, q, :, :])
                    ins.then_inc(vt_ready, 1)
                    if at >= 1:
                        take_taps(g - 1)
                trig(0, 0, False)
                groups(act, step)
                take_taps(NG - 1)

            @block.tensor
            def _(pe):
                def taps(g, b, wait):
                    pe.wait_ge(vl_ready, g + 1)
                    if wait:
                        pe.wait_ge(kt_taken, g)
                    for h in range(GH):
                        for n, (r, part, c) in enumerate((r, part, c) for r in range(2)
                                                         for part, c in ((0, CMH), (0, CML), (1, CMH))):
                            last = pe.matmul(ktp[:, h, :], VP[b][:, part, r, h, :], c[:, g * GH + h, r, :],
                                             start=(n == 0), stop=(n == 5))
                    last.then_inc(kt_ready, 1)

                def step(g, b, at):
                    pe.matmul(xp[:], anti[:], XN4[:, :, :, bass.ds(g * GH, GH)],
                              start=True, stop=True).then_inc(xp_ready, 1)
                    pe.wait_ge(v_ready, g + 1)
                    for m in range(2 * GH):
                        last = pe.transpose(vtp[:, m // 4, m % 4, :], V[b][:, m // GH, m % GH, :], ident[:])
                    last.then_inc(vtp_ready, 1)
                    if at >= 1:
                        taps(g - 1, 1 - b, at >= 2)
                    pe.wait_ge(xg_ready, g + 1)
                    pe.wait_ge(vt_ready, g + 1)
                    if at >= 2:
                        pe.wait_ge(s_ready, g - 1)
                    for m in range(2 * GH):
                        for q in range(2):
                            half = slice(q * NST, (q + 1) * NST)
                            last = pe.matmul(bp[b][half, m // GH, m % GH, :], VT[:, m // 4, m % 4, half],
                                             xg[:, :, q, m % GH], start=True, stop=True)
                    last.then_inc(bp_ready, 1)
                XN4 = XN[:].rearrange("p c (g h) -> p c g h", g=2)
                groups(pe, step)
                taps(NG - 1, 1, True)

            @block.sync
            def _(sp):
                def store(g, b, at):
                    sp.wait_ge(vl_ready, g + 1)
                    sp.dma_start(v_dram[g], VP[b][:].rearrange("p t r h l -> p (t r h l)")).then_inc(v_stored[b], 16)
                groups(sp, store)
                for b in range(2):
                    sp.wait_ge(v_stored[b], 8 * NG)


def stage_s4d_scan(nc, WR, WQ, S, KT, ident, kp_dram):
    with Core(nc) as k:
        a, q = k.sb("d_a", [P, 2, P]), k.sb("d_q", [P, 2, P])
        kp = k.sb("d_kp", [P, 2, 2 * P, 2], BF16)
        ktt = k.ps("d_ktt", [P, 2, P])
        link, zeroed, turned = k.sem("d_link"), k.sem("d_zeroed"), k.sem("d_turned")
        kph_ready = k.sem("d_kph_ready")
        kp_ready, kp_stored = k.sem("d_kp_ready"), k.sem("d_kp_stored")
        with nc.Block() as block:

            @block.vector
            def _(ve):
                ve.wait_ge(kph_ready, 1)
                taps = kp[:, :, P - 1:2 * P - 1, :]
                ve.tensor_tensor(taps[:, :, :, 1], ktt[:], taps[:, :, :, 0], ALU.subtract).then_inc(kp_ready, 1)
                with ve.Fori(1, NC - 1) as c:
                    before, here = S[:, c - 1, :, :], S[:, c, :, :]
                    n = 4 * c - 4
                    ve.tensor_tensor(a[:], before, WR[:], ALU.mult).then_inc(link, 1)
                    for r in range(2):
                        ins = ve.tensor_tensor(q[:, r, :], S[:, c - 1, 1 - r, :], WQ[:, r, :], ALU.mult)
                    ins.then_inc(link, 1)
                    ve.wait_ge(link, n + 1)
                    ve.tensor_tensor(a[:], a[:], here, ALU.add).then_inc(link, 1)
                    ve.wait_ge(link, n + 3)
                    ve.tensor_tensor(here, a[:], q[:], ALU.add).then_inc(link, 1)
                    ve.wait_ge(link, n + 4)

            @block.gpsimd
            def _(pool):
                pool.memset(kp[:], 0.0).then_inc(zeroed, 1)

            @block.tensor
            def _(pe):
                for g in range(2):
                    last = pe.transpose(ktt[:, g, :], KT[:, g, :], ident[:])
                last.then_inc(turned, 1)

            @block.scalar
            def _(act):
                act.wait_ge(zeroed, 1)
                act.wait_ge(turned, 1)
                act.copy(kp[:, :, P - 1:2 * P - 1, 0], ktt[:]).then_inc(kph_ready, 1)

            @block.sync
            def _(sp):
                sp.wait_ge(kp_ready, 1)
                sp.dma_start(kp_dram.rearrange("(g h) m -> h g m", g=2),
                             kp[:].rearrange("p g m t -> p g (m t)").bitcast(F32)).then_inc(kp_stored, 16)
                sp.wait_ge(kp_stored, 16)


def stage_s4d_outputs(nc, S, XN, anti, v_dram, kp_dram, Y):
    with Core(nc) as k:
        V = [k.sb(f"e_v{b}", [P, 2, 2, GH, P], BF16) for b in range(2)]
        tz = [k.sb(f"e_tz{b}", [P, 2, GH, P]) for b in range(2)]
        sg = [k.sb(f"e_sg{b}", [P, 2, GH, 2, NC], BF16) for b in range(2)]
        xg = [k.sb(f"e_xg{b}", [P, 2, NC, 2, GH], BF16) for b in range(2)]
        xp = [k.ps(f"e_xp{b}", [P, NC, 2, GH]) for b in range(2)]
        yp = [[k.ps(f"e_yp{b}{q}", [P, GH * 2, NC]) for q in range(2)] for b in range(2)]
        loaded = [k.sem(f"e_loaded{b}") for b in range(2)]
        xp_ready, xh_ready, sh_ready = k.sem("e_xp_ready"), k.sem("e_xh_ready"), k.sem("e_sh_ready")
        xl_ready, sl_ready = k.sem("e_xl_ready"), k.sem("e_sl_ready")
        yp_ready, y_ready = k.sem("e_yp_ready"), k.sem("e_y_ready")
        PARTS = ((0, 0), (0, 1), (1, 0))

        def groups(eng, step):
            for b in range(2):
                step(b, b, True)
            with eng.Fori(1, NG // 2) as i:
                for b in range(2):
                    step(2 * i + b, b, False)

        def states_of(g):
            return S[:, :, :, bass.ds(g * GH, GH)].rearrange("p c r h -> p h r c")

        with nc.Block() as block:

            @block.sync
            def _(sp):
                def load(g, b, first):
                    if not first:
                        sp.wait_ge(yp_ready, g - 1)
                    sp.dma_start(V[b][:].rearrange("p t r h l -> p (t r h l)"), v_dram[g]).then_inc(loaded[b], 16)
                    for q in range(2):
                        rows = bass.AP(kp_dram.tensor, (q * P + g * GH) * 2 * P, [[1, P], [2 * P, GH], [1, P]])
                        sp.dma_start(tz[b][:, q, :, :], rows).then_inc(loaded[b], 16)
                groups(sp, load)

            @block.scalar
            def _(act):
                def step(g, b, first):
                    if not first:
                        act.wait_ge(yp_ready, g - 1)
                    act.wait_ge(xp_ready, g + 1)
                    act.copy(xg[b][:, 0], xp[b][:]).then_inc(xh_ready, 1)
                    act.copy(sg[b][:, 0], states_of(g)).then_inc(sh_ready, 1)
                groups(act, step)

            @block.gpsimd
            def _(pool):
                def step(g, b, first):
                    pool.wait_ge(sh_ready, g + 1)
                    pool.tensor_tensor(sg[b][:, 1], states_of(g), sg[b][:, 0], ALU.subtract).then_inc(sl_ready, 1)
                groups(pool, step)

            @block.tensor
            def _(pe):
                XN4 = XN[:].rearrange("p c (g h) -> p c g h", g=2)

                def turn(g, b):
                    pe.matmul(xp[b][:], anti[:], XN4[:, :, :, bass.ds(g * GH, GH)],
                              start=True, stop=True).then_inc(xp_ready, 1)

                def outputs(g, b, first):
                    pe.wait_ge(xl_ready, g + 1)
                    pe.wait_ge(sl_ready, g + 1)
                    pe.wait_ge(loaded[b], 24 * (g - b) + 48)
                    if not first:
                        pe.wait_ge(y_ready, g - 1)
                    for h in range(GH):
                        for q in range(2):
                            rows = slice(q * NST, (q + 1) * NST)
                            o = yp[b][q][:, h, :]
                            taps = tz[b][:, q, h, :].bitcast(BF16).rearrange("p (l t) -> p t l", t=2)
                            for n, (i, j) in enumerate(PARTS):
                                pe.matmul(o, taps[:, i, :], xg[b][:, j, :, q, h], start=(n == 0), stop=False)
                            for n, (r, i, j) in enumerate((r, i, j) for r in range(2) for i, j in PARTS):
                                last = pe.matmul(o[:, 1:NC], V[b][rows, i, r, h, :], sg[b][rows, j, h, r, 0:NC - 1],
                                                 start=False, stop=(n == 5))
                    last.then_inc(yp_ready, 1)

                turn(0, 0)
                turn(1, 1)
                for b in range(2):
                    outputs(b, b, True)
                    turn(2 + b, b)
                with pe.Fori(1, NG // 2 - 1) as i:
                    for b in range(2):
                        outputs(2 * i + b, b, False)
                        turn(2 * i + b + 2, b)
                outputs(NG - 2, 0, False)
                outputs(NG - 1, 1, False)

            @block.vector
            def _(ve):
                Y4 = Y[:].rearrange("p c (g h) -> p g h c", g=2)

                def part(g, b):
                    ve.wait_ge(xh_ready, g + 1)
                    ve.tensor_tensor(xg[b][:, 1], xp[b][:], xg[b][:, 0], ALU.subtract).then_inc(xl_ready, 1)

                def take(g, b):
                    ve.wait_ge(yp_ready, g + 1)
                    for q in range(2):
                        ins = ve.tensor_copy(Y4[:, q, bass.ds(g * GH, GH), :], yp[b][q][:, 0:GH, :])
                    ins.then_inc(y_ready, 1)

                part(0, 0)
                part(1, 1)
                with ve.Fori(0, NG // 2 - 1) as i:
                    for b in range(2):
                        take(2 * i + b, b)
                        part(2 * i + b + 2, b)
                take(NG - 2, 0)
                take(NG - 1, 1)


def stage_mix0(nc, x, d_skip, ln_w, ln_b, XN, G0, Y, x1_dram, xn1_dram):
    BC = 4
    NBK = NC // BC
    with Core(nc) as k:
        d1, lw, lb = k.sb("f_d1", [P, D]), k.sb("f_lw", [P, D]), k.sb("f_lb", [P, D])
        xr = [k.sb(f"f_xr{b}", [P, BC, D]) for b in range(2)]
        stats = k.sb("f_stats", [P, NC, 6])
        mean, rstd, tmp = k.sb("f_mean", [P, NC]), k.sb("f_rstd", [P, NC]), k.sb("f_tmp", [P, NC])
        shift = k.sb("f_shift", [P, NC])
        rows_in = k.sem("f_rows_in")
        x_in = [k.sem(f"f_x_in{b}") for b in range(2)]
        ve_link, d1_ready = k.sem("f_dve"), k.sem("f_d1_ready")
        skip_ready, var_ready, std_ready = k.sem("f_skip_ready"), k.sem("f_var_ready"), k.sem("f_std_ready")
        scale_ready, norm_ready, lnw_ready = k.sem("f_scale_ready"), k.sem("f_norm_ready"), k.sem("f_lnw_ready")
        x1_ready, xn1_ready, stored = k.sem("f_x1_ready"), k.sem("f_xn1_ready"), k.sem("f_stored")
        out_link = k.sem("f_out_link")

        def rows(a):
            return a[:].unsqueeze(1).to_broadcast([P, BC, D])

        def block_of(a, i):
            return a[:, bass.ds(i * BC, BC), :]

        def dram_block(a, i):
            return a[bass.ds(i * BC * P, BC * P), :].rearrange("(c s) d -> s c d", s=P)

        with nc.Block() as block:

            @block.sync
            def _(sp):
                for dst, src in ((d1, d_skip), (lw, ln_w), (lb, ln_b)):
                    sp.dma_start(dst[:], src.partition_broadcast(P)).then_inc(rows_in, 16)
                for b in range(2):
                    sp.dma_start(xr[b][:], dram_block(x[0], b)).then_inc(x_in[b], 16)
                with sp.Fori(1, NBK // 2) as i:
                    for b in range(2):
                        sp.wait_ge(x1_ready, 2 * i + b - 1)
                        sp.dma_start(xr[b][:], dram_block(x[0], 2 * i + b)).then_inc(x_in[b], 16)

            @block.gpsimd
            def _(pool):
                pool.wait_ge(d1_ready, 1)
                with pool.Fori(0, NBK) as i:
                    pool.tensor_tensor(block_of(XN, i), block_of(XN, i), rows(d1), ALU.mult).then_inc(skip_ready, 1)
                with pool.Fori(0, NBK) as i:
                    pool.wait_ge(norm_ready, i + 1)
                    pool.tensor_tensor(block_of(Y, i), block_of(Y, i), rows(lw), ALU.mult).then_inc(lnw_ready, 1)

            @block.scalar
            def _(act):
                act.preload_act_table(ACT.Sqrt)
                act.wait_ge(var_ready, 1)
                act.activation(rstd[:], rstd[:], ACT.Sqrt).then_inc(std_ready, 1)
                act.wait_ge(scale_ready, 1)
                with act.Fori(0, NBK) as i:
                    for j in range(BC):
                        c = i * BC + j
                        ins = act.activation(Y[:, c, :], Y[:, c, :], ACT.Identity, bias=shift[:, bass.ds(c, 1)],
                                             scale=rstd[:, bass.ds(c, 1)])
                    ins.then_inc(norm_ready, 1)
                with act.Fori(0, NBK) as i:
                    act.wait_ge(x1_ready, i + 1)
                    act.dma_start(dram_block(x1_dram, i), block_of(Y, i)).then_inc(stored, 16)
                act.wait_ge(var_ready, 2)
                act.activation(rstd[:], rstd[:], ACT.Sqrt).then_inc(std_ready, 1)
                with act.Fori(0, NBK) as i:
                    act.wait_ge(xn1_ready, i + 1)
                    act.dma_start(dram_block(xn1_dram, i), block_of(XN, i)).then_inc(stored, 16)
                act.wait_ge(stored, 32 * NBK)

            @block.vector
            def _(ve):
                link = Chain(ve, ve_link)
                ve.wait_ge(rows_in, 48)
                ve.tensor_scalar(d1[:], d1[:], 1.0, None, ALU.add).then_inc(d1_ready, 1)

                def statistics(src, i):
                    for j in range(BC):
                        ve.bn_stats(stats[:, i * BC + j, :], src[:, i * BC + j, :])

                def scales(n):
                    ve.drain()
                    moments_to_scale(ve, link, stats, mean[:], rstd[:], tmp[:])
                    ve.sem_inc(var_ready, 1)
                    ve.wait_ge(std_ready, n)
                    link(ve.reciprocal(rstd[:], rstd[:]))
                    link(ve.scalar_tensor_tensor(shift[:], mean[:], -1.0, rstd[:], ALU.mult, ALU.mult))

                with ve.Fori(0, NBK) as i:
                    ve.wait_ge(skip_ready, i + 1)
                    ve.tensor_tensor(block_of(Y, i), block_of(Y, i), block_of(XN, i), ALU.add).then_inc(out_link, 1)
                    ve.wait_ge(out_link, i + 1)
                    statistics(Y, i)
                scales(1)
                ve.sem_inc(scale_ready, 1)
                with ve.Fori(0, NBK // 2) as i:
                    for b in range(2):
                        n = 2 * i + b
                        y = block_of(Y, n)
                        ve.wait_ge(lnw_ready, n + 1)
                        ve.tensor_tensor(y, y, rows(lb), ALU.add).then_inc(out_link, 1)
                        ve.wait_ge(out_link, 2 * n + NBK + 1)
                        ve.tensor_tensor(y, y, block_of(G0, n), ALU.mult).then_inc(out_link, 1)
                        ve.wait_ge(out_link, 2 * n + NBK + 2)
                        ve.wait_ge(x_in[b], 16 * i + 16)
                        ve.tensor_tensor(y, y, xr[b][:], ALU.add).then_inc(x1_ready, 1)
                        ve.wait_ge(x1_ready, n + 1)
                        statistics(Y, n)
                scales(2)
                with ve.Fori(0, NBK) as i:
                    for j in range(BC):
                        c = i * BC + j
                        ins = ve.tensor_scalar(XN[:, c, :], Y[:, c, :], mean[:, bass.ds(c, 1)],
                                               rstd[:, bass.ds(c, 1)], ALU.subtract, ALU.mult)
                    ins.then_inc(xn1_ready, 1)

NJ = T // P
NH, DH = 8, 32
NE, TOPK = 32, 4
HM, HS = 128, 256
CAP = 4 * T * TOPK // NE
GT = 256
NGR = T * TOPK // GT + NE
SLOTS = NGR * GT
SHIFTS = [64, 32, 16, 8, 4, 2, 1]
OFFSETS = [0] + [1 << i for i in range(12)]
POOL_SCORES = [9, 10, 11, 12]
POOL_SUMS = [6, 7, 8, 9, 10, 11, 12]
KCONV = 7
LEAD = KCONV - 1
FAR = 1.0e30


def token_rows(a, j):
    return a.rearrange("(p j) d -> p j d", j=NJ)[:, bass.ds(j, 1), :].rearrange("p a d -> p (a d)")


def by_twos(eng, n, step):
    for b in range(2):
        step(b, b, True)
    with eng.Fori(1, n // 2) as i:
        for b in range(2):
            step(2 * i + b, b, False)


def stage_projections(nc, w_qkv, w_gate, ws1, ws2, ws3, xn1_dram, z_dram, vt_dram, ident, Q, K, V, L, KVB):
    KD = D // P
    with Core(nc) as k:
        wqv, wkg = k.sb("g_wqv", [P, KD, 2 * D]), k.sb("g_wkg", [P, KD, D + NE])
        w1s, w3s, w2s = k.sb("g_w1", [P, KD, HS]), k.sb("g_w3", [P, KD, HS]), k.sb("g_w2", [P, KD, D])
        xf = [k.sb(f"g_xf{b}", [P, D]) for b in range(2)]
        xT = [k.sb(f"g_xT{b}", [P, KD, P]) for b in range(2)]
        low = [k.sb(f"g_low{b}", [P, D]) for b in range(2)]
        fk = [k.sb(f"g_fk{b}", [P, D]) for b in range(2)]
        vs = [k.sb(f"g_vs{b}", [P, D + 1]) for b in range(2)]
        th = [k.sb(f"g_th{b}", [P, KD, P]) for b in range(2)]
        gate = [k.sb(f"g_gate{b}", [P, KD, P]) for b in range(2)]
        zs = [k.sb(f"g_zs{b}", [P, D]) for b in range(2)]
        vt = [k.sb(f"g_vt{b}", [P, KD, P]) for b in range(2)]
        tp = k.ps("g_tp", [P, KD, P])
        qvp = [k.ps(f"g_qvp{b}", [P, 2 * D]) for b in range(2)]
        kgp = k.ps("g_kgp", [P, D + NE])
        hp = k.ps("g_hp", [P, 2, KD, P])
        zvp = k.ps("g_zvp", [P, 2, D])
        zp, vtp = zvp[:, 0, :], zvp[:, 1, :]
        kv = [k.ps(f"g_kv{m}", [P, 2 * D]) for m in range(KD)]
        w_in, x_in = k.sem("g_w_in"), [k.sem(f"g_x_in{b}") for b in range(2)]
        ones_ready = k.sem("g_ones_ready")
        tp_ready, xT_ready, qv_ready, kg_ready = (k.sem(f"g_{n}_ready") for n in ("tp", "xT", "qv", "kg"))
        h_ready, th_ready, gate_ready, z_ready = (k.sem(f"g_{n}_ready") for n in ("h", "th", "gate", "z"))
        low_ready, ex_ready, fk_ready, vs_ready = (k.sem(f"g_{n}_ready") for n in ("low", "ex", "fk", "vs"))
        zs_ready, z_stored = k.sem("g_zs_ready"), [k.sem(f"g_z_stored{b}") for b in range(2)]
        kv_done, half_gate, v_copied = k.sem("g_kv_done"), k.sem("g_half_gate"), k.sem("g_v_copied")
        q_taken = k.sem("g_q_taken")

        def heads(a, j):
            return a[:, :, bass.ds(j, 1), :].rearrange("p h a d -> p h (a d)")

        with nc.Block() as block:

            @block.sync
            def _(sp):
                def store(j, b):
                    sp.dma_start(token_rows(z_dram, j), zs[b][:]).then_inc(z_stored[b], 16)
                    sp.dma_start(vt_dram[:, :, bass.ds(j, 1), :].rearrange("c m a p -> c m (a p)"), vt[b][:]
                                 ).then_inc(z_stored[b], 16)

                def step(j, b, first):
                    if not first:
                        sp.wait_ge(tp_ready, j - 1)
                    sp.dma_start(xf[b][:], token_rows(xn1_dram, j)).then_inc(x_in[b], 16)
                    if not first:
                        sp.wait_ge(zs_ready, j - 1)
                        store(j - 2, b)
                for i in range(2):
                    sp.dma_start(wqv[:, :, i * D:(i + 1) * D],
                                 w_qkv[:, 2 * i * D:2 * i * D + D].rearrange("(k p) n -> p k n", p=P)
                                 ).then_inc(w_in, 16)
                by_twos(sp, NJ, step)
                for b in range(2):
                    sp.wait_ge(zs_ready, NJ - 1 + b)
                    store(NJ - 2 + b, b)
                for b in range(2):
                    sp.wait_ge(z_stored[b], 16 * NJ)

            @block.gpsimd
            def _(pool):
                for b in range(2):
                    pool.memset(vs[b][:, D:D + 1], 1.0)
                pool.memset(KVB[:], 0.0).then_inc(ones_ready, 1)

                def step(j, b, first):
                    pool.wait_ge(vs_ready, j + 1)
                    pool.tensor_copy(heads(V, j), vs[b][:, 0:D].rearrange("p (h d) -> p h d", h=NH)
                                     ).then_inc(v_copied, 1)
                by_twos(pool, NJ, step)

            @block.tensor
            def _(pe):
                pe.wait_ge(w_in, 112)
                pe.wait_ge(ones_ready, 1)

                def transposes(j, b):
                    pe.wait_ge(x_in[b], 8 * (j - b) + 16)
                    for d in range(KD):
                        last = pe.transpose(tp[:, d, :], xf[b][:, d * P:(d + 1) * P], ident[:])
                    last.then_inc(tp_ready, 1)

                def products(j, b, first):
                    pe.wait_ge(xT_ready, j + 1)
                    if first < 2:
                        pe.wait_ge(q_taken, j - 1)
                    for d in range(KD):
                        last = pe.matmul(qvp[b][:], xT[b][:, d, :], wqv[:, d, :], start=(d == 0), stop=(d == KD - 1))
                    last.then_inc(qv_ready, 1)
                    if first < 3:
                        pe.wait_ge(fk_ready, j)
                    for d in range(KD):
                        last = pe.matmul(kgp[:], xT[b][:, d, :], wkg[:, d, :], start=(d == 0), stop=(d == KD - 1))
                    last.then_inc(kg_ready, 1)
                    if first < 3:
                        pe.wait_ge(gate_ready, j)
                    for s, w in enumerate((w1s, w3s)):
                        for m in range(KD):
                            for d in range(KD):
                                last = pe.matmul(hp[:, s, m, :], w[:, d, m * P:(m + 1) * P], xT[b][:, d, :],
                                                 start=(d == 0), stop=(d == KD - 1))
                    last.then_inc(h_ready, 1)

                def sums(j, b, at):
                    pe.wait_ge(fk_ready, j + 1)
                    pe.wait_ge(vs_ready, j + 1)
                    for m in range(KD):
                        last = pe.matmul(kv[m][:, 0:D + 1], fk[b][:, m * P:(m + 1) * P], vs[b][:],
                                         start=(at == 0), stop=(at == 2), skip_group_check=True)
                    last.then_inc(kv_done, 1)
                    pe.wait_ge(gate_ready, j + 1)
                    if at:
                        pe.wait_ge(zs_ready, j)
                    for m in range(KD):
                        pe.transpose(vtp[:, m * P:(m + 1) * P], vs[b][:, m * P:(m + 1) * P], ident[:])
                    for m in range(KD):
                        last = pe.matmul(zp, gate[b][:, m, :], w2s[:, m, :], start=(m == 0), stop=(m == KD - 1))
                    last.then_inc(z_ready, 1)

                transposes(0, 0)
                products(0, 0, 3)
                transposes(1, 1)
                products(1, 1, 2)
                sums(0, 0, 0)
                with pe.Fori(1, NJ // 2) as i:
                    for b in range(2):
                        j = 2 * i + b
                        transposes(j, b)
                        products(j, b, 0)
                        sums(j - 1, 1 - b, 1)
                sums(NJ - 1, 1, 2)

            @block.scalar
            def _(act):
                act.dma_start(wkg[:, :, 0:D], w_qkv[:, D:2 * D].rearrange("(k p) n -> p k n", p=P)
                              ).then_inc(w_in, 16)
                act.dma_start(wkg[:, :, D:D + NE], w_gate.rearrange("(k p) n -> p k n", p=P)).then_inc(w_in, 16)
                for dst, src in ((w1s, ws1), (w3s, ws3), (w2s, ws2)):
                    act.dma_start(dst[:], src.rearrange("(k p) n -> p k n", p=P)).then_inc(w_in, 16)
                act.preload_act_table(ACT.Exp)

                def store_z(j, b, wait):
                    act.wait_ge(z_ready, j + 1)
                    if wait:
                        act.wait_ge(z_stored[b], 16 * (j - b))
                    act.copy(vt[b][:].rearrange("p m c -> p (m c)"), vtp)
                    act.mul(zs[b][:], zp, 0.5).then_inc(zs_ready, 1)

                def step(j, b, first):
                    act.wait_ge(tp_ready, j + 1)
                    act.copy(xT[b][:], tp[:]).then_inc(xT_ready, 1)
                    act.wait_ge(qv_ready, j + 1)
                    if not first:
                        act.wait_ge(v_copied, j - 1)
                        act.wait_ge(kv_done, j - 1)
                    act.copy(vs[b][:, 0:D], qvp[b][:, D:2 * D]).then_inc(vs_ready, 1)
                    act.copy(heads(Q, j), qvp[b][:, 0:D].rearrange("p (h d) -> p h d", h=NH)).then_inc(q_taken, 1)
                    act.wait_ge(low_ready, j + 1)
                    act.activation(low[b][:], low[b][:], ACT.Exp).then_inc(ex_ready, 1)
                    act.wait_ge(h_ready, j + 1)
                    act.activation(th[b][:], hp[:, 0, :, :], ACT.Tanh, scale=0.5).then_inc(th_ready, 1)

                for b in range(2):
                    step(b, b, True)
                store_z(0, 0, False)
                step(2, 0, False)
                store_z(1, 1, False)
                step(3, 1, False)
                with act.Fori(2, NJ // 2) as i:
                    for b in range(2):
                        j = 2 * i + b
                        store_z(j - 2, b, True)
                        step(j, b, False)
                store_z(NJ - 2, 0, True)
                store_z(NJ - 1, 1, True)

            @block.vector
            def _(ve):
                def step(j, b, first):
                    ve.wait_ge(kg_ready, j + 1)
                    kj = kgp[:, 0:D]
                    ve.tensor_scalar(low[b][:], kj, 0.0, None, ALU.min).then_inc(low_ready, 1)
                    ve.tensor_copy(heads(K, j), kj.rearrange("p (h d) -> p h d", h=NH))
                    ve.tensor_copy(L[:, bass.ds(j, 1), :].rearrange("p a e -> p (a e)"), kgp[:, D:D + NE])
                    ve.wait_ge(ex_ready, j + 1)
                    if not first:
                        ve.wait_ge(kv_done, j - 1)
                    ve.scalar_tensor_tensor(fk[b][:], kj, 0.0, low[b][:], ALU.max, ALU.add).then_inc(fk_ready, 1)
                    ve.wait_ge(th_ready, j + 1)
                    ve.scalar_tensor_tensor(th[b][:], th[b][:], 1.0, hp[:, 0, :, :], ALU.add, ALU.mult
                                            ).then_inc(half_gate, 1)
                    ve.wait_ge(half_gate, j + 1)
                    if not first:
                        ve.wait_ge(z_ready, j - 1)
                    ve.tensor_tensor(gate[b][:], th[b][:], hp[:, 1, :, :], ALU.mult).then_inc(gate_ready, 1)
                by_twos(ve, NJ, step)
                ve.wait_ge(kv_done, NJ)
                ve.wait_ge(ones_ready, 1)
                for h in range(NH):
                    m, q = h // 4, slice(DH * (h % 4), DH * (h % 4) + DH)
                    ve.tensor_copy(KVB[q, m, q], kv[m][q, h * DH:(h + 1) * DH])
                    ve.tensor_copy(KVB[q, m, P + h % 4:P + h % 4 + 1], kv[m][q, D:D + 1])


def stage_routing(nc, L, WK, SIDX, GIDX, EXP):
    with Core(nc) as k:
        one = [P, NJ, NE]
        E, A, B, OH = k.sb("h_e", one), k.sb("h_a", one), k.sb("h_b", one), k.sb("h_oh", one)
        SL, PR = k.sb("h_sl", one), k.sb("h_pr", one)
        G1 = k.sb("h_g1", [P, NGR, NE])
        M8, I8 = k.sb("h_m8", [P, NJ, 8]), k.sb("h_i8", [P, NJ, 8], U32)
        IF = k.sb("h_if", [P, NJ, 8])
        mx, POS, KEPT = k.sb("h_mx", [P, NJ]), k.sb("h_pos", [P, NJ, TOPK]), k.sb("h_kept", [P, NJ, TOPK])
        ie, ig = k.sb("h_ie", [P, NE]), k.sb("h_ig", [P, NGR])
        tri, ones = k.sb("h_tri", [P, P]), k.sb("h_ones", [P, P])
        ng, sa, sb_, ex = k.sb("h_ng", [P, NE]), k.sb("h_sa", [P, NE]), k.sb("h_sb", [P, NE]), k.sb("h_ex", [P, NGR])
        cnt = k.ps("h_cnt", [P, 2, NE])
        pl, vl, const_ready = k.sem("h_pl"), k.sem("h_vl"), k.sem("h_const")
        shifted, exped, tot_ready, cnt_ready = (k.sem(f"h_{n}") for n in ("shifted", "exped", "tot", "cnt"))
        with nc.Block() as block:

            @block.gpsimd
            def _(pool):
                link = Chain(pool, pl)
                link(pool.iota(ie[:], pattern=[[1, NE]], base=0, channel_multiplier=0,
                               allow_small_or_imprecise_dtypes=True))
                link(pool.iota(ig[:], pattern=[[1, NGR]], base=0, channel_multiplier=0,
                               allow_small_or_imprecise_dtypes=True))
                link(pool.memset(ones[:], 1.0))
                link(pool.affine_select(out=tri[:], in_=ones[:], compare_op=ALU.is_ge, fill=0.0, base=-1,
                                        pattern=[[1, P]], channel_multiplier=-1))
                pool.sem_inc(const_ready, 1)

            @block.scalar
            def _(act):
                act.wait_ge(shifted, 1)
                act.activation(E[:], E[:], ACT.Exp).then_inc(exped, 1)

            @block.tensor
            def _(pe):
                pe.wait_ge(const_ready, 1)
                pe.wait_ge(tot_ready, 1)
                pe.matmul(cnt[:, 0, :], tri[:], sa[:], start=True, stop=True)
                pe.matmul(cnt[:, 1, :], ones[:], sa[:], start=True, stop=True).then_inc(cnt_ready, 1)

            @block.vector
            def _(ve):
                link = Chain(ve, vl)

                def tt(o, a, b, op):
                    link(ve.tensor_tensor(o, a, b, op))

                def ts(o, a, s1, s2, op0, op1=ALU.bypass):
                    link(ve.tensor_scalar(o, a, s1, s2, op0, op1))

                def over_e(a):
                    return a.unsqueeze(2).to_broadcast(one)

                def over_j(a):
                    return a.unsqueeze(1).to_broadcast(one)

                link(ve.tensor_reduce(mx[:], L[:], AX_X, ALU.max))
                ve.tensor_tensor(E[:], L[:], over_e(mx[:]), ALU.subtract).then_inc(shifted, 1)
                ve.wait_ge(exped, 1)
                link(ve.tensor_reduce(mx[:], E[:], AX_X, ALU.add))
                link(ve.reciprocal(mx[:], mx[:]))
                tt(E[:], E[:], over_e(mx[:]), ALU.mult)
                for j in range(NJ):
                    ve.max(M8[:, j, :], E[:, j, :])
                ve.drain()
                for j in range(NJ):
                    ve.max_index(I8[:, j, :], M8[:, j, :], E[:, j, :])
                ve.drain()
                link(ve.tensor_copy(IF[:], I8[:]))
                ve.wait_ge(const_ready, 1)
                for n in range(TOPK):
                    tt(OH[:], over_j(ie[:]), over_e(IF[:, :, n]), ALU.is_equal)
                    if n == 0:
                        link(ve.tensor_copy(A[:], OH[:]))
                    else:
                        tt(A[:], A[:], OH[:], ALU.add)
                link(ve.tensor_copy(SL[:], A[:]))
                a, b, s = A, B, 1
                while s < NJ:
                    link(ve.tensor_copy(b[:, 0:s, :], a[:, 0:s, :]))
                    tt(b[:, s:NJ, :], a[:, s:NJ, :], a[:, 0:NJ - s, :], ALU.add)
                    a, b, s = b, a, 2 * s
                link(ve.tensor_copy(sa[:], a[:, NJ - 1, :]))
                ve.sem_inc(tot_ready, 1)
                ve.wait_ge(cnt_ready, 1)
                tt(a[:], a[:], SL[:], ALU.subtract)
                tt(a[:], a[:], over_j(cnt[:, 0, :]), ALU.add)
                ts(ng[:], cnt[:, 1, :], float(CAP), None, ALU.min)
                ts(ng[:], ng[:], 1.0 / GT, (GT - 1.0) / GT - 0.5 + 0.5 / GT, ALU.mult, ALU.add)
                ts(ng[:], ng[:], MAGIC, MAGIC, ALU.add, ALU.subtract)
                link(ve.tensor_copy(sa[:], ng[:]))
                c, d, s = sa, sb_, 1
                while s < NE:
                    link(ve.tensor_copy(d[:, 0:s], c[:, 0:s]))
                    tt(d[:, s:NE], c[:, s:NE], c[:, 0:NE - s], ALU.add)
                    c, d, s = d, c, 2 * s
                tt(G1[:], c[:].unsqueeze(1).to_broadcast([P, NGR, NE]), ig[:].unsqueeze(2).to_broadcast([P, NGR, NE]),
                   ALU.is_le)
                link(ve.tensor_reduce(ex[:], G1[:], AX_X, ALU.add))
                ts(ex[:], ex[:], NE - 1.0, None, ALU.min)
                link(ve.tensor_copy(EXP[:], ex[:]))
                tt(d[:], c[:], ng[:], ALU.subtract)
                ts(d[:], d[:], float(GT), None, ALU.mult)
                ts(SL[:], a[:], float(CAP), 4.0 * SLOTS, ALU.is_ge, ALU.mult)
                tt(SL[:], SL[:], a[:], ALU.add)
                tt(SL[:], SL[:], over_j(d[:]), ALU.add)
                for n in range(TOPK):
                    tt(OH[:], over_j(ie[:]), over_e(IF[:, :, n]), ALU.is_equal)
                    tt(PR[:], OH[:], SL[:], ALU.mult)
                    link(ve.tensor_reduce(POS[:, :, n], PR[:], AX_X, ALU.add))
                link(ve.tensor_copy(SIDX[:], POS[:]))
                ts(KEPT[:], POS[:], float(SLOTS), None, ALU.is_lt)
                tt(WK[:], M8[:, :, 0:TOPK], KEPT[:], ALU.mult)
                tt(POS[:], POS[:], KEPT[:], ALU.mult)
                link(ve.tensor_copy(GIDX[:], POS[:]))


def stage_scatter_and_convolution(nc, conv_w, vt_dram, conv_dram, xn1_dram, xs_dram, ident, SIDX):
    KD = D // P
    BLK = 4
    with Core(nc) as k:
        VT = k.sb("i_vt", [P, KD, LEAD + NJ, P])
        cw = k.sb("i_cw", [P, KD, KCONV])
        dg = k.sb("i_dg", [P, KD, KCONV, P])
        cs = [k.sb(f"i_cs{m}", [P, BLK, P]) for m in range(KD)]
        cp = [k.ps(f"i_cp{m}", [P, BLK, P]) for m in range(KD)]
        vt_in, cw_in, led = k.sem("i_vt_in"), k.sem("i_cw_in"), k.sem("i_led")
        dg_ready, cp_ready, cs_ready = k.sem("i_dg_ready"), k.sem("i_cp_ready"), k.sem("i_cs_ready")
        conv_stored = k.sem("i_conv_stored")
        xr = [k.sb(f"i_x{b}", [P, D]) for b in range(2)]
        ix = [k.sb(f"i_ix{b}", [P, TOPK], U32) for b in range(2)]
        x_in = [k.sem(f"i_x_in{b}") for b in range(2)]
        ix_ready, sent = k.sem("i_ix_ready"), [k.sem(f"i_sent{b}") for b in range(2)]
        waited = k.sem("i_waited")
        with nc.Block() as block:

            @block.vector
            def _(ve):
                ve.memset(VT[:, :, 0:LEAD, 0:1], 0.0).then_inc(led, 1)
                ve.wait_ge(cw_in, 16)
                for m in range(KD):
                    for o in range(KCONV):
                        t = KCONV - 1 - o
                        ve.tensor_scalar(dg[:, m, o, :], ident[:], cw[:, m, t:t + 1], None, ALU.mult
                                         ).then_inc(dg_ready, 1)

            @block.tensor
            def _(pe):
                pe.wait_ge(led, 1)
                pe.wait_ge(dg_ready, KD * KCONV)
                pe.wait_ge(vt_in, 32 * KD)

                def step(i, first):
                    for m in range(KD):
                        if not first:
                            pe.wait_ge(cs_ready, KD * i - KD + m + 1)
                        for o in range(KCONV):
                            last = pe.matmul(cp[m][:], dg[:, m, o, :], VT[:, m, bass.ds(BLK * i + LEAD - o, BLK), :],
                                             start=(o == 0), stop=(o == KCONV - 1))
                        last.then_inc(cp_ready, 1)
                step(0, True)
                with pe.Fori(1, NJ // BLK) as i:
                    step(i, False)

            @block.scalar
            def _(act):
                act.dma_start(cw[:], conv_w.rearrange("(m c) t -> c m t", c=P)).then_inc(cw_in, 16)
                for m in range(KD):
                    act.dma_start(VT[:, m, LEAD:LEAD + NJ, :], vt_dram[:, m]).then_inc(vt_in, 16)
                    act.dma_start(VT[:, m, 0:LEAD, 1:P], vt_dram[:, m, NJ - LEAD:NJ, 0:P - 1]).then_inc(vt_in, 16)

                def step(i, first):
                    for m in range(KD):
                        act.wait_ge(cp_ready, KD * i + m + 1)
                        if not first:
                            act.wait_ge(conv_stored, 16 * KD * i)
                        act.copy(cs[m][:], cp[m][:]).then_inc(cs_ready, 1)
                    for m in range(KD):
                        act.wait_ge(cs_ready, KD * i + m + 1)
                        act.dma_start(conv_dram[:, m, bass.ds(BLK * i, BLK), :], cs[m][:]).then_inc(conv_stored, 16)
                step(0, True)
                with act.Fori(1, NJ // BLK) as i:
                    step(i, False)
                act.wait_ge(conv_stored, 16 * KD * NJ // BLK)

            @block.sync
            def _(sp):
                def step(j, b, first):
                    if not first:
                        sp.wait_ge(sent[b], 8 * TOPK * (j - b))
                    sp.dma_start(xr[b][:], token_rows(xn1_dram, j)).then_inc(x_in[b], 16)
                by_twos(sp, NJ, step)

            @block.gpsimd
            def _(pool):
                def step(j, b, first):
                    if not first:
                        pool.wait_ge(sent[b], 8 * TOPK * (j - b))
                        pool.sem_inc(waited, 1)
                    pool.tensor_copy(ix[b][:], SIDX[:, bass.ds(j, 1), :].rearrange("p a n -> p (a n)")
                                     ).then_inc(ix_ready, 1)
                    pool.wait_ge(ix_ready, j + 1)
                    pool.sem_inc(waited, 1)
                    pool.wait_ge(x_in[b], 8 * (j - b) + 16)
                    pool.sem_inc(waited, 1)
                    for n in range(TOPK):
                        pool.indirect_dma_start(xs_dram, bass.IndirectOffsetOnAxis(ix[b][:, n:n + 1], 0), xr[b][:],
                                                None, bounds_check=SLOTS - 1, oob_is_err=False
                                                ).then_inc(sent[b], 16)
                by_twos(pool, NJ, step)
                for b in range(2):
                    pool.wait_ge(sent[b], 8 * TOPK * NJ)


def stage_experts_and_attention(nc, w1, w2, w3, xs_dram, o_dram, ident, EXP, Q, K, V):
    KD = D // P
    PER = NGR // NH
    SCALE = float(DH) ** -0.5
    GATES_BESIDE_SCORES, GATES_BESIDE_SUMS = (1, 3, 4, 6, 8, 10, 12), (0, 1, 2, 4, 5)
    EXP_AT = len(GATES_BESIDE_SCORES) - 2
    with Core(nc) as k:
        KC, VC = (k.sb(n, [P, len(SHIFTS), NJ, DH]) for n in ("j_kc", "j_vc"))
        prod, acc = k.sb("j_prod", [P, NJ, DH]), k.sb("j_acc", [P, NJ, DH])
        pprod = [k.sb(f"j_pprod{i}", [P, NJ, DH]) for i in range(len(POOL_SCORES))]
        pacc = pprod[-1]
        SC, MASK = k.sb("j_sc", [P, len(OFFSETS), NJ]), k.sb("j_mask", [P, len(OFFSETS), NJ])
        PW = k.sb("j_pw", [P, len(POOL_SUMS), NJ])
        mx = k.sb("j_mx", [P, NJ])
        WA = [k.sb(f"j_wa{b}", [P, 2, KD, HM]) for b in range(2)]
        WB = [k.sb(f"j_wb{b}", [P, D]) for b in range(2)]
        xs = [k.sb(f"j_xs{b}", [P, 2, D]) for b in range(2)]
        xT = [k.sb(f"j_xT{b}", [P, KD, GT]) for b in range(2)]
        th = [k.sb(f"j_th{b}", [P, GT]) for b in range(2)]
        gate = [k.sb(f"j_gate{b}", [P, GT]) for b in range(2)]
        ob = [k.sb(f"j_ob{b}", [P, 2, D]) for b in range(2)]
        tp = [k.ps(f"j_tp{b}", [P, KD, GT]) for b in range(2)]
        hp = [k.ps(f"j_hp{b}", [P, 2, GT]) for b in range(2)]
        op = [k.ps(f"j_op{b}", [P, 2, D]) for b in range(2)]
        wa_in, wb_in, x_in = ([k.sem(f"j_{n}_in{b}") for b in range(2)] for n in ("wa", "wb", "x"))
        tp_ready, xT_ready, h_ready, th_ready = (k.sem(f"j_{n}_ready") for n in ("tp", "xT", "h", "th"))
        gate_ready, o_ready, ob_ready = (k.sem(f"j_{n}") for n in ("gated", "o", "ob"))
        stored = [k.sem(f"j_stored{b}") for b in range(2)]
        pl, vl, zeroed = k.sem("j_pl"), k.sem("j_vl"), k.sem("j_zeroed")
        k_in, v_in, multiplied = k.sem("j_k_in"), k.sem("j_v_in"), k.sem("j_multiplied")
        weighed, shifted, exped = (k.sem(f"j_{n}") for n in ("weighed", "shifted", "exped"))
        summed, whole = k.sem("j_summed"), k.sem("j_whole")

        def heads(eng, body):
            body(0, 0)
            with eng.Fori(1, NH - 1) as h:
                body(h, 1)
            body(NH - 1, 2)

        def head(a, h):
            return a[:, bass.ds(h, 1), :, :].rearrange("p a j d -> p (a j) d")

        def back(copies, a, h, o):
            if o == 0:
                return [(slice(0, NJ), head(a, h))]
            if o < NJ:
                return [(slice(0, o), copies[:, SHIFTS.index(1), NJ - o:NJ, :]),
                        (slice(o, NJ), head(a, h)[:, 0:NJ - o, :])]
            return [(slice(0, NJ), copies[:, SHIFTS.index(o // NJ), :, :])]

        def shifted_copies(eng, dst, src, h, sem, which=range(len(SHIFTS))):
            for i in which:
                m = SHIFTS[i]
                eng.dma_start(dst[m:P, i, :, :], head(src, h)[0:P - m]).then_inc(sem, 16)

        def two_of(i):
            return range(2 * i, min(2 * i + 2, len(SHIFTS)))

        COPIED = 16 * len(SHIFTS)

        class HeadChain:

            def __init__(self, eng, sem, before=0):
                self.eng, self.sem, self.before, self.per, self.n, self.h = eng, sem, before, None, 0, 0

            def start(self, h, which):
                if which == 1:
                    self.per = self.n
                self.h, self.n = h, 0

            def __call__(self, *steps):
                for ins in steps:
                    self.n += 1
                    ins.then_inc(self.sem, 1)
                done = self.before + self.n if self.per is None else self.before + self.per * self.h + self.n
                self.eng.wait_ge(self.sem, done)

        with nc.Block() as block:

            @block.sync
            def _(sp):
                def load_tokens(g, b, first):
                    if not first:
                        sp.wait_ge(tp_ready, g - 1)
                    sp.dma_start(xs[b][:], xs_dram[bass.ds(g * GT, GT), :].rearrange("(t p) d -> p t d", p=P)
                                 ).then_inc(x_in[b], 16)

                def load_weights(g, b, first):
                    e = sp.value_load(EXP[0:1, bass.ds(g, 1)], min_val=0, max_val=NE - 1)
                    if not first:
                        sp.wait_ge(h_ready, g - 1)
                    for i, w in enumerate((w1, w3)):
                        sp.dma_start(WA[b][:, i, :, :], w[bass.ds(e, 1)].rearrange("e (k p) n -> p (e k) n", p=P)
                                     ).then_inc(wa_in[b], 16)
                    if not first:
                        sp.wait_ge(o_ready, g - 1)
                    sp.dma_start(WB[b][:], w2[bass.ds(e, 1)].rearrange("e p n -> p (e n)")).then_inc(wb_in[b], 16)

                load_tokens(0, 0, True)
                load_tokens(1, 1, True)
                for b in range(2):
                    load_weights(b, b, True)
                    load_tokens(2 + b, b, False)
                with sp.Fori(1, NGR // 2 - 1) as i:
                    for b in range(2):
                        load_weights(2 * i + b, b, False)
                        load_tokens(2 * i + b + 2, b, False)
                for b in range(2):
                    load_weights(NGR - 2 + b, b, False)

            @block.tensor
            def _(pe):
                def transposes(g, b):
                    pe.wait_ge(x_in[b], 8 * (g - b) + 16)
                    for t in range(2):
                        for d in range(KD):
                            last = pe.transpose(tp[b][:, d, t * P:(t + 1) * P], xs[b][:, t, d * P:(d + 1) * P],
                                                ident[:])
                    last.then_inc(tp_ready, 1)

                def hidden(g, b):
                    pe.wait_ge(xT_ready, g + 1)
                    pe.wait_ge(wa_in[b], 16 * (g - b) + 32)
                    for i in range(2):
                        for d in range(KD):
                            last = pe.matmul(hp[b][:, i, :], WA[b][:, i, d, :], xT[b][:, d, :],
                                             start=(d == 0), stop=(d == KD - 1))
                    last.then_inc(h_ready, 1)

                def outputs(g, b, first):
                    pe.wait_ge(gate_ready, g + 1)
                    pe.wait_ge(wb_in[b], 8 * (g - b) + 16)
                    if not first:
                        pe.wait_ge(ob_ready, g - 1)
                    for t in range(2):
                        last = pe.matmul(op[b][:, t, :], gate[b][:, t * P:(t + 1) * P], WB[b][:],
                                         start=True, stop=True)
                    last.then_inc(o_ready, 1)

                def step(g, b, first):
                    transposes(g + 2, b)
                    hidden(g + 1, 1 - b)
                    outputs(g, b, first)

                transposes(0, 0)
                transposes(1, 1)
                hidden(0, 0)
                by_twos(pe, NGR - 2, step)
                hidden(NGR - 1, 1)
                outputs(NGR - 2, 0, False)
                outputs(NGR - 1, 1, False)

            @block.scalar
            def _(act):
                act.preload_act_table(ACT.Silu)
                act.wait_ge(zeroed, 1)
                shifted_copies(act, KC, K, 0, k_in)
                shifted_copies(act, VC, V, 0, v_in)

                def move_xT(g, b, wait):
                    act.wait_ge(tp_ready, g + 1)
                    if wait:
                        act.wait_ge(h_ready, g - 1)
                    act.copy(xT[b][:], tp[b][:]).then_inc(xT_ready, 1)

                def silu(g, b, wait):
                    act.wait_ge(h_ready, g + 1)
                    if wait:
                        act.wait_ge(gate_ready, g - 1)
                    act.activation(th[b][:], hp[b][:, 0, :], ACT.Silu).then_inc(th_ready, 1)

                def move_out(g, b, wait):
                    act.wait_ge(o_ready, g + 1)
                    if wait:
                        act.wait_ge(stored[b], 8 * (g - b))
                    act.copy(ob[b][:], op[b][:]).then_inc(ob_ready, 1)

                def store(g, b):
                    act.wait_ge(ob_ready, g + 1)
                    act.dma_start(o_dram[bass.ds(g * GT, GT), :].rearrange("(t p) d -> p t d", p=P), ob[b][:]
                                  ).then_inc(stored[b], 16)

                def body(h, which):
                    for n in range(PER):
                        g, b, end = h * PER + n, n % 2, which == 2 and n >= PER - 2
                        if not end:
                            move_xT(g + 2, b, True)
                        if which > 0 or n > 0:
                            store(g - 1, 1 - b)
                        if not (end and n == PER - 1):
                            silu(g + 1, 1 - b, which > 0 or n > 0)
                        move_out(g, b, which > 0 or n > 1)
                        if n == EXP_AT:
                            act.wait_ge(shifted, h + 1)
                            act.activation(SC[:], SC[:], ACT.Exp, scale=SCALE).then_inc(exped, 1)
                        if EXP_AT - 4 < n <= EXP_AT and which > 0:
                            act.wait_ge(whole, h)
                            shifted_copies(act, VC, V, h, v_in, two_of(n - EXP_AT + 3))
                        if EXP_AT <= n < EXP_AT + 4 and which < 2:
                            shifted_copies(act, KC, K, h + 1, k_in, two_of(n - EXP_AT))

                move_xT(0, 0, False)
                move_xT(1, 1, False)
                silu(0, 0, False)
                heads(act, body)
                store(NGR - 1, 1)
                for b in range(2):
                    act.wait_ge(stored[b], 8 * NGR)

            @block.gpsimd
            def _(pool):
                link = Chain(pool, pl)
                link(pool.memset(KC[:], 0.0))
                link(pool.memset(VC[:], 0.0))
                link(pool.memset(MASK[:], 0.0))
                for s, o in enumerate(OFFSETS):
                    link(pool.affine_select(out=MASK[:, s, :], in_=MASK[:, s, :], compare_op=ALU.is_ge, fill=-FAR,
                                            base=-o, pattern=[[1, NJ]], channel_multiplier=NJ))
                pool.sem_inc(zeroed, 1)

                def products(h, link):
                    pool.wait_ge(k_in, COPIED * h + COPIED)
                    for i, s in enumerate(POOL_SCORES):
                        link(*[pool.tensor_tensor(pprod[i][:, js, :], head(Q, h)[:, js, :], src, ALU.mult)
                               for js, src in back(KC, K, h, OFFSETS[s])])
                        pool.sem_inc(multiplied, 1)

                products(0, link)
                hlink = HeadChain(pool, pl, link.n)

                def body(h, which):
                    hlink.start(h, which)
                    pool.wait_ge(weighed, h + 1)
                    pool.wait_ge(v_in, COPIED * h + COPIED)
                    for i, s in enumerate(POOL_SUMS):
                        w = PW[:, i, :].unsqueeze(2).to_broadcast([P, NJ, DH])
                        dst = pprod[0] if i else pacc
                        hlink(*[pool.tensor_tensor(dst[:, js, :], src, w[:, js, :], ALU.mult)
                                for js, src in back(VC, V, h, OFFSETS[s])])
                        if i:
                            hlink(pool.tensor_tensor(pacc[:], pacc[:], pprod[0][:], ALU.add))
                    pool.wait_ge(summed, h + 1)
                    hlink(pool.tensor_tensor(head(K, h), acc[:], pacc[:], ALU.add))
                    pool.sem_inc(whole, 1)
                    if which < 2:
                        products(h + 1, hlink)
                heads(pool, body)

            @block.vector
            def _(ve):
                hlink = HeadChain(ve, vl)
                ve.wait_ge(zeroed, 1)

                def gated(g, b, wait):
                    ve.wait_ge(th_ready, g + 1)
                    if wait:
                        ve.wait_ge(o_ready, g - 1)
                    ve.tensor_tensor(gate[b][:], th[b][:], hp[b][:, 1, :], ALU.mult).then_inc(gate_ready, 1)

                def body(h, which):
                    hlink.start(h, which)
                    ve.wait_ge(k_in, COPIED * h + COPIED)
                    n = 0
                    own = [s for s in range(len(OFFSETS)) if s not in POOL_SCORES]
                    for i, s in enumerate(own + POOL_SCORES):
                        if s in POOL_SCORES:
                            src = pprod[POOL_SCORES.index(s)]
                            ve.wait_ge(multiplied, len(POOL_SCORES) * h + POOL_SCORES.index(s) + 1)
                        else:
                            src = prod
                            hlink(*[ve.tensor_tensor(prod[:, js, :], head(Q, h)[:, js, :], ks, ALU.mult)
                                    for js, ks in back(KC, K, h, OFFSETS[s])])
                        hlink(ve.tensor_reduce(SC[:, s, :], src[:], AX_X, ALU.add))
                        if i in GATES_BESIDE_SCORES:
                            gated(h * PER + n, n % 2, which > 0 or n > 1)
                            n += 1
                    by_token = SC[:].rearrange("p s j -> p j s")

                    def every(count):
                        return mx[:].unsqueeze(1).to_broadcast([P, count, NJ])

                    hlink(ve.tensor_tensor(SC[:], SC[:], MASK[:], ALU.add))
                    hlink(ve.tensor_reduce(mx[:], by_token, AX_X, ALU.max))
                    ve.tensor_tensor(SC[:], SC[:], every(len(OFFSETS)), ALU.subtract).then_inc(shifted, 1)
                    ve.wait_ge(exped, h + 1)
                    hlink(ve.tensor_reduce(mx[:], by_token, AX_X, ALU.add))
                    hlink(ve.reciprocal(mx[:], mx[:]))
                    first = POOL_SUMS[0]
                    hlink(ve.tensor_tensor(PW[:], SC[:, first:, :], every(len(POOL_SUMS)), ALU.mult))
                    ve.sem_inc(weighed, 1)
                    hlink(ve.tensor_tensor(SC[:, 0:first, :], SC[:, 0:first, :], every(first), ALU.mult))
                    ve.wait_ge(v_in, COPIED * h + COPIED)
                    for s in range(first):
                        w = SC[:, s, :].unsqueeze(2).to_broadcast([P, NJ, DH])
                        dst = prod if s else acc
                        hlink(*[ve.tensor_tensor(dst[:, js, :], src, w[:, js, :], ALU.mult)
                                for js, src in back(VC, V, h, OFFSETS[s])])
                        if s:
                            hlink(ve.tensor_tensor(acc[:], acc[:], prod[:], ALU.add))
                        if s in GATES_BESIDE_SUMS:
                            gated(h * PER + n, n % 2, True)
                            n += 1
                    ve.sem_inc(summed, 1)
                heads(ve, body)


def stage_mix1(nc, w_o, xn1_dram, x1_dram, z_dram, o_dram, conv_dram, ident, Q, K, KVB, WK, GIDX, out):
    KD = D // P
    RING = 4
    LW = P + 4
    with Core(nc) as k:
        wo = k.sb("m_wo", [P, KD, D])
        two, ring = range(2), range(RING)
        xr = [k.sb(f"m_xn{b}", [P, D]) for b in ring]
        x1 = [k.sb(f"m_x1{b}", [P, D]) for b in ring]
        zr = [k.sb(f"m_z{b}", [P, D]) for b in ring]
        cT = [k.sb(f"m_cT{b}", [P, KD, P]) for b in ring]
        ix = [k.sb(f"m_ix{b}", [P, TOPK], U32) for b in ring]
        gt = [k.sb(f"m_gt{b}", [P, TOPK, D]) for b in ring]
        ex = [k.sb(f"m_ex{b}", [P, D]) for b in two]
        fq = [k.sb(f"m_fq{b}", [P, D]) for b in two]
        fqT = [k.sb(f"m_fqT{b}", [P, KD, P]) for b in two]
        rz = [k.sb(f"m_rz{b}", [P, KD, 4]) for b in two]
        hs = [k.sb(f"m_h{b}", [P, D]) for b in two]
        hT = [k.sb(f"m_hT{b}", [P, KD, P]) for b in two]
        s1 = [k.sb(f"m_s1{b}", [P, D]) for b in two]
        th = [k.sb(f"m_th{b}", [P, D]) for b in two]
        res = [k.sb(f"m_res{b}", [P, D]) for b in two]
        qp = [k.ps(f"m_qp{b}", [P, KD, P]) for b in two]
        lp = [k.ps(f"m_lp{b}", [P, KD, LW]) for b in two]
        hp = [k.ps(f"m_hp{b}", [P, KD, P]) for b in two]
        ap = [k.ps(f"m_ap{b}", [P, D]) for b in two]
        wo_in, cT_in = k.sem("m_wo_in"), [k.sem(f"m_cT_in{b}") for b in ring]
        rows_in, got = [k.sem(f"m_rows_in{b}") for b in ring], [k.sem(f"m_got{b}") for b in ring]
        ix_ready, vl, stored = k.sem("m_ix_ready"), k.sem("m_vl"), [k.sem(f"m_stored{b}") for b in two]
        min_ready, ex_ready, fq_ready, qp_ready = (k.sem(f"m_{n}_ready") for n in ("min", "ex", "fq", "qp"))
        fqT_ready, lp_ready, hs_ready, hp_ready = (k.sem(f"m_{n}_ready") for n in ("fqT", "lp", "hs", "hp"))
        hT_ready, ap_ready, f_ready, th_ready = (k.sem(f"m_{n}_ready") for n in ("hT", "ap", "f", "th"))
        res_ready = k.sem("m_res_ready")
        waited = k.sem("m_waited")

        def heads(a, j):
            return a[:, :, bass.ds(j, 1), :].rearrange("p h a d -> p h (a d)")

        def steps(eng, step):
            def single(j):
                step(j, j % RING, lambda lag: 0 <= j - lag < NJ)

            for j in ring:
                single(j)
            with eng.Fori(1, NJ // RING - 1) as i:
                for r in ring:
                    step(RING * i + r, r, lambda lag: True)
            for j in range(NJ - RING, NJ + 2):
                single(j)

        def by_head(a):
            return a[:].rearrange("p (h d) -> p h d", h=NH)

        with nc.Block() as block:

            @block.sync
            def _(sp):
                sp.dma_start(wo[:], w_o.rearrange("(k p) n -> p k n", p=P)).then_inc(wo_in, 16)

                def store(j, b):
                    sp.dma_start(token_rows(out[0], j), res[b][:]).then_inc(stored[b], 16)

                def load(j, r, first):
                    if not first:
                        sp.wait_ge(res_ready, j - RING + 1)
                        store(j - RING, r % 2)
                    for dst, src in ((zr, z_dram), (xr, xn1_dram), (x1, x1_dram)):
                        sp.dma_start(dst[r][:], token_rows(src, j)).then_inc(rows_in[r], 16)
                    sp.dma_start(cT[r][:], conv_dram[:, :, bass.ds(j, 1), :].rearrange("c m a p -> c m (a p)")
                                 ).then_inc(cT_in[r], 16)
                for j in ring:
                    load(j, j, True)
                with sp.Fori(1, NJ // RING) as i:
                    for r in ring:
                        load(RING * i + r, r, False)
                for j in range(NJ - RING, NJ):
                    sp.wait_ge(res_ready, j + 1)
                    store(j, j % 2)
                for b in two:
                    sp.wait_ge(stored[b], 8 * NJ)

            @block.gpsimd
            def _(pool):
                def step(j, b, first):
                    if not first:
                        pool.wait_ge(got[b], 4 * TOPK * (j - b))
                        pool.sem_inc(waited, 1)
                        pool.wait_ge(f_ready, j - RING + 1)
                        pool.sem_inc(waited, 1)
                    pool.tensor_copy(ix[b][:], GIDX[:, bass.ds(j, 1), :].rearrange("p a n -> p (a n)")
                                     ).then_inc(ix_ready, 1)
                    pool.wait_ge(ix_ready, j + 1)
                    pool.sem_inc(waited, 1)
                    for n in range(TOPK):
                        pool.indirect_dma_start(gt[b][:, n, :], None, o_dram,
                                                bass.IndirectOffsetOnAxis(ix[b][:, n:n + 1], 0)).then_inc(got[b], 16)
                for j in ring:
                    step(j, j, True)
                with pool.Fori(1, NJ // RING) as i:
                    for r in ring:
                        step(RING * i + r, r, False)

            @block.tensor
            def _(pe):
                pe.wait_ge(wo_in, 16)

                def product(j, r, part, first):
                    b = r % 2
                    for d in range(KD):
                        last = pe.matmul(ap[b][:], part[:, d, :], wo[:, d, :], start=(first and d == 0),
                                         stop=(not first and d == KD - 1))
                    return last

                def step(j, r, has):
                    b, r1 = r % 2, (r - 1) % RING
                    if has(0):
                        pe.wait_ge(fq_ready, j + 1)
                        for d in range(KD):
                            last = pe.transpose(qp[b][:, d, :], fq[b][:, d * P:(d + 1) * P], ident[:])
                        last.then_inc(qp_ready, 1)
                    if has(1):
                        pe.wait_ge(cT_in[r1], 4 * (j - 1 - r1) + 16)
                        if has(3):
                            pe.wait_ge(res_ready, j - 2)
                        product(j - 1, r1, cT[r1], True)
                    if has(0):
                        pe.wait_ge(fqT_ready, j + 1)
                        for m in range(KD):
                            last = pe.matmul(lp[b][:, m, :], fqT[b][:, m, :], KVB[:, m, :], start=True, stop=True)
                        last.then_inc(lp_ready, 1)
                    if has(1):
                        pe.wait_ge(hs_ready, j)
                        for d in range(KD):
                            last = pe.transpose(hp[1 - b][:, d, :], hs[1 - b][:, d * P:(d + 1) * P], ident[:])
                        last.then_inc(hp_ready, 1)
                        pe.wait_ge(hT_ready, j)
                        product(j - 1, r1, hT[1 - b], False).then_inc(ap_ready, 1)

                steps(pe, step)

            @block.scalar
            def _(act):
                act.preload_act_table(ACT.Exp)

                def exp(j, b):
                    act.wait_ge(min_ready, j + 1)
                    act.activation(ex[b][:], ex[b][:], ACT.Exp).then_inc(ex_ready, 1)

                def step(j, r, has):
                    b = r % 2
                    if has(0):
                        act.wait_ge(qp_ready, j + 1)
                        act.copy(fqT[b][:], qp[b][:]).then_inc(fqT_ready, 1)
                    if has(1):
                        act.wait_ge(f_ready, j)
                        act.activation(th[1 - b][:], zr[(r - 1) % RING][:], ACT.Tanh, scale=0.5).then_inc(th_ready, 1)
                        act.wait_ge(hp_ready, j)
                        act.copy(hT[1 - b][:], hp[1 - b][:]).then_inc(hT_ready, 1)
                    if has(-1):
                        exp(j + 1, 1 - b)
                exp(0, 0)
                steps(act, step)

            @block.vector
            def _(ve):
                PER_STEP = (TOPK - 1) + 4 + 3
                place = [0, 0]

                def link(ins):
                    place[1] += 1
                    ins.then_inc(vl, 1)
                    return place[1]

                def need(n):
                    ve.wait_ge(vl, place[0] + n)

                def low(j, b):
                    ve.tensor_scalar(by_head(ex[b]), heads(Q, j), 0.0, None, ALU.min).then_inc(min_ready, 1)

                def step(j, r, has):
                    b, c, r1, r2 = r % 2, 1 - r % 2, (r - 1) % RING, (r - 2) % RING
                    if type(j) is int and j < RING:
                        place[0] += place[1]
                    else:
                        place[0] = whole_steps(j)
                    place[1] = 0
                    z, l, h = zr[r1], lp[c], hs[c]
                    h4 = h[:].rearrange("p (m h d) -> p m h d", m=KD, h=4)

                    def expert(n):
                        wn = WK[:, bass.ds(j - 1, 1), n]
                        return ve.scalar_tensor_tensor(z[:], gt[r1][:, n, :], wn, z[:], ALU.mult, ALU.add)

                    def over_normaliser(m):
                        return link(ve.tensor_tensor(h4[:, m, :, :],
                                                     l[:, m, 0:P].rearrange("p (h d) -> p h d", h=4),
                                                     rz[c][:, m, :].unsqueeze(2).to_broadcast([P, 4, DH]), ALU.mult))

                    if has(0):
                        ve.wait_ge(ex_ready, j + 1)
                        ve.scalar_tensor_tensor(by_head(fq[b]), heads(Q, j), 0.0, by_head(ex[b]), ALU.max, ALU.add
                                                ).then_inc(fq_ready, 1)
                    if has(1):
                        ve.wait_ge(lp_ready, j)
                        bias = link(ve.tensor_scalar(rz[c][:], l[:, :, P:LW], 1e-6, None, ALU.add))
                        ve.wait_ge(rows_in[r1], 12 * (j - 1 - r1) + 48)
                        ve.wait_ge(got[r1], 4 * TOPK * (j - 1 - r1) + 16 * TOPK)
                        z0 = link(expert(0))
                        need(bias)
                        recip = link(ve.reciprocal(rz[c][:], rz[c][:]))
                        need(z0)
                        z1 = link(expert(1))
                        need(recip)
                        over_normaliser(0)
                        m1 = over_normaliser(1)
                        need(z1)
                        z2 = link(expert(2))
                        need(m1)
                        ve.tensor_tensor(by_head(h), heads(K, j - 1), by_head(h), ALU.add).then_inc(hs_ready, 1)
                        need(z2)
                        expert(TOPK - 1).then_inc(f_ready, 1)
                    if has(2):
                        ve.wait_ge(th_ready, j - 1)
                        gate = link(ve.scalar_tensor_tensor(th[b][:], th[b][:], 1.0, zr[r2][:], ALU.add, ALU.mult))
                        ve.wait_ge(ap_ready, j - 1)
                        total = link(ve.tensor_tensor(s1[b][:], ap[b][:], xr[r2][:], ALU.add))
                    if has(-1):
                        low(j + 1, c)
                    if has(2):
                        need(total)
                        part = link(ve.scalar_tensor_tensor(th[b][:], th[b][:], 0.5, s1[b][:], ALU.mult, ALU.mult))
                        if has(4):
                            ve.wait_ge(stored[b], 8 * (j - 2 - b))
                        need(part)
                        ve.tensor_tensor(res[b][:], th[b][:], x1[r2][:], ALU.add).then_inc(res_ready, 1)

                def whole_steps(j):
                    return PER_STEP * j - PER_STEP - 3
                low(0, 0)
                steps(ve, step)


def gated_s4d_then_ripple_moe(nc, x, log_a_re, a_im, c_re, c_im, log_dt, d_skip, ln_w, ln_b, ffn_w, disha,
                              w_qkv, w_o, conv_w, w_gate, w1, w2, w3, ws1, ws2, ws3, out):
    v_dram = nc.dram_tensor("v_powers", (NG, P, 4 * GH * P), BF16, kind="Internal").ap()
    kp_dram = nc.dram_tensor("padded_taps", (D, 2 * P), F32, kind="Internal").ap()
    x1_dram = nc.dram_tensor("x1", (T, D), F32, kind="Internal").ap()
    xn1_dram = nc.dram_tensor("xn1", (T, D), F32, kind="Internal").ap()
    z_dram = nc.dram_tensor("shared_out", (T, D), F32, kind="Internal").ap()
    vt_dram = nc.dram_tensor("v_channels_first", (P, D // P, NJ, P), F32, kind="Internal").ap()
    conv_dram = nc.dram_tensor("convolved", (P, D // P, NJ, P), F32, kind="Internal").ap()
    xs_dram = nc.dram_tensor("slots_in", (SLOTS, D), F32, kind="Internal").ap()
    o_dram = nc.dram_tensor("slots_out", (SLOTS, D), F32, kind="Internal").ap()
    Core.used = []
    with Core(nc) as k:
        ident = k.sb("ident", [P, P])
        with Core(nc) as l0:
            anti = l0.sb("anti", [P, P])
            XN, G0 = l0.sb("XN", [P, NC, D]), l0.sb("G0", [P, NC, D])
            stage_norm_gate0(nc, x, ffn_w, disha, ident, anti, XN, G0, xs_dram)
            with Core(nc) as s4d:
                S = s4d.sb("S", [P, NC, 2, P])
                with Core(nc) as c:
                    turns, KT = c.sb("turns", [P, P]), c.sb("KT", [P, 2, P])
                    WR, WQ = c.sb("WR", [P, 2, P]), c.sb("WQ", [P, 2, P])
                    with Core(nc) as m:
                        DP = m.sb("DP", [P, 7, P])
                        CMH, CML = (m.sb(n, [P, P, 2, 2], BF16) for n in ("CMH", "CML"))
                        MR, MRN, MI = m.sb("MR", [P, P]), m.sb("MRN", [P, P]), m.sb("MI", [P, P])
                        stage_s4d_constants(nc, log_a_re, a_im, c_re, c_im, log_dt, ident, turns, DP, CMH, CML, MR, MRN,
                                            MI, WR, WQ)
                        stage_s4d_states(nc, turns, DP, CMH, CML, MR, MRN, MI, ident, anti, XN, KT, S, v_dram)
                    stage_s4d_scan(nc, WR, WQ, S, KT, ident, kp_dram)
                with Core(nc) as o:
                    Y = o.sb("Y", [P, NC, D])
                    stage_s4d_outputs(nc, S, XN, anti, v_dram, kp_dram, Y)
                    stage_mix0(nc, x, d_skip, ln_w, ln_b, XN, G0, Y, x1_dram, xn1_dram)
        k.recycle()
        with Core(nc) as l1:
            WK = l1.sb("WK", [P, NJ, TOPK])
            SIDX, GIDX = l1.sb("SIDX", [P, NJ, TOPK], U32), l1.sb("GIDX", [P, NJ, TOPK], U32)
            EXP = l1.sb("EXP", [P, NGR], I32)
            KVB = l1.sb("KVB", [P, 2, P + 4])
            Q, K, V = (l1.sb(n, [P, NH, NJ, DH]) for n in "QKV")
            with Core(nc) as g:
                L = g.sb("L", [P, NJ, NE])
                stage_projections(nc, w_qkv, w_gate, ws1, ws2, ws3, xn1_dram, z_dram, vt_dram, ident, Q, K, V, L, KVB)
                stage_routing(nc, L, WK, SIDX, GIDX, EXP)
            stage_scatter_and_convolution(nc, conv_w, vt_dram, conv_dram, xn1_dram, xs_dram, ident, SIDX)
            stage_experts_and_attention(nc, w1, w2, w3, xs_dram, o_dram, ident, EXP, Q, K, V)
            stage_mix1(nc, w_o, xn1_dram, x1_dram, z_dram, o_dram, conv_dram, ident, Q, K, KVB, WK, GIDX,
                       out)


_INS = ['L0_attn_x', 'L0_attn_log_A_real', 'L0_attn_A_imag', 'L0_attn_C_re', 'L0_attn_C_im', 'L0_attn_log_dt',
        'L0_attn_D', 'L0_attn_ln_w', 'L0_attn_ln_b', 'L0_ffn_weight', 'L0_ffn_disha', 'L1_attn_Wqkv', 'L1_attn_Wo',
        'L1_attn_conv_w', 'L1_ffn_Wg', 'L1_ffn_W1', 'L1_ffn_W2', 'L1_ffn_W3', 'L1_ffn_Ws1', 'L1_ffn_Ws2',
        'L1_ffn_Ws3']
_OUTS = [((1, 4096, 256), 'float32')]


def kernel(**inputs):
    import numpy as _np
    import concourse.bacc as _bacc
    from concourse import mybir as _mybir
    from concourse.bass_utils import run_bass_kernel_spmd as _run

    nc = _bacc.Bacc("TRN2", target_bir_lowering=False, num_devices=1)
    arrays, args = {}, []
    for name in _INS:
        a = _np.ascontiguousarray(inputs[name])
        arrays[f"in_{name}_dram"] = a
        args.append(nc.dram_tensor(f"in_{name}_dram", a.shape, _mybir.dt.from_np(a.dtype), kind="ExternalInput").ap())
    for i, (shape, dtype) in enumerate(_OUTS):
        dt = _mybir.dt.from_np(_np.dtype(dtype))
        args.append(nc.dram_tensor(f"out_{i}_dram", shape, dt, kind="ExternalOutput").ap())
    gated_s4d_then_ripple_moe(nc, *args)
    r = _run(nc, [arrays], core_ids=[0])
    return r.results[0]["out_0_dram"]
```

```python
from contextlib import ExitStack

import concourse.bass as bass
from concourse import mybir

F32 = mybir.dt.float32
BF16 = mybir.dt.bfloat16
I32 = mybir.dt.int32
U32 = mybir.dt.uint32
ALU = mybir.AluOpType
ACT = mybir.ActivationFunctionType
AX_X = mybir.AxisListType.X

P = 128
T, D = 4096, 256
NC = T // P
NST = 64
GH = 8
NG = P // GH
EPS = 1e-5
PI = 3.14159265358979
TWO_PI = 6.2831850
MAGIC = 12582912.0


class Chain:

    def __init__(self, eng, sem):
        self.eng, self.sem, self.n = eng, sem, 0

    def __call__(self, ins):
        self.n += 1
        ins.then_inc(self.sem, 1)
        self.eng.wait_ge(self.sem, self.n)


class Core:
    used = []

    def __init__(self, nc):
        self.nc, self.stack = nc, ExitStack()

    def __enter__(self):
        return self

    def __exit__(self, *a):
        self.stack.close()

    def sb(self, name, shape, dt=F32):
        return self.stack.enter_context(self.nc.sbuf_tensor(name, shape, dt))

    def ps(self, name, shape, dt=F32):
        return self.stack.enter_context(self.nc.psum_tensor(name, shape, dt))

    def sem(self, name):
        Core.used.append(self.nc.alloc_semaphore(name=name))
        return Core.used[-1]

    def recycle(self):
        self.nc.clear_and_free_semaphores(Core.used)
        self.nc.all_engine_barrier()
        Core.used = []


def moments_to_scale(ve, link, stats, mean, rstd, tmp):
    me, mo = stats[:, :, 1], stats[:, :, 4]
    link(ve.tensor_tensor(mean, me, mo, ALU.add))
    link(ve.tensor_tensor(tmp, me, mo, ALU.subtract))
    link(ve.tensor_scalar(mean, mean, 0.5, None, ALU.mult))
    link(ve.tensor_tensor(tmp, tmp, tmp, ALU.mult))
    link(ve.tensor_tensor(rstd, stats[:, :, 2], stats[:, :, 5], ALU.add))
    link(ve.tensor_scalar(rstd, rstd, 1.0 / D, EPS, ALU.mult, ALU.add))
    link(ve.scalar_tensor_tensor(rstd, tmp, 0.25, rstd, ALU.mult, ALU.add))


def make_identity(pool, link, tile, base=0, step=-1):
    link(pool.memset(tile, 0.0))
    link(pool.affine_select(out=tile, in_=tile, compare_op=ALU.not_equal, fill=1.0, base=base,
                            pattern=[[step, P]], channel_multiplier=1))


def clear_slots(sp, xs_dram, zero, cleared, first, last):
    ROWS = 1024
    for i in range(first, last):
        sp.dma_start(xs_dram[i * ROWS:(i + 1) * ROWS, :].rearrange("(p r) d -> p r d", p=P),
                     zero[:].unsqueeze(1).to_broadcast([P, ROWS // P, D])).then_inc(cleared, 16)


def stage_norm_gate0(nc, x, weight, disha, ident, anti, XN, G0, zero, xs_dram):
    KD = D // P
    with Core(nc) as k:
        X = k.sb("a_x", [P, NC, D])
        wraw = k.sb("a_wraw", [P, KD, D])
        drep = k.sb("a_drep", [P, D])
        weff = k.sb("a_weff", [P, KD, D])
        stats = k.sb("a_stats", [P, NC, 6])
        zeroed, cleared = k.sem("a_zeroed"), k.sem("a_cleared")
        mean = k.sb("a_mean", [P, NC])
        rstd = k.sb("a_rstd", [P, NC])
        tmp = k.sb("a_tmp", [P, NC])
        xf = [k.sb(f"a_xf{b}", [P, D]) for b in range(2)]
        xT = [k.sb(f"a_xT{b}", [P, KD, P]) for b in range(2)]
        tp = [k.ps(f"a_tp{b}", [P, KD, P]) for b in range(2)]
        gp = [k.ps(f"a_gp{b}", [P, D]) for b in range(2)]
        wt = k.ps("a_wt", [P, KD, D])
        x_in = [k.sem(f"a_x_in{i}") for i in range(4)]
        w_in = k.sem("a_w_in")
        pool_link, dve_link = k.sem("a_pool"), k.sem("a_dve")
        ident_ready = k.sem("a_ident_ready")
        wt_ready, weff_ready = k.sem("a_wt_ready"), k.sem("a_weff_ready")
        var_ready, std_ready = k.sem("a_var_ready"), k.sem("a_std_ready")
        xf_ready = k.sem("a_xf_ready")
        tp_ready, xT_ready = k.sem("a_tp_ready"), k.sem("a_xT_ready")
        gp_ready, g_ready = k.sem("a_gp_ready"), k.sem("a_g_ready")
        with nc.Block() as block:

            @block.sync
            def _(sp):
                for i in range(4):
                    c0 = i * NC // 4
                    sp.dma_start(X[:, c0:c0 + NC // 4, :],
                                 x[0, c0 * P:(c0 + NC // 4) * P, :].rearrange("(c s) d -> s c d", s=P)
                                 ).then_inc(x_in[i], 16)
                sp.wait_ge(zeroed, 1)
                clear_slots(sp, xs_dram, zero, cleared, 0, 9)
                sp.wait_ge(cleared, 16 * 9)

            @block.gpsimd
            def _(pool):
                link = Chain(pool, pool_link)
                pool.memset(zero[:], 0.0).then_inc(zeroed, 1)
                make_identity(pool, link, ident[:])
                make_identity(pool, link, anti[:], base=-(P - 1), step=1)
                pool.sem_inc(ident_ready, 1)

            @block.vector
            def _(ve):
                link = Chain(ve, dve_link)
                for i in range(4):
                    ve.wait_ge(x_in[i], 16)
                    for c in range(i * NC // 4, (i + 1) * NC // 4):
                        ve.bn_stats(stats[:, c, :], X[:, c, :])
                ve.drain()
                moments_to_scale(ve, link, stats, mean[:], rstd[:], tmp[:])
                ve.sem_inc(var_ready, 1)
                ve.wait_ge(std_ready, 1)
                link(ve.reciprocal(rstd[:], rstd[:]))
                ve.wait_ge(w_in, 48)
                ve.wait_ge(wt_ready, 1)
                for j in range(KD):
                    ve.tensor_tensor(weff[:, j, :], wt[:, j, :], drep[:], ALU.add).then_inc(weff_ready, 1)
                for b in range(2):
                    ve.tensor_scalar(xf[b][:], X[:, b, :], mean[:, b:b + 1], rstd[:, b:b + 1],
                                     ALU.subtract, ALU.mult).then_inc(xf_ready, 1)
                    ve.tensor_scalar(XN[:, b, :], X[:, b, :], mean[:, b:b + 1], rstd[:, b:b + 1],
                                     ALU.subtract, ALU.mult)
                with ve.Fori(1, NC // 2) as i:
                    for b in range(2):
                        c = 2 * i + b
                        ve.wait_ge(tp_ready, 2 * i + b - 1)
                        ve.tensor_scalar(xf[b][:], X[:, c, :], mean[:, bass.ds(c, 1)], rstd[:, bass.ds(c, 1)],
                                         ALU.subtract, ALU.mult).then_inc(xf_ready, 1)
                        ve.tensor_scalar(XN[:, c, :], X[:, c, :], mean[:, bass.ds(c, 1)], rstd[:, bass.ds(c, 1)],
                                         ALU.subtract, ALU.mult)

            @block.scalar
            def _(act):
                act.dma_start(wraw[:], weight.rearrange("(j o) d -> o j d", o=P)).then_inc(w_in, 16)
                for j in range(2):
                    act.dma_start(drep[64 * j:64 * j + 64, :], disha).then_inc(w_in, 16)
                act.wait_ge(var_ready, 1)
                act.activation(rstd[:], rstd[:], ACT.Sqrt).then_inc(std_ready, 1)
                act.preload_act_table(ACT.Silu)

                def move(c, b):
                    act.wait_ge(tp_ready, c + 1)
                    act.copy(xT[b][:], tp[b][:]).then_inc(xT_ready, 1)

                def gate(c, b):
                    act.wait_ge(gp_ready, c + 1)
                    act.activation(G0[:, c, :], gp[b][:], ACT.Silu).then_inc(g_ready, 1)

                for b in range(2):
                    move(b, b)
                with act.Fori(0, NC // 2 - 1) as i:
                    for b in range(2):
                        move(2 * i + b + 2, b)
                        gate(2 * i + b, b)
                for b in range(2):
                    gate(NC - 2 + b, b)

            @block.tensor
            def _(pe):
                pe.wait_ge(ident_ready, 1)
                pe.wait_ge(w_in, 48)
                for j in range(KD):
                    for d in range(KD):
                        last = pe.transpose(wt[:, d, j * P:(j + 1) * P], wraw[:, j, d * P:(d + 1) * P], ident[:])
                last.then_inc(wt_ready, 1)
                pe.wait_ge(weff_ready, KD)

                def transposes(c, b):
                    pe.wait_ge(xf_ready, c + 1)
                    for d in range(KD):
                        last = pe.transpose(tp[b][:, d, :], xf[b][:, d * P:(d + 1) * P], ident[:])
                    last.then_inc(tp_ready, 1)

                def products(c, b, first):
                    pe.wait_ge(xT_ready, c + 1)
                    if not first:
                        pe.wait_ge(g_ready, c - 1)
                    for d in range(KD):
                        last = pe.matmul(gp[b][:], xT[b][:, d, :], weff[:, d, :],
                                         start=(d == 0), stop=(d == KD - 1))
                    last.then_inc(gp_ready, 1)

                transposes(0, 0)
                transposes(1, 1)
                for b in range(2):
                    products(b, b, True)
                    transposes(2 + b, b)
                with pe.Fori(1, NC // 2 - 1) as i:
                    for b in range(2):
                        products(2 * i + b, b, False)
                        transposes(2 * i + b + 2, b)
                for b in range(2):
                    products(NC - 2 + b, b, False)




def frac_turns(ve, link, out, turns, tmp):
    link(ve.tensor_scalar(tmp, turns, MAGIC, MAGIC, ALU.add, ALU.subtract))
    link(ve.tensor_tensor(out, turns, tmp, ALU.subtract))


def stage_s4d_constants(nc, log_a_re, a_im, c_re, c_im, log_dt, ident, turns, DP, CMH, CML, MR, MRN, MI, WR, WQ,
                        zero, xs_dram):
    with Core(nc) as k:
        raw = [k.sb(f"b_raw{i}", [P, 2, NST]) for i in range(4)]
        names = ["e1", "ai", "cr", "ci", "dt", "th", "em", "den", "f", "t1", "t2", "t3", "sh", "ch", "re", "im",
                 "xr", "xi", "ctr", "cti", "mag", "decay", "hpi"]
        v = {n: k.sb(f"b_{n}", [P, P])[:] for n in names}
        CM = k.sb("b_cm", [P, P, 2, 2])
        tp = k.ps("b_tp", [P, 4, P])
        raw_in, dt_in = k.sem("b_raw_in"), k.sem("b_dt_in")
        tp_ready, ve_link, act_link = k.sem("b_tp_ready"), k.sem("b_dve"), k.sem("b_act")
        cleared = k.sem("b_cleared")
        asked, act_done = k.sem("b_asked"), k.sem("b_act_done")
        with nc.Block() as block:

            @block.sync
            def _(sp):
                for i, a in enumerate((log_a_re, a_im, c_re, c_im)):
                    sp.dma_start(raw[i][:], a.rearrange("(g p) n -> p g n", g=2)).then_inc(raw_in, 16)
                for g in range(2):
                    sp.dma_start(v["dt"][g * NST:(g + 1) * NST, :],
                                 log_dt[g * P:(g + 1) * P].partition_broadcast(NST)).then_inc(dt_in, 16)
                clear_slots(sp, xs_dram, zero, cleared, 9, 18)
                sp.wait_ge(cleared, 16 * 9)

            @block.tensor
            def _(pe):
                pe.wait_ge(raw_in, 64)
                for i in range(4):
                    last = pe.transpose(tp[:, i, :], raw[i][:].rearrange("p g n -> p (g n)"), ident[:])
                last.then_inc(tp_ready, 1)

            @block.scalar
            def _(act):
                act.wait_ge(tp_ready, 1)
                act.wait_ge(dt_in, 32)
                act.activation(v["e1"], tp[:, 0, :], ACT.Exp).then_inc(act_done, 1)
                act.activation(v["dt"], v["dt"], ACT.Exp).then_inc(act_done, 1)
                act.wait_ge(asked, 1)
                act.activation(v["em"], v["decay"], ACT.Tanh, scale=0.5).then_inc(act_done, 1)
                act.wait_ge(asked, 2)
                act.activation(v["sh"], v["f"], ACT.Sin, scale=TWO_PI).then_inc(act_done, 1)
                act.activation(v["t3"], v["f"], ACT.Abs).then_inc(act_link, 1)
                act.wait_ge(act_link, 1)
                act.activation(v["ch"], v["t3"], ACT.Sin, scale=-TWO_PI, bias=v["hpi"][:, 0:1]).then_inc(act_done, 1)
                act.wait_ge(asked, 3)
                act.activation(v["xi"], v["f"], ACT.Sin, scale=TWO_PI).then_inc(act_done, 1)
                act.activation(v["t3"], v["f"], ACT.Abs).then_inc(act_link, 1)
                act.wait_ge(act_link, 2)
                act.activation(v["xr"], v["t3"], ACT.Sin, scale=-TWO_PI, bias=v["hpi"][:, 0:1]).then_inc(act_done, 1)

            @block.vector
            def _(ve):
                link = Chain(ve, ve_link)
                mul, add, sub = ALU.mult, ALU.add, ALU.subtract

                def tt(o, a, b, op):
                    link(ve.tensor_tensor(o, a, b, op))

                def ts(o, a, s1, s2, op0, op1=ALU.bypass):
                    link(ve.tensor_scalar(o, a, s1, s2, op0, op1))

                link(ve.memset(v["hpi"], PI / 2))
                ve.wait_ge(act_done, 2)
                link(ve.tensor_copy(v["ai"], tp[:, 1, :]))
                link(ve.tensor_copy(v["cr"], tp[:, 2, :]))
                link(ve.tensor_copy(v["ci"], tp[:, 3, :]))
                link(ve.scalar_tensor_tensor(v["decay"], v["e1"], -1.0, v["dt"], mul, mul))
                tt(v["th"], v["ai"], v["dt"], mul)
                ts(turns[:], v["th"], 0.15915494309189535, None, mul)
                ve.sem_inc(asked, 1)
                ts(v["t1"], turns[:], 0.5, None, mul)
                frac_turns(ve, link, v["f"], v["t1"], v["t2"])
                ve.sem_inc(asked, 1)
                ve.wait_ge(act_done, 3)
                ts(v["t1"], v["em"], -1.0, 1.0, mul, add)
                link(ve.reciprocal(v["t1"], v["t1"]))
                link(ve.scalar_tensor_tensor(v["em"], v["em"], 2.0, v["t1"], mul, mul))
                tt(v["t1"], v["e1"], v["e1"], mul)
                tt(v["t2"], v["ai"], v["ai"], mul)
                tt(v["den"], v["t1"], v["t2"], add)
                link(ve.reciprocal(v["den"], v["den"]))
                ve.wait_ge(act_done, 5)
                ts(v["t1"], v["em"], 1.0, None, add)
                tt(v["t2"], v["sh"], v["sh"], mul)
                tt(v["t2"], v["t2"], v["t1"], mul)
                link(ve.scalar_tensor_tensor(v["re"], v["t2"], -2.0, v["em"], mul, add))
                tt(v["t2"], v["sh"], v["ch"], mul)
                link(ve.scalar_tensor_tensor(v["im"], v["t2"], 2.0, v["t1"], mul, mul))
                ts(v["t1"], turns[:], float(P), None, mul)
                frac_turns(ve, link, v["f"], v["t1"], v["t2"])
                ve.sem_inc(asked, 1)
                ve.wait_ge(act_done, 7)
                ts(DP[:, 0, :], v["em"], 1.0, None, add)
                for i in range(6):
                    tt(DP[:, i + 1, :], DP[:, i, :], DP[:, i, :], mul)
                tt(v["mag"], DP[:, 6, :], DP[:, 6, :], mul)
                for r in range(2):
                    tt(WR[:, r, :], v["mag"], v["xr"], mul)
                tt(WQ[:, 0, :], v["mag"], v["xi"], mul)
                ts(WQ[:, 1, :], WQ[:, 0, :], -1.0, None, mul)
                tt(v["t1"], v["re"], v["e1"], mul)
                tt(v["t2"], v["im"], v["ai"], mul)
                tt(v["xr"], v["t2"], v["t1"], sub)
                tt(v["t1"], v["im"], v["e1"], mul)
                tt(v["t2"], v["re"], v["ai"], mul)
                link(ve.scalar_tensor_tensor(v["xi"], v["t1"], -1.0, v["t2"], mul, sub))
                tt(v["xr"], v["xr"], v["den"], mul)
                tt(v["xi"], v["xi"], v["den"], mul)
                tt(v["t1"], v["cr"], v["xr"], mul)
                tt(v["t2"], v["ci"], v["xi"], mul)
                tt(v["t3"], v["t1"], v["t2"], sub)
                ts(v["ctr"], v["t3"], 2.0, None, mul)
                tt(v["t1"], v["cr"], v["xi"], mul)
                tt(v["t2"], v["ci"], v["xr"], mul)
                tt(v["t3"], v["t1"], v["t2"], add)
                ts(v["cti"], v["t3"], 2.0, None, mul)
                tt(v["t1"], v["ctr"], v["re"], mul)
                tt(v["t2"], v["cti"], v["im"], mul)
                tt(v["t3"], v["t1"], v["t2"], sub)
                tt(MR[:], v["t3"], v["ctr"], add)
                ts(MRN[:], MR[:], -1.0, None, mul)
                tt(v["t1"], v["ctr"], v["im"], mul)
                tt(v["t2"], v["cti"], v["re"], mul)
                tt(v["t3"], v["t1"], v["t2"], add)
                tt(MI[:], v["t3"], v["cti"], add)
                link(ve.memset(CM[:], 0.0))
                for g in range(2):
                    q = slice(g * NST, (g + 1) * NST)
                    link(ve.tensor_copy(CM[q, :, 0, g], v["ctr"][q, :]))
                    ts(CM[q, :, 1, g], v["cti"][q, :], -1.0, None, mul)
                link(ve.tensor_copy(CMH[:], CM[:]))
                tt(CML[:], CM[:], CMH[:], sub)


def stage_s4d_states(nc, turns, DP, CMH, CML, MR, MRN, MI, ident, anti, XN, KT, S, v_dram):
    KP = 7
    with Core(nc) as k:
        lag = k.sb("c_lag", [P, P])
        hpi = k.sb("c_hpi", [P, 1])
        ea = [k.sb(f"c_ea{b}", [P, GH, P]) for b in range(2)]
        fr = [k.sb(f"c_fr{b}", [P, GH, P]) for b in range(2)]
        co = [k.sb(f"c_co{b}", [P, GH, P]) for b in range(2)]
        si = [k.sb(f"c_si{b}", [P, GH, P]) for b in range(2)]
        rn = k.sb("c_rn", [P, GH, P])
        V = [k.sb(f"c_v{b}", [P, 2, GH, P]) for b in range(2)]
        VP = [k.sb(f"c_vp{b}", [P, 2, 2, GH, P], BF16) for b in range(2)]
        VT = k.sb("c_vt", [P, 4, 4, P])
        xg = k.sb("c_xg", [P, NC, 2, GH])
        t1, t2 = k.sb("c_t1", [P, GH, NC]), k.sb("c_t2", [P, GH, NC])
        xp = k.ps("c_xp", [P, NC, 2, GH])
        vtp = k.ps("c_vtp", [P, 4, 4, P])
        ktp = k.ps("c_ktp", [P, GH, 2])
        bp = [k.ps(f"c_bp{b}", [P, 2, GH, NC]) for b in range(2)]
        pool_link, ve_link, act_link = k.sem("c_pool"), k.sem("c_dve"), k.sem("c_act")
        st_link, v_half, kt_taken = k.sem("c_sums"), k.sem("c_v_half"), k.sem("c_kt_taken")
        lag_ready, ea_ready = k.sem("c_lag_ready"), k.sem("c_ea_ready")
        fr_ready, trig_ready = k.sem("c_fr_ready"), k.sem("c_trig_ready")
        v_ready, v_stored = k.sem("c_v_ready"), [k.sem(f"c_v_stored{b}") for b in range(2)]
        xp_ready, xg_ready = k.sem("c_xp_ready"), k.sem("c_xg_ready")
        vtp_ready, vt_ready = k.sem("c_vtp_ready"), k.sem("c_vt_ready")
        vh_ready, vl_ready = k.sem("c_vh_ready"), k.sem("c_vl_ready")
        kt_ready, bp_ready, s_ready = k.sem("c_kt_ready"), k.sem("c_bp_ready"), k.sem("c_s_ready")
        lags = lag[:].unsqueeze(1).to_broadcast([P, GH, P])

        def columns(a, g, n):
            return a[:, bass.ds(g * GH, GH)].unsqueeze(2).to_broadcast([P, GH, n])

        def groups(eng, step):
            step(0, 0, 0)
            step(1, 1, 1)
            with eng.Fori(1, NG // 2 - 1) as i:
                for b in range(2):
                    step(2 * i + b, b, 2)
            step(NG - 2, 0, 2)
            step(NG - 1, 1, NG - 1)

        with nc.Block() as block:

            @block.gpsimd
            def _(pool):
                link = Chain(pool, pool_link)
                link(pool.iota(lag[:], pattern=[[1, P]], base=0, channel_multiplier=0,
                               allow_small_or_imprecise_dtypes=True))
                link(pool.memset(hpi[:], PI / 2))
                pool.sem_inc(lag_ready, 1)
                for b in range(2):
                    link(pool.memset(ea[b][:, :, 0:1], 1.0))

                def magnitudes(g, b, wait):
                    if wait:
                        pool.wait_ge(v_ready, g - 1)
                    for m in range(KP):
                        n = 1 << m
                        ins = pool.tensor_tensor(ea[b][:, :, n:2 * n], ea[b][:, :, 0:n],
                                                 columns(DP[:, m, :], g, n), ALU.mult)
                        if m < KP - 1:
                            ins.then_inc(pool_link, 1)
                            pool.wait_ge(pool_link, link.n + (KP - 1) * g + m + 1)
                        else:
                            ins.then_inc(ea_ready, 1)

                def step(g, b, at):
                    if at != NG - 1:
                        magnitudes(g + 1, 1 - b, at >= 1)
                    if at >= 2:
                        pool.wait_ge(v_stored[b], 8 * (g - b) if at == 2 else 8 * (NG - 2))
                        pool.wait_ge(kt_ready, g - 1)
                    pool.wait_ge(vh_ready, g + 1)
                    pool.tensor_tensor(VP[b][:, 1], V[b][:], VP[b][:, 0], ALU.subtract).then_inc(vl_ready, 1)
                magnitudes(0, 0, False)
                groups(pool, step)

            @block.vector
            def _(ve):
                ve.wait_ge(lag_ready, 1)

                def phase(g, b):
                    ve.tensor_tensor(fr[b][:], columns(turns, g, P), lags, ALU.mult).then_inc(ve_link, 1)
                    ve.wait_ge(ve_link, 2 * g + 1)
                    ve.tensor_scalar(rn[:], fr[b][:], MAGIC, MAGIC, ALU.add, ALU.subtract).then_inc(ve_link, 1)
                    ve.wait_ge(ve_link, 2 * g + 2)
                    ve.tensor_tensor(fr[b][:], fr[b][:], rn[:], ALU.subtract).then_inc(fr_ready, 1)

                def add_to_states(g, b):
                    ve.wait_ge(bp_ready, g + 1)
                    br, bi = bp[b][:, 0, :, :], bp[b][:, 1, :, :]
                    for r, (m1, m2) in enumerate(((MR, MI), (MI, MRN))):
                        ve.tensor_tensor(t1[:], br, columns(m1, g, NC), ALU.mult).then_inc(st_link, 1)
                        ve.tensor_tensor(t2[:], bi, columns(m2, g, NC), ALU.mult).then_inc(st_link, 1)
                        ve.wait_ge(st_link, 6 * g + 3 * r + 2)
                        o = S[:, :, r, bass.ds(g * GH, GH)].rearrange("p c h -> p h c")
                        if r == 0:
                            ins = ve.tensor_tensor(o, t1[:], t2[:], ALU.subtract)
                        else:
                            ins = ve.tensor_tensor(o, t2[:], t1[:], ALU.subtract)
                        ins.then_inc(st_link, 1)
                        ve.wait_ge(st_link, 6 * g + 3 * r + 3)
                    ve.sem_inc(s_ready, 1)

                def step(g, b, at):
                    if at != NG - 1:
                        phase(g + 1, 1 - b)
                    ve.wait_ge(ea_ready, g + 1)
                    ve.wait_ge(trig_ready, g + 1)
                    if at >= 2:
                        ve.wait_ge(vl_ready, g - 1)
                    ve.tensor_tensor(V[b][:, 0, :, :], ea[b][:], co[b][:], ALU.mult).then_inc(v_half, 1)
                    ve.tensor_tensor(V[b][:, 1, :, :], ea[b][:], si[b][:], ALU.mult).then_inc(v_ready, 1)
                    if at >= 1:
                        add_to_states(g - 1, 1 - b)
                phase(0, 0)
                groups(ve, step)
                add_to_states(NG - 1, 1)

            @block.scalar
            def _(act):
                act.preload_act_table(ACT.Sin)
                act.wait_ge(lag_ready, 1)

                def trig(g, b, wait):
                    act.wait_ge(fr_ready, g + 1)
                    if wait:
                        act.wait_ge(v_ready, g - 1)
                    act.activation(si[b][:], fr[b][:], ACT.Sin, scale=TWO_PI).then_inc(act_link, 1)
                    act.wait_ge(act_link, 2 * g + 1)
                    act.activation(fr[b][:], fr[b][:], ACT.Abs).then_inc(act_link, 1)
                    act.wait_ge(act_link, 2 * g + 2)
                    act.activation(co[b][:], fr[b][:], ACT.Sin, scale=-TWO_PI, bias=hpi[:]).then_inc(trig_ready, 1)

                def take_taps(g):
                    act.wait_ge(kt_ready, g + 1)
                    act.copy(KT[:, :, bass.ds(g * GH, GH)], ktp[:].rearrange("p h g -> p g h")
                             ).then_inc(kt_taken, 1)

                def step(g, b, at):
                    act.wait_ge(v_ready, g + 1)
                    if at >= 2:
                        act.wait_ge(v_stored[b], 8 * (g - b) if at == 2 else 8 * (NG - 2))
                    act.copy(VP[b][:, 0], V[b][:]).then_inc(vh_ready, 1)
                    if at != NG - 1:
                        trig(g + 1, 1 - b, at >= 1)
                    if at >= 1:
                        act.wait_ge(bp_ready, g)
                    act.wait_ge(xp_ready, g + 1)
                    act.copy(xg[:], xp[:]).then_inc(xg_ready, 1)
                    act.wait_ge(vtp_ready, g + 1)
                    for q in range(4):
                        ins = act.copy(VT[:, q, :, :], vtp[:, q, :, :])
                    ins.then_inc(vt_ready, 1)
                    if at >= 1:
                        take_taps(g - 1)
                trig(0, 0, False)
                groups(act, step)
                take_taps(NG - 1)

            @block.tensor
            def _(pe):
                def taps(g, b, wait):
                    pe.wait_ge(vl_ready, g + 1)
                    if wait:
                        pe.wait_ge(kt_taken, g)
                    for h in range(GH):
                        for n, (r, part, c) in enumerate((r, part, c) for r in range(2)
                                                         for part, c in ((0, CMH), (0, CML), (1, CMH))):
                            last = pe.matmul(ktp[:, h, :], VP[b][:, part, r, h, :], c[:, g * GH + h, r, :],
                                             start=(n == 0), stop=(n == 5))
                    last.then_inc(kt_ready, 1)

                def step(g, b, at):
                    pe.matmul(xp[:], anti[:], XN4[:, :, :, bass.ds(g * GH, GH)],
                              start=True, stop=True).then_inc(xp_ready, 1)
                    pe.wait_ge(v_ready, g + 1)
                    for m in range(2 * GH):
                        last = pe.transpose(vtp[:, m // 4, m % 4, :], V[b][:, m // GH, m % GH, :], ident[:])
                    last.then_inc(vtp_ready, 1)
                    if at >= 1:
                        taps(g - 1, 1 - b, at >= 2)
                    pe.wait_ge(xg_ready, g + 1)
                    pe.wait_ge(vt_ready, g + 1)
                    if at >= 2:
                        pe.wait_ge(s_ready, g - 1)
                    for m in range(2 * GH):
                        for q in range(2):
                            half = slice(q * NST, (q + 1) * NST)
                            last = pe.matmul(bp[b][half, m // GH, m % GH, :], VT[:, m // 4, m % 4, half],
                                             xg[:, :, q, m % GH], start=True, stop=True)
                    last.then_inc(bp_ready, 1)
                XN4 = XN[:].rearrange("p c (g h) -> p c g h", g=2)
                groups(pe, step)
                taps(NG - 1, 1, True)

            @block.sync
            def _(sp):
                def store(g, b, at):
                    sp.wait_ge(vl_ready, g + 1)
                    sp.dma_start(v_dram[g], VP[b][:].rearrange("p t r h l -> p (t r h l)")).then_inc(v_stored[b], 16)
                groups(sp, store)
                for b in range(2):
                    sp.wait_ge(v_stored[b], 8 * NG)


def stage_s4d_scan(nc, WR, WQ, S, KT, ident, kp_dram, zero, xs_dram):
    with Core(nc) as k:
        a, q = k.sb("d_a", [P, 2, P]), k.sb("d_q", [P, 2, P])
        kp = k.sb("d_kp", [P, 2, 2 * P, 2], BF16)
        ktt = k.ps("d_ktt", [P, 2, P])
        link, zeroed, turned = k.sem("d_link"), k.sem("d_zeroed"), k.sem("d_turned")
        kph_ready = k.sem("d_kph_ready")
        crossed, stepped = k.sem("d_crossed"), k.sem("d_stepped")
        kp_ready, kp_stored, cleared = k.sem("d_kp_ready"), k.sem("d_kp_stored"), k.sem("d_cleared")
        with nc.Block() as block:

            @block.vector
            def _(ve):
                ve.wait_ge(kph_ready, 1)
                taps = kp[:, :, P - 1:2 * P - 1, :]
                ve.tensor_tensor(taps[:, :, :, 1], ktt[:], taps[:, :, :, 0], ALU.subtract).then_inc(kp_ready, 1)
                with ve.Fori(1, NC - 1) as c:
                    before, here = S[:, c - 1, :, :], S[:, c, :, :]
                    ve.tensor_tensor(a[:], before, WR[:], ALU.mult).then_inc(link, 1)
                    ve.tensor_tensor(q[:, 0, :], S[:, c - 1, 1, :], WQ[:, 0, :], ALU.mult).then_inc(link, 1)
                    ve.wait_ge(link, 3 * c - 2)
                    ve.tensor_tensor(a[:], a[:], here, ALU.add).then_inc(link, 1)
                    ve.wait_ge(link, 3 * c)
                    ve.wait_ge(crossed, c)
                    ve.tensor_tensor(here, a[:], q[:], ALU.add).then_inc(stepped, 1)
                    ve.wait_ge(stepped, c)

            @block.gpsimd
            def _(pool):
                pool.memset(kp[:], 0.0).then_inc(zeroed, 1)

                def cross(c, first):
                    if not first:
                        pool.wait_ge(stepped, c - 1)
                    pool.tensor_tensor(q[:, 1, :], S[:, c - 1, 0, :], WQ[:, 1, :], ALU.mult).then_inc(crossed, 1)
                cross(1, True)
                with pool.Fori(2, NC - 1) as c:
                    cross(c, False)

            @block.tensor
            def _(pe):
                for g in range(2):
                    last = pe.transpose(ktt[:, g, :], KT[:, g, :], ident[:])
                last.then_inc(turned, 1)

            @block.scalar
            def _(act):
                act.wait_ge(zeroed, 1)
                act.wait_ge(turned, 1)
                act.copy(kp[:, :, P - 1:2 * P - 1, 0], ktt[:]).then_inc(kph_ready, 1)

            @block.sync
            def _(sp):
                sp.wait_ge(kp_ready, 1)
                sp.dma_start(kp_dram.rearrange("(g h) m -> h g m", g=2),
                             kp[:].rearrange("p g m t -> p g (m t)").bitcast(F32)).then_inc(kp_stored, 16)
                clear_slots(sp, xs_dram, zero, cleared, 18, 24)
                sp.wait_ge(kp_stored, 16)
                sp.wait_ge(cleared, 16 * 6)


def stage_s4d_outputs(nc, S, XN, anti, v_dram, kp_dram, Y):
    with Core(nc) as k:
        V = [k.sb(f"e_v{b}", [P, 2, 2, GH, P], BF16) for b in range(2)]
        tz = [k.sb(f"e_tz{b}", [P, 2, GH, P]) for b in range(2)]
        sg = [k.sb(f"e_sg{b}", [P, 2, GH, 2, NC], BF16) for b in range(2)]
        xg = [k.sb(f"e_xg{b}", [P, 2, NC, 2, GH], BF16) for b in range(2)]
        xp = [k.ps(f"e_xp{b}", [P, NC, 2, GH]) for b in range(2)]
        yp = [[k.ps(f"e_yp{b}{q}", [P, GH * 2, NC]) for q in range(2)] for b in range(2)]
        loaded = [k.sem(f"e_loaded{b}") for b in range(2)]
        xp_ready, xh_ready, sh_ready = k.sem("e_xp_ready"), k.sem("e_xh_ready"), k.sem("e_sh_ready")
        xl_ready, sl_ready = k.sem("e_xl_ready"), k.sem("e_sl_ready")
        yp_ready, y_ready = k.sem("e_yp_ready"), k.sem("e_y_ready")
        PARTS = ((0, 0), (0, 1), (1, 0))

        def groups(eng, step):
            for b in range(2):
                step(b, b, True)
            with eng.Fori(1, NG // 2) as i:
                for b in range(2):
                    step(2 * i + b, b, False)

        def states_of(g):
            return S[:, :, :, bass.ds(g * GH, GH)].rearrange("p c r h -> p h r c")

        with nc.Block() as block:

            @block.sync
            def _(sp):
                def load(g, b, first):
                    if not first:
                        sp.wait_ge(yp_ready, g - 1)
                    sp.dma_start(V[b][:].rearrange("p t r h l -> p (t r h l)"), v_dram[g]).then_inc(loaded[b], 16)
                    for q in range(2):
                        rows = bass.AP(kp_dram.tensor, (q * P + g * GH) * 2 * P, [[1, P], [2 * P, GH], [1, P]])
                        sp.dma_start(tz[b][:, q, :, :], rows).then_inc(loaded[b], 16)
                groups(sp, load)

            @block.scalar
            def _(act):
                def step(g, b, first):
                    if not first:
                        act.wait_ge(yp_ready, g - 1)
                    act.wait_ge(xp_ready, g + 1)
                    act.copy(xg[b][:, 0], xp[b][:]).then_inc(xh_ready, 1)
                    act.copy(sg[b][:, 0], states_of(g)).then_inc(sh_ready, 1)
                groups(act, step)

            @block.gpsimd
            def _(pool):
                def step(g, b, first):
                    pool.wait_ge(sh_ready, g + 1)
                    pool.tensor_tensor(sg[b][:, 1], states_of(g), sg[b][:, 0], ALU.subtract).then_inc(sl_ready, 1)
                groups(pool, step)

            @block.tensor
            def _(pe):
                XN4 = XN[:].rearrange("p c (g h) -> p c g h", g=2)

                def turn(g, b):
                    pe.matmul(xp[b][:], anti[:], XN4[:, :, :, bass.ds(g * GH, GH)],
                              start=True, stop=True).then_inc(xp_ready, 1)

                def outputs(g, b, first):
                    pe.wait_ge(xl_ready, g + 1)
                    pe.wait_ge(sl_ready, g + 1)
                    pe.wait_ge(loaded[b], 24 * (g - b) + 48)
                    if not first:
                        pe.wait_ge(y_ready, g - 1)
                    for h in range(GH):
                        for q in range(2):
                            rows = slice(q * NST, (q + 1) * NST)
                            o = yp[b][q][:, h, :]
                            taps = tz[b][:, q, h, :].bitcast(BF16).rearrange("p (l t) -> p t l", t=2)
                            for n, (i, j) in enumerate(PARTS):
                                pe.matmul(o, taps[:, i, :], xg[b][:, j, :, q, h], start=(n == 0), stop=False)
                            for n, (r, i, j) in enumerate((r, i, j) for r in range(2) for i, j in PARTS):
                                last = pe.matmul(o[:, 1:NC], V[b][rows, i, r, h, :], sg[b][rows, j, h, r, 0:NC - 1],
                                                 start=False, stop=(n == 5))
                    last.then_inc(yp_ready, 1)

                turn(0, 0)
                turn(1, 1)
                for b in range(2):
                    outputs(b, b, True)
                    turn(2 + b, b)
                with pe.Fori(1, NG // 2 - 1) as i:
                    for b in range(2):
                        outputs(2 * i + b, b, False)
                        turn(2 * i + b + 2, b)
                outputs(NG - 2, 0, False)
                outputs(NG - 1, 1, False)

            @block.vector
            def _(ve):
                Y4 = Y[:].rearrange("p c (g h) -> p g h c", g=2)

                def part(g, b):
                    ve.wait_ge(xh_ready, g + 1)
                    ve.tensor_tensor(xg[b][:, 1], xp[b][:], xg[b][:, 0], ALU.subtract).then_inc(xl_ready, 1)

                def take(g, b):
                    ve.wait_ge(yp_ready, g + 1)
                    for q in range(2):
                        ins = ve.tensor_copy(Y4[:, q, bass.ds(g * GH, GH), :], yp[b][q][:, 0:GH, :])
                    ins.then_inc(y_ready, 1)

                part(0, 0)
                part(1, 1)
                with ve.Fori(0, NG // 2 - 1) as i:
                    for b in range(2):
                        take(2 * i + b, b)
                        part(2 * i + b + 2, b)
                take(NG - 2, 0)
                take(NG - 1, 1)


def stage_mix0(nc, x, d_skip, ln_w, ln_b, XN, G0, Y, x1_dram, xn1_dram):
    BC = 4
    NBK = NC // BC
    DVE_SHARE = 2
    with Core(nc) as k:
        d1, lw, lb = k.sb("f_d1", [P, D]), k.sb("f_lw", [P, D]), k.sb("f_lb", [P, D])
        xr = [k.sb(f"f_xr{b}", [P, BC, D]) for b in range(2)]
        stats = k.sb("f_stats", [P, NC, 6])
        mean, rstd, tmp = k.sb("f_mean", [P, NC]), k.sb("f_rstd", [P, NC]), k.sb("f_tmp", [P, NC])
        shift = k.sb("f_shift", [P, NC])
        rows_in = k.sem("f_rows_in")
        x_in = [k.sem(f"f_x_in{b}") for b in range(2)]
        ve_link, d1_ready = k.sem("f_dve"), k.sem("f_d1_ready")
        skip_ready, var_ready, std_ready = k.sem("f_skip_ready"), k.sem("f_var_ready"), k.sem("f_std_ready")
        scale_ready, norm_ready, lnw_ready = k.sem("f_scale_ready"), k.sem("f_norm_ready"), k.sem("f_lnw_ready")
        x1_ready, xn1_ready, stored = k.sem("f_x1_ready"), k.sem("f_xn1_ready"), k.sem("f_stored")
        out_link = k.sem("f_out_link")
        xn1_scaled, xn1_stored = k.sem("f_xn1_scaled"), k.sem("f_xn1_stored")

        def rows(a):
            return a[:].unsqueeze(1).to_broadcast([P, BC, D])

        def block_of(a, i):
            return a[:, bass.ds(i * BC, BC), :]

        def dram_block(a, i):
            return a[bass.ds(i * BC * P, BC * P), :].rearrange("(c s) d -> s c d", s=P)

        with nc.Block() as block:

            @block.sync
            def _(sp):
                for dst, src in ((d1, d_skip), (lw, ln_w), (lb, ln_b)):
                    sp.dma_start(dst[:], src.partition_broadcast(P)).then_inc(rows_in, 16)
                for b in range(2):
                    sp.dma_start(xr[b][:], dram_block(x[0], b)).then_inc(x_in[b], 16)
                with sp.Fori(1, NBK // 2) as i:
                    for b in range(2):
                        sp.wait_ge(x1_ready, 2 * i + b - 1)
                        sp.dma_start(xr[b][:], dram_block(x[0], 2 * i + b)).then_inc(x_in[b], 16)
                with sp.Fori(0, NBK) as i:
                    sp.wait_ge(xn1_ready, i + 1)
                    sp.wait_ge(xn1_scaled, i + 1)
                    sp.dma_start(dram_block(xn1_dram, i), block_of(XN, i)).then_inc(xn1_stored, 16)
                sp.wait_ge(xn1_stored, 16 * NBK)

            @block.gpsimd
            def _(pool):
                pool.wait_ge(d1_ready, 1)
                with pool.Fori(0, NBK) as i:
                    pool.tensor_tensor(block_of(XN, i), block_of(XN, i), rows(d1), ALU.mult).then_inc(skip_ready, 1)
                with pool.Fori(0, NBK) as i:
                    pool.wait_ge(norm_ready, i + 1)
                    pool.tensor_tensor(block_of(Y, i), block_of(Y, i), rows(lw), ALU.mult).then_inc(lnw_ready, 1)

            @block.scalar
            def _(act):
                act.preload_act_table(ACT.Sqrt)
                act.wait_ge(var_ready, 1)
                act.activation(rstd[:], rstd[:], ACT.Sqrt).then_inc(std_ready, 1)
                act.wait_ge(scale_ready, 1)
                with act.Fori(0, NBK) as i:
                    for j in range(BC):
                        c = i * BC + j
                        ins = act.activation(Y[:, c, :], Y[:, c, :], ACT.Identity, bias=shift[:, bass.ds(c, 1)],
                                             scale=rstd[:, bass.ds(c, 1)])
                    ins.then_inc(norm_ready, 1)
                with act.Fori(0, NBK) as i:
                    act.wait_ge(x1_ready, i + 1)
                    act.dma_start(dram_block(x1_dram, i), block_of(Y, i)).then_inc(stored, 16)
                act.wait_ge(var_ready, 2)
                act.activation(rstd[:], rstd[:], ACT.Sqrt).then_inc(std_ready, 1)
                act.wait_ge(scale_ready, 2)
                with act.Fori(0, NBK) as i:
                    for j in range(DVE_SHARE, BC):
                        c = i * BC + j
                        ins = act.activation(XN[:, c, :], Y[:, c, :], ACT.Identity, bias=shift[:, bass.ds(c, 1)],
                                             scale=rstd[:, bass.ds(c, 1)])
                    ins.then_inc(xn1_scaled, 1)
                act.wait_ge(stored, 16 * NBK)

            @block.vector
            def _(ve):
                link = Chain(ve, ve_link)
                ve.wait_ge(rows_in, 48)
                ve.tensor_scalar(d1[:], d1[:], 1.0, None, ALU.add).then_inc(d1_ready, 1)

                def statistics(src, i):
                    for j in range(BC):
                        ve.bn_stats(stats[:, i * BC + j, :], src[:, i * BC + j, :])

                def scales(n):
                    ve.drain()
                    moments_to_scale(ve, link, stats, mean[:], rstd[:], tmp[:])
                    ve.sem_inc(var_ready, 1)
                    ve.wait_ge(std_ready, n)
                    link(ve.reciprocal(rstd[:], rstd[:]))
                    link(ve.scalar_tensor_tensor(shift[:], mean[:], -1.0, rstd[:], ALU.mult, ALU.mult))

                with ve.Fori(0, NBK) as i:
                    ve.wait_ge(skip_ready, i + 1)
                    ve.tensor_tensor(block_of(Y, i), block_of(Y, i), block_of(XN, i), ALU.add).then_inc(out_link, 1)
                    ve.wait_ge(out_link, i + 1)
                    statistics(Y, i)
                scales(1)
                ve.sem_inc(scale_ready, 1)
                with ve.Fori(0, NBK // 2) as i:
                    for b in range(2):
                        n = 2 * i + b
                        y = block_of(Y, n)
                        ve.wait_ge(lnw_ready, n + 1)
                        ve.tensor_tensor(y, y, rows(lb), ALU.add).then_inc(out_link, 1)
                        ve.wait_ge(out_link, 2 * n + NBK + 1)
                        ve.tensor_tensor(y, y, block_of(G0, n), ALU.mult).then_inc(out_link, 1)
                        ve.wait_ge(out_link, 2 * n + NBK + 2)
                        ve.wait_ge(x_in[b], 16 * i + 16)
                        ve.tensor_tensor(y, y, xr[b][:], ALU.add).then_inc(x1_ready, 1)
                        ve.wait_ge(x1_ready, n + 1)
                        statistics(Y, n)
                scales(2)
                ve.sem_inc(scale_ready, 1)
                with ve.Fori(0, NBK) as i:
                    for j in range(DVE_SHARE):
                        c = i * BC + j
                        ins = ve.tensor_scalar(XN[:, c, :], Y[:, c, :], mean[:, bass.ds(c, 1)],
                                               rstd[:, bass.ds(c, 1)], ALU.subtract, ALU.mult)
                    ins.then_inc(xn1_ready, 1)

NJ = T // P
NH, DH = 8, 32
NE, TOPK = 32, 4
HM, HS = 128, 256
CAP = 4 * T * TOPK // NE
GT = 256
NGR = T * TOPK // GT + NE
SLOTS = NGR * GT
SHIFTS = [64, 32, 16, 8, 4, 2, 1]
OFFSETS = [0] + [1 << i for i in range(12)]
POOL_SCORES = [9, 10, 11, 12]
POOL_SUMS = [6, 7, 8, 9, 10, 11, 12]
RING = 4
KCONV = 7
LEAD = KCONV - 1
FAR = 1.0e30


def token_rows(a, j):
    return a.rearrange("(p j) d -> p j d", j=NJ)[:, bass.ds(j, 1), :].rearrange("p a d -> p (a d)")


def by_twos(eng, n, step):
    for b in range(2):
        step(b, b, True)
    with eng.Fori(1, n // 2) as i:
        for b in range(2):
            step(2 * i + b, b, False)


def by_rings(eng, n, step):
    for b in range(RING):
        step(b, b, True)
    with eng.Fori(1, n // RING) as i:
        for b in range(RING):
            step(RING * i + b, b, False)


def stage_projections(nc, w_qkv, w_gate, ws1, ws2, ws3, xn1_dram, z_dram, vt_dram, ident, Q, K, V, L, KVB):
    KD = D // P
    with Core(nc) as k:
        wqv, wkg = k.sb("g_wqv", [P, KD, 2 * D]), k.sb("g_wkg", [P, KD, D + NE])
        w1s, w3s, w2s = k.sb("g_w1", [P, KD, HS]), k.sb("g_w3", [P, KD, HS]), k.sb("g_w2", [P, KD, D])
        xf = [k.sb(f"g_xf{b}", [P, D]) for b in range(2)]
        xT = [k.sb(f"g_xT{b}", [P, KD, P]) for b in range(2)]
        low = [k.sb(f"g_low{b}", [P, D]) for b in range(2)]
        fk = [k.sb(f"g_fk{b}", [P, D]) for b in range(2)]
        vs = [k.sb(f"g_vs{b}", [P, D + 1]) for b in range(2)]
        th = [k.sb(f"g_th{b}", [P, KD, P]) for b in range(2)]
        gate = [k.sb(f"g_gate{b}", [P, KD, P]) for b in range(2)]
        zs = [k.sb(f"g_zs{b}", [P, D]) for b in range(2)]
        vt = [k.sb(f"g_vt{b}", [P, KD, P]) for b in range(2)]
        tp = k.ps("g_tp", [P, KD, P])
        qvp = [k.ps(f"g_qvp{b}", [P, 2 * D]) for b in range(2)]
        kgp = k.ps("g_kgp", [P, D + NE])
        hp = k.ps("g_hp", [P, 2, KD, P])
        zvp = k.ps("g_zvp", [P, 2, D])
        zp, vtp = zvp[:, 0, :], zvp[:, 1, :]
        kv = [k.ps(f"g_kv{m}", [P, 2 * D]) for m in range(KD)]
        w_in, x_in = k.sem("g_w_in"), [k.sem(f"g_x_in{b}") for b in range(2)]
        ones_ready = k.sem("g_ones_ready")
        tp_ready, xT_ready, qv_ready, kg_ready = (k.sem(f"g_{n}_ready") for n in ("tp", "xT", "qv", "kg"))
        h_ready, th_ready, gate_ready, z_ready = (k.sem(f"g_{n}_ready") for n in ("h", "th", "gate", "z"))
        low_ready, ex_ready, fk_ready, vs_ready = (k.sem(f"g_{n}_ready") for n in ("low", "ex", "fk", "vs"))
        zs_ready, z_stored = k.sem("g_zs_ready"), [k.sem(f"g_z_stored{b}") for b in range(2)]
        kv_done, half_gate, v_copied = k.sem("g_kv_done"), k.sem("g_half_gate"), k.sem("g_v_copied")
        q_taken = k.sem("g_q_taken")

        def heads(a, j):
            return a[:, :, bass.ds(j, 1), :].rearrange("p h a d -> p h (a d)")

        with nc.Block() as block:

            @block.sync
            def _(sp):
                def store(j, b):
                    sp.dma_start(token_rows(z_dram, j), zs[b][:]).then_inc(z_stored[b], 16)
                    sp.dma_start(vt_dram[:, :, bass.ds(j, 1), :].rearrange("c m a p -> c m (a p)"), vt[b][:]
                                 ).then_inc(z_stored[b], 16)

                def step(j, b, first):
                    if not first:
                        sp.wait_ge(tp_ready, j - 1)
                    sp.dma_start(xf[b][:], token_rows(xn1_dram, j)).then_inc(x_in[b], 16)
                    if not first:
                        sp.wait_ge(zs_ready, j - 1)
                        store(j - 2, b)
                for i in range(2):
                    sp.dma_start(wqv[:, :, i * D:(i + 1) * D],
                                 w_qkv[:, 2 * i * D:2 * i * D + D].rearrange("(k p) n -> p k n", p=P)
                                 ).then_inc(w_in, 16)
                by_twos(sp, NJ, step)
                for b in range(2):
                    sp.wait_ge(zs_ready, NJ - 1 + b)
                    store(NJ - 2 + b, b)
                for b in range(2):
                    sp.wait_ge(z_stored[b], 16 * NJ)

            @block.gpsimd
            def _(pool):
                for b in range(2):
                    pool.memset(vs[b][:, D:D + 1], 1.0)
                pool.memset(KVB[:], 0.0).then_inc(ones_ready, 1)

                def step(j, b, first):
                    pool.wait_ge(vs_ready, j + 1)
                    pool.tensor_copy(heads(V, j), vs[b][:, 0:D].rearrange("p (h d) -> p h d", h=NH)
                                     ).then_inc(v_copied, 1)
                by_twos(pool, NJ, step)

            @block.tensor
            def _(pe):
                pe.wait_ge(w_in, 112)
                pe.wait_ge(ones_ready, 1)

                def transposes(j, b):
                    pe.wait_ge(x_in[b], 8 * (j - b) + 16)
                    for d in range(KD):
                        last = pe.transpose(tp[:, d, :], xf[b][:, d * P:(d + 1) * P], ident[:])
                    last.then_inc(tp_ready, 1)

                def products(j, b, first):
                    pe.wait_ge(xT_ready, j + 1)
                    if first < 2:
                        pe.wait_ge(q_taken, j - 1)
                    for d in range(KD):
                        last = pe.matmul(qvp[b][:], xT[b][:, d, :], wqv[:, d, :], start=(d == 0), stop=(d == KD - 1))
                    last.then_inc(qv_ready, 1)
                    if first < 3:
                        pe.wait_ge(fk_ready, j)
                    for d in range(KD):
                        last = pe.matmul(kgp[:], xT[b][:, d, :], wkg[:, d, :], start=(d == 0), stop=(d == KD - 1))
                    last.then_inc(kg_ready, 1)
                    if first < 3:
                        pe.wait_ge(gate_ready, j)
                    for s, w in enumerate((w1s, w3s)):
                        for m in range(KD):
                            for d in range(KD):
                                last = pe.matmul(hp[:, s, m, :], w[:, d, m * P:(m + 1) * P], xT[b][:, d, :],
                                                 start=(d == 0), stop=(d == KD - 1))
                    last.then_inc(h_ready, 1)

                def sums(j, b, at):
                    pe.wait_ge(fk_ready, j + 1)
                    pe.wait_ge(vs_ready, j + 1)
                    for m in range(KD):
                        last = pe.matmul(kv[m][:, 0:D + 1], fk[b][:, m * P:(m + 1) * P], vs[b][:],
                                         start=(at == 0), stop=(at == 2), skip_group_check=True)
                    last.then_inc(kv_done, 1)
                    pe.wait_ge(gate_ready, j + 1)
                    if at:
                        pe.wait_ge(zs_ready, j)
                    for m in range(KD):
                        pe.transpose(vtp[:, m * P:(m + 1) * P], vs[b][:, m * P:(m + 1) * P], ident[:])
                    for m in range(KD):
                        last = pe.matmul(zp, gate[b][:, m, :], w2s[:, m, :], start=(m == 0), stop=(m == KD - 1))
                    last.then_inc(z_ready, 1)

                transposes(0, 0)
                products(0, 0, 3)
                transposes(1, 1)
                products(1, 1, 2)
                transposes(2, 0)
                sums(0, 0, 0)
                with pe.Fori(1, NJ // 2 - 1) as i:
                    for b in range(2):
                        j = 2 * i + b
                        products(j, b, 0)
                        transposes(j + 1, 1 - b)
                        sums(j - 1, 1 - b, 1)
                products(NJ - 2, 0, 0)
                transposes(NJ - 1, 1)
                sums(NJ - 3, 1, 1)
                products(NJ - 1, 1, 0)
                sums(NJ - 2, 0, 1)
                sums(NJ - 1, 1, 2)

            @block.scalar
            def _(act):
                act.dma_start(wkg[:, :, 0:D], w_qkv[:, D:2 * D].rearrange("(k p) n -> p k n", p=P)
                              ).then_inc(w_in, 16)
                act.dma_start(wkg[:, :, D:D + NE], w_gate.rearrange("(k p) n -> p k n", p=P)).then_inc(w_in, 16)
                for dst, src in ((w1s, ws1), (w3s, ws3), (w2s, ws2)):
                    act.dma_start(dst[:], src.rearrange("(k p) n -> p k n", p=P)).then_inc(w_in, 16)
                act.preload_act_table(ACT.Exp)

                def store_z(j, b, wait):
                    act.wait_ge(z_ready, j + 1)
                    if wait:
                        act.wait_ge(z_stored[b], 16 * (j - b))
                    act.copy(vt[b][:].rearrange("p m c -> p (m c)"), vtp)
                    act.mul(zs[b][:], zp, 0.5).then_inc(zs_ready, 1)

                def move_xT(j, b):
                    act.wait_ge(tp_ready, j + 1)
                    act.copy(xT[b][:], tp[:]).then_inc(xT_ready, 1)

                def step(j, b, first):
                    act.wait_ge(qv_ready, j + 1)
                    if not first:
                        act.wait_ge(v_copied, j - 1)
                        act.wait_ge(kv_done, j - 1)
                    act.copy(vs[b][:, 0:D], qvp[b][:, D:2 * D]).then_inc(vs_ready, 1)
                    act.copy(heads(Q, j), qvp[b][:, 0:D].rearrange("p (h d) -> p h d", h=NH)).then_inc(q_taken, 1)
                    act.wait_ge(low_ready, j + 1)
                    act.activation(low[b][:], low[b][:], ACT.Exp).then_inc(ex_ready, 1)
                    act.wait_ge(h_ready, j + 1)
                    act.activation(th[b][:], hp[:, 0, :, :], ACT.Tanh, scale=0.5).then_inc(th_ready, 1)

                for b in range(2):
                    move_xT(b, b)
                    step(b, b, True)
                for b in range(2):
                    move_xT(2 + b, b)
                    store_z(b, b, False)
                    step(2 + b, b, False)
                with act.Fori(2, NJ // 2) as i:
                    for b in range(2):
                        j = 2 * i + b
                        move_xT(j, b)
                        store_z(j - 2, b, True)
                        step(j, b, False)
                store_z(NJ - 2, 0, True)
                store_z(NJ - 1, 1, True)

            @block.vector
            def _(ve):
                def step(j, b, first):
                    ve.wait_ge(kg_ready, j + 1)
                    kj = kgp[:, 0:D]
                    ve.tensor_scalar(low[b][:], kj, 0.0, None, ALU.min).then_inc(low_ready, 1)
                    ve.tensor_copy(heads(K, j), kj.rearrange("p (h d) -> p h d", h=NH))
                    ve.tensor_copy(L[:, bass.ds(j, 1), :].rearrange("p a e -> p (a e)"), kgp[:, D:D + NE])
                    ve.wait_ge(ex_ready, j + 1)
                    if not first:
                        ve.wait_ge(kv_done, j - 1)
                    ve.scalar_tensor_tensor(fk[b][:], kj, 0.0, low[b][:], ALU.max, ALU.add).then_inc(fk_ready, 1)
                    ve.wait_ge(th_ready, j + 1)
                    ve.scalar_tensor_tensor(th[b][:], th[b][:], 1.0, hp[:, 0, :, :], ALU.add, ALU.mult
                                            ).then_inc(half_gate, 1)
                    ve.wait_ge(half_gate, j + 1)
                    if not first:
                        ve.wait_ge(z_ready, j - 1)
                    ve.tensor_tensor(gate[b][:], th[b][:], hp[:, 1, :, :], ALU.mult).then_inc(gate_ready, 1)
                by_twos(ve, NJ, step)
                ve.wait_ge(kv_done, NJ)
                ve.wait_ge(ones_ready, 1)
                for h in range(NH):
                    m, q = h // 4, slice(DH * (h % 4), DH * (h % 4) + DH)
                    ve.tensor_copy(KVB[q, m, q], kv[m][q, h * DH:(h + 1) * DH])
                    ve.tensor_copy(KVB[q, m, P + h % 4:P + h % 4 + 1], kv[m][q, D:D + 1])


def stage_routing_and_convolution(nc, conv_w, vt_dram, conv_dram, ident, L, WK, SIDX, GIDX, EXP):
    KD = D // P
    BLK = 4
    OWN = 2 * BLK
    with Core(nc) as k:
        VT = k.sb("i_vt", [P, KD, LEAD + NJ, P])
        cw = k.sb("i_cw", [P, KD, KCONV])
        dg = k.sb("i_dg", [P, KD, KCONV, P])
        cs = [k.sb(f"i_cs{b}", [P, BLK, P]) for b in range(2)]
        own = [k.sb(f"i_own{m}", [P, OWN, P]) for m in range(KD)]
        own_ready, own_stored = k.sem("i_own_ready"), k.sem("i_own_stored")
        cp = [k.ps(f"i_cp{b}", [P, BLK, P]) for b in range(2)]
        vt_in = [k.sem(f"i_vt_in{m}") for m in range(KD)]
        cw_in, led = k.sem("i_cw_in"), k.sem("i_led")
        dg_ready, cp_ready, cs_ready = k.sem("i_dg_ready"), k.sem("i_cp_ready"), k.sem("i_cs_ready")
        conv_stored = [k.sem(f"i_conv_stored{b}") for b in range(2)]

        def blocks(eng, unit, between=None):
            NB = (NJ - OWN) // BLK
            for b in range(2):
                unit(0, b, b, b, True)
            if between:
                between()
            for m in range(KD):
                with eng.Fori(1 - m, NB // 2) as i:
                    for b in range(2):
                        unit(m, 2 * i + b, b, NB * m + 2 * i + b, False)

        one = [P, NJ, NE]
        E, A, B, OH = k.sb("h_e", one), k.sb("h_a", one), k.sb("h_b", one), k.sb("h_oh", one)
        SL, PR = k.sb("h_sl", one), k.sb("h_pr", one)
        G1 = k.sb("h_g1", [P, NGR, NE])
        M8, I8 = k.sb("h_m8", [P, NJ, 8]), k.sb("h_i8", [P, NJ, 8], U32)
        IF = k.sb("h_if", [P, NJ, 8])
        mx, POS, KEPT = k.sb("h_mx", [P, NJ]), k.sb("h_pos", [P, NJ, TOPK]), k.sb("h_kept", [P, NJ, TOPK])
        ie, ig = k.sb("h_ie", [P, NE]), k.sb("h_ig", [P, NGR])
        tri, ones = k.sb("h_tri", [P, P]), k.sb("h_ones", [P, P])
        ng, sa, sb_, ex = k.sb("h_ng", [P, NE]), k.sb("h_sa", [P, NE]), k.sb("h_sb", [P, NE]), k.sb("h_ex", [P, NGR])
        cnt = k.ps("h_cnt", [P, 2, NE])
        pl, vl, const_ready = k.sem("h_pl"), k.sem("h_vl"), k.sem("h_const")
        shifted, exped, tot_ready, cnt_ready = (k.sem(f"h_{n}") for n in ("shifted", "exped", "tot", "cnt"))
        with nc.Block() as block:

            @block.gpsimd
            def _(pool):
                link = Chain(pool, pl)
                link(pool.iota(ie[:], pattern=[[1, NE]], base=0, channel_multiplier=0,
                               allow_small_or_imprecise_dtypes=True))
                link(pool.iota(ig[:], pattern=[[1, NGR]], base=0, channel_multiplier=0,
                               allow_small_or_imprecise_dtypes=True))
                link(pool.memset(ones[:], 1.0))
                link(pool.affine_select(out=tri[:], in_=ones[:], compare_op=ALU.is_ge, fill=0.0, base=-1,
                                        pattern=[[1, P]], channel_multiplier=-1))
                pool.sem_inc(const_ready, 1)

            @block.scalar
            def _(act):
                act.dma_start(cw[:], conv_w.rearrange("(m c) t -> c m t", c=P)).then_inc(cw_in, 16)
                for m in range(KD):
                    act.dma_start(VT[:, m, LEAD:LEAD + NJ, :], vt_dram[:, m]).then_inc(vt_in[m], 16)
                    act.dma_start(VT[:, m, 0:LEAD, 1:P], vt_dram[:, m, NJ - LEAD:NJ, 0:P - 1]).then_inc(vt_in[m], 16)
                act.wait_ge(shifted, 1)
                act.activation(E[:], E[:], ACT.Exp).then_inc(exped, 1)

                def unit(m, i, b, n, first):
                    act.wait_ge(cp_ready, n + 1)
                    if not first:
                        act.wait_ge(conv_stored[b], 8 * (n - b))
                    act.copy(cs[b][:], cp[b][:]).then_inc(cs_ready, 1)
                    act.wait_ge(cs_ready, n + 1)
                    act.dma_start(conv_dram[:, m, bass.ds(BLK * i, BLK), :], cs[b][:]).then_inc(conv_stored[b], 16)
                blocks(act, unit)
                for b in range(2):
                    act.wait_ge(conv_stored[b], 8 * KD * (NJ - OWN) // BLK)

            @block.tensor
            def _(pe):
                pe.wait_ge(led, 1)
                pe.wait_ge(dg_ready, KD * KCONV)

                def unit(m, i, b, n, first):
                    pe.wait_ge(vt_in[m], 32)
                    if not first:
                        pe.wait_ge(cs_ready, n - 1)
                    for o in range(KCONV):
                        last = pe.matmul(cp[b][:], dg[:, m, o, :], VT[:, m, bass.ds(BLK * i + LEAD - o, BLK), :],
                                         start=(o == 0), stop=(o == KCONV - 1))
                    last.then_inc(cp_ready, 1)

                def counts():
                    pe.wait_ge(const_ready, 1)
                    pe.wait_ge(tot_ready, 1)
                    pe.matmul(cnt[:, 0, :], tri[:], sa[:], start=True, stop=True)
                    pe.matmul(cnt[:, 1, :], ones[:], sa[:], start=True, stop=True).then_inc(cnt_ready, 1)
                blocks(pe, unit, counts)

            @block.vector
            def _(ve):
                ve.memset(VT[:, :, 0:LEAD, 0:1], 0.0).then_inc(led, 1)
                ve.wait_ge(cw_in, 16)
                for m in range(KD):
                    for o in range(KCONV):
                        t = KCONV - 1 - o
                        ve.tensor_scalar(dg[:, m, o, :], ident[:], cw[:, m, t:t + 1], None, ALU.mult
                                         ).then_inc(dg_ready, 1)
                link = Chain(ve, vl)

                def tt(o, a, b, op):
                    link(ve.tensor_tensor(o, a, b, op))

                def ts(o, a, s1, s2, op0, op1=ALU.bypass):
                    link(ve.tensor_scalar(o, a, s1, s2, op0, op1))

                def over_e(a):
                    return a.unsqueeze(2).to_broadcast(one)

                def over_j(a):
                    return a.unsqueeze(1).to_broadcast(one)

                link(ve.tensor_reduce(mx[:], L[:], AX_X, ALU.max))
                ve.tensor_tensor(E[:], L[:], over_e(mx[:]), ALU.subtract).then_inc(shifted, 1)
                ve.wait_ge(exped, 1)
                link(ve.tensor_reduce(mx[:], E[:], AX_X, ALU.add))
                link(ve.reciprocal(mx[:], mx[:]))
                tt(E[:], E[:], over_e(mx[:]), ALU.mult)
                for j in range(NJ):
                    ve.max(M8[:, j, :], E[:, j, :])
                ve.drain()
                for j in range(NJ):
                    ve.max_index(I8[:, j, :], M8[:, j, :], E[:, j, :])
                ve.drain()
                link(ve.tensor_copy(IF[:], I8[:]))
                ve.wait_ge(const_ready, 1)
                for n in range(TOPK):
                    tt(OH[:], over_j(ie[:]), over_e(IF[:, :, n]), ALU.is_equal)
                    if n == 0:
                        link(ve.tensor_copy(A[:], OH[:]))
                    else:
                        tt(A[:], A[:], OH[:], ALU.add)
                link(ve.tensor_copy(SL[:], A[:]))
                a, b, s = A, B, 1
                while s < NJ:
                    link(ve.tensor_copy(b[:, 0:s, :], a[:, 0:s, :]))
                    tt(b[:, s:NJ, :], a[:, s:NJ, :], a[:, 0:NJ - s, :], ALU.add)
                    a, b, s = b, a, 2 * s
                link(ve.tensor_copy(sa[:], a[:, NJ - 1, :]))
                ve.sem_inc(tot_ready, 1)
                ve.wait_ge(cnt_ready, 1)
                tt(a[:], a[:], SL[:], ALU.subtract)
                tt(a[:], a[:], over_j(cnt[:, 0, :]), ALU.add)
                ts(ng[:], cnt[:, 1, :], float(CAP), None, ALU.min)
                ts(ng[:], ng[:], 1.0 / GT, (GT - 1.0) / GT - 0.5 + 0.5 / GT, ALU.mult, ALU.add)
                ts(ng[:], ng[:], MAGIC, MAGIC, ALU.add, ALU.subtract)
                link(ve.tensor_copy(sa[:], ng[:]))
                c, d, s = sa, sb_, 1
                while s < NE:
                    link(ve.tensor_copy(d[:, 0:s], c[:, 0:s]))
                    tt(d[:, s:NE], c[:, s:NE], c[:, 0:NE - s], ALU.add)
                    c, d, s = d, c, 2 * s
                tt(G1[:], c[:].unsqueeze(1).to_broadcast([P, NGR, NE]), ig[:].unsqueeze(2).to_broadcast([P, NGR, NE]),
                   ALU.is_le)
                link(ve.tensor_reduce(ex[:], G1[:], AX_X, ALU.add))
                ts(ex[:], ex[:], NE - 1.0, None, ALU.min)
                link(ve.tensor_copy(EXP[:], ex[:]))
                tt(d[:], c[:], ng[:], ALU.subtract)
                ts(d[:], d[:], float(GT), None, ALU.mult)
                ts(SL[:], a[:], float(CAP), 4.0 * SLOTS, ALU.is_ge, ALU.mult)
                tt(SL[:], SL[:], a[:], ALU.add)
                tt(SL[:], SL[:], over_j(d[:]), ALU.add)
                for n in range(TOPK):
                    tt(OH[:], over_j(ie[:]), over_e(IF[:, :, n]), ALU.is_equal)
                    tt(PR[:], OH[:], SL[:], ALU.mult)
                    link(ve.tensor_reduce(POS[:, :, n], PR[:], AX_X, ALU.add))
                link(ve.tensor_copy(SIDX[:], POS[:]))
                ts(KEPT[:], POS[:], float(SLOTS), None, ALU.is_lt)
                tt(WK[:], M8[:, :, 0:TOPK], KEPT[:], ALU.mult)
                tt(POS[:], POS[:], KEPT[:], ALU.mult)
                link(ve.tensor_copy(GIDX[:], POS[:]))
                for m in range(KD):
                    ve.wait_ge(vt_in[m], 32)
                    for o in range(KCONV):
                        v = VT[:, m, LEAD + NJ - OWN - o:LEAD + NJ - o, :]
                        w = cw[:, m, KCONV - 1 - o:KCONV - o]
                        if o == 0:
                            ts(own[m][:], v, w, None, ALU.mult)
                        else:
                            link(ve.scalar_tensor_tensor(own[m][:], v, w, own[m][:], ALU.mult, ALU.add))
                    ve.sem_inc(own_ready, 1)

            @block.sync
            def _(sp):
                for m in range(KD):
                    sp.wait_ge(own_ready, m + 1)
                    sp.dma_start(conv_dram[:, m, NJ - OWN:NJ, :], own[m][:]).then_inc(own_stored, 16)
                sp.wait_ge(own_stored, 16 * KD)




def stage_experts_and_attention(nc, w1, w2, w3, xn1_dram, xs_dram, o_dram, ident, SIDX, EXP, Q, K, V):
    KD = D // P
    SOLO = 2
    PER = NGR // (NH - SOLO)
    SCALE = float(DH) ** -0.5
    GATES_BESIDE_SCORES, GATES_BESIDE_SUMS = (0, 1, 2, 4, 5, 6, 8, 9, 10, 12), (0, 1, 2, 3, 4, 5)
    K_COPIES = ((0, 1), (2, 3), (4,), (5,), (6,))
    EXP_AT = len(GATES_BESIDE_SCORES) - 2
    with Core(nc) as k:
        KC, VC = (k.sb(n, [P, len(SHIFTS), NJ, DH]) for n in ("j_kc", "j_vc"))
        prod, acc = k.sb("j_prod", [P, NJ, DH]), k.sb("j_acc", [P, NJ, DH])
        pprod = [k.sb(f"j_pprod{i}", [P, NJ, DH]) for i in range(len(POOL_SCORES))]
        pacc = pprod[-1]
        SC, MASK = k.sb("j_sc", [P, len(OFFSETS), NJ]), k.sb("j_mask", [P, len(OFFSETS), NJ])
        PW = k.sb("j_pw", [P, len(POOL_SUMS), NJ])
        mx = k.sb("j_mx", [P, NJ])
        WA = [k.sb(f"j_wa{b}", [P, 2, KD, HM]) for b in range(2)]
        WB = [k.sb(f"j_wb{r}", [P, D]) for r in range(RING)]
        xs = [k.sb(f"j_xs{b}", [P, 2, D]) for b in range(2)]
        xT = [k.sb(f"j_xT{b}", [P, KD, GT]) for b in range(2)]
        th = [k.sb(f"j_th{b}", [P, GT]) for b in range(2)]
        gate = [k.sb(f"j_gate{b}", [P, GT]) for b in range(2)]
        ob = [k.sb(f"j_ob{b}", [P, 2, D]) for b in range(2)]
        tp = [k.ps(f"j_tp{b}", [P, KD, GT]) for b in range(2)]
        hp = [k.ps(f"j_hp{b}", [P, 2, GT]) for b in range(2)]
        op = [k.ps(f"j_op{b}", [P, 2, D]) for b in range(2)]
        wa_in, x_in = ([k.sem(f"j_{n}_in{b}") for b in range(2)] for n in ("wa", "x"))
        wb_in = [k.sem(f"j_wb_in{r}") for r in range(RING)]
        tp_ready, xT_ready, h_ready, th_ready = (k.sem(f"j_{n}_ready") for n in ("tp", "xT", "h", "th"))
        gate_ready, o_ready, ob_ready = (k.sem(f"j_{n}") for n in ("gated", "o", "ob"))
        stored = [k.sem(f"j_stored{b}") for b in range(2)]
        pl, vl, zeroed, masked = (k.sem(f"j_{n}") for n in ("pl", "vl", "zeroed", "masked"))
        k_in, v_in, multiplied = k.sem("j_k_in"), k.sem("j_v_in"), k.sem("j_multiplied")
        weighed, shifted, exped = (k.sem(f"j_{n}") for n in ("weighed", "shifted", "exped"))
        summed, whole, alone = k.sem("j_summed"), k.sem("j_whole"), k.sem("j_alone")
        ring = range(RING)
        xr = [ob[b // 2][:, b % 2, :] for b in ring]
        ix = [k.sb(f"j_ix{b}", [P, TOPK], U32) for b in ring]
        row_in = [k.sem(f"j_row_in{b}") for b in ring]
        ix_ready, sent, scattered = k.sem("j_ix_ready"), [k.sem(f"j_sent{b}") for b in ring], k.sem("j_scattered")
        waited = k.sem("j_waited")

        def heads(eng, body):
            body(SOLO, 0)
            with eng.Fori(SOLO + 1, NH - 1) as h:
                body(h, 1)
            body(NH - 1, 2)

        def head(a, h):
            return a[:, bass.ds(h, 1), :, :].rearrange("p a j d -> p (a j) d")

        def back(copies, a, h, o):
            if o == 0:
                return [(slice(0, NJ), head(a, h))]
            if o < NJ:
                return [(slice(0, o), copies[:, SHIFTS.index(1), NJ - o:NJ, :]),
                        (slice(o, NJ), head(a, h)[:, 0:NJ - o, :])]
            return [(slice(0, NJ), copies[:, SHIFTS.index(o // NJ), :, :])]

        def shifted_copies(eng, dst, src, h, sem, which=range(len(SHIFTS))):
            for i in which:
                m = SHIFTS[i]
                eng.dma_start(dst[m:P, i, :, :], head(src, h)[0:P - m]).then_inc(sem, 16)

        COPIED = 16 * len(SHIFTS)

        class HeadChain:

            def __init__(self, eng, sem, before=0):
                self.eng, self.sem, self.before, self.per, self.n, self.h = eng, sem, before, None, 0, 0

            def start(self, h, which):
                if which == 1:
                    self.per = self.n
                self.h, self.n = h, 0

            def __call__(self, *steps):
                for ins in steps:
                    self.n += 1
                    ins.then_inc(self.sem, 1)
                done = self.before + self.n if self.per is None else self.before + self.per * (self.h - SOLO) + self.n
                self.eng.wait_ge(self.sem, done)

        with nc.Block() as block:

            @block.sync
            def _(sp):
                def load_tokens(g, b, first):
                    if not first:
                        sp.wait_ge(tp_ready, g - 1)
                    sp.dma_start(xs[b][:], xs_dram[bass.ds(g * GT, GT), :].rearrange("(t p) d -> p t d", p=P)
                                 ).then_inc(x_in[b], 16)

                def load_weights(g, r, first):
                    b = r % 2
                    e = sp.value_load(EXP[0:1, bass.ds(g, 1)], min_val=0, max_val=NE - 1)
                    if first < 2:
                        sp.wait_ge(h_ready, g - 1)
                    for i, w in enumerate((w1, w3)):
                        sp.dma_start(WA[b][:, i, :, :], w[bass.ds(e, 1)].rearrange("e (k p) n -> p (e k) n", p=P)
                                     ).then_inc(wa_in[b], 16)
                    if first < 1:
                        sp.wait_ge(o_ready, g - RING + 1)
                    sp.dma_start(WB[r][:], w2[bass.ds(e, 1)].rearrange("e p n -> p (e n)")).then_inc(wb_in[r], 16)

                def load_row(j, b, first):
                    if not first:
                        sp.wait_ge(sent[b], 16 * TOPK // RING * (j - b))
                    sp.dma_start(xr[b], token_rows(xn1_dram, j)).then_inc(row_in[b], 16)

                by_rings(sp, NJ, load_row)
                sp.wait_ge(scattered, 1)
                load_tokens(0, 0, True)
                load_tokens(1, 1, True)
                for g in range(RING):
                    load_weights(g, g, 2 if g < 2 else 1)
                    load_tokens(g + 2, g % 2, False)
                with sp.Fori(1, NGR // RING - 1) as i:
                    for r in range(RING):
                        load_weights(RING * i + r, r, 0)
                        load_tokens(RING * i + r + 2, r % 2, False)
                for g in range(NGR - RING, NGR):
                    load_weights(g, g % RING, 0)
                    if g + 2 < NGR:
                        load_tokens(g + 2, g % 2, False)

            @block.tensor
            def _(pe):
                def transposes(g, b):
                    pe.wait_ge(x_in[b], 8 * (g - b) + 16)
                    for t in range(2):
                        for d in range(KD):
                            last = pe.transpose(tp[b][:, d, t * P:(t + 1) * P], xs[b][:, t, d * P:(d + 1) * P],
                                                ident[:])
                    last.then_inc(tp_ready, 1)

                def hidden(g, b):
                    pe.wait_ge(xT_ready, g + 1)
                    pe.wait_ge(wa_in[b], 16 * (g - b) + 32)
                    for i in range(2):
                        for d in range(KD):
                            last = pe.matmul(hp[b][:, i, :], WA[b][:, i, d, :], xT[b][:, d, :],
                                             start=(d == 0), stop=(d == KD - 1))
                    last.then_inc(h_ready, 1)

                def outputs(g, r, first):
                    b = r % 2
                    pe.wait_ge(gate_ready, g + 1)
                    pe.wait_ge(wb_in[r], 16 // RING * (g - r) + 16)
                    if not first:
                        pe.wait_ge(ob_ready, g - 1)
                    for t in range(2):
                        last = pe.matmul(op[b][:, t, :], gate[b][:, t * P:(t + 1) * P], WB[r][:],
                                         start=True, stop=True)
                    last.then_inc(o_ready, 1)

                def step(g, r, first):
                    transposes(g + 2, r % 2)
                    hidden(g + 1, 1 - r % 2)
                    outputs(g, r, first)

                transposes(0, 0)
                transposes(1, 1)
                hidden(0, 0)
                for g in range(RING):
                    step(g, g, g < 2)
                with pe.Fori(1, NGR // RING - 1) as i:
                    for r in range(RING):
                        step(RING * i + r, r, False)
                for g in (NGR - 4, NGR - 3):
                    step(g, g % RING, False)
                hidden(NGR - 1, 1)
                for g in (NGR - 2, NGR - 1):
                    outputs(g, g % RING, False)

            @block.scalar
            def _(act):
                act.preload_act_table(ACT.Exp)
                act.wait_ge(zeroed, 1)
                shifted_copies(act, KC, K, 0, k_in)
                act.wait_ge(zeroed, 2)
                shifted_copies(act, VC, V, 0, v_in)
                for h in range(SOLO):
                    act.wait_ge(shifted, h + 1)
                    act.activation(SC[:], SC[:], ACT.Exp, scale=SCALE).then_inc(exped, 1)
                    shifted_copies(act, KC, K, h + 1, k_in)
                    act.wait_ge(alone, h + 1)
                    shifted_copies(act, VC, V, h + 1, v_in)
                act.preload_act_table(ACT.Silu)

                def move_xT(g, b, wait):
                    act.wait_ge(tp_ready, g + 1)
                    if wait:
                        act.wait_ge(h_ready, g - 1)
                    act.copy(xT[b][:], tp[b][:]).then_inc(xT_ready, 1)

                def silu(g, b, wait):
                    act.wait_ge(h_ready, g + 1)
                    if wait:
                        act.wait_ge(gate_ready, g - 1)
                    act.activation(th[b][:], hp[b][:, 0, :], ACT.Silu).then_inc(th_ready, 1)

                def move_out(g, b, wait):
                    act.wait_ge(o_ready, g + 1)
                    if wait:
                        act.wait_ge(stored[b], 8 * (g - b))
                    act.copy(ob[b][:], op[b][:]).then_inc(ob_ready, 1)

                def store(g, b):
                    act.wait_ge(ob_ready, g + 1)
                    act.dma_start(o_dram[bass.ds(g * GT, GT), :].rearrange("(t p) d -> p t d", p=P), ob[b][:]
                                  ).then_inc(stored[b], 16)

                def body(h, which):
                    for n in range(PER):
                        g, b, end = (h - SOLO) * PER + n, n % 2, which == 2 and n >= PER - 2
                        if not end:
                            move_xT(g + 2, b, True)
                        if which > 0 or n > 0:
                            store(g - 1, 1 - b)
                        if not (end and n == PER - 1):
                            silu(g + 1, 1 - b, which > 0 or n > 0)
                        move_out(g, b, which > 0 or n > 1)
                        if n == EXP_AT:
                            act.wait_ge(shifted, h + 1)
                            act.activation(SC[:], SC[:], ACT.Exp, scale=SCALE).then_inc(exped, 1)
                        if 0 <= EXP_AT - n < len(SHIFTS) and which > 0:
                            act.wait_ge(whole, h - SOLO)
                            shifted_copies(act, VC, V, h, v_in, (EXP_AT - n,))
                        if EXP_AT <= n < EXP_AT + len(K_COPIES) and which < 2:
                            shifted_copies(act, KC, K, h + 1, k_in, K_COPIES[n - EXP_AT])

                move_xT(0, 0, False)
                move_xT(1, 1, False)
                silu(0, 0, False)
                heads(act, body)
                store(NGR - 1, 1)
                for b in range(2):
                    act.wait_ge(stored[b], 8 * NGR)

            @block.gpsimd
            def _(pool):
                link = Chain(pool, pl)
                link(pool.memset(MASK[:], 0.0))
                for s, o in enumerate(OFFSETS):
                    link(pool.affine_select(out=MASK[:, s, :], in_=MASK[:, s, :], compare_op=ALU.is_ge, fill=-FAR,
                                            base=-o, pattern=[[1, NJ]], channel_multiplier=NJ))
                pool.sem_inc(masked, 1)

                def products(h, link):
                    pool.wait_ge(k_in, COPIED * h + COPIED)
                    for i, s in enumerate(POOL_SCORES):
                        link(*[pool.tensor_tensor(pprod[i][:, js, :], head(Q, h)[:, js, :], src, ALU.mult)
                               for js, src in back(KC, K, h, OFFSETS[s])])
                        pool.sem_inc(multiplied, 1)

                def scatter(j, b, first):
                    if not first:
                        pool.wait_ge(sent[b], 16 * TOPK // RING * (j - b))
                        pool.sem_inc(waited, 1)
                    pool.tensor_copy(ix[b][:], SIDX[:, bass.ds(j, 1), :].rearrange("p a n -> p (a n)")
                                     ).then_inc(ix_ready, 1)
                    pool.wait_ge(ix_ready, j + 1)
                    pool.sem_inc(waited, 1)
                    pool.wait_ge(row_in[b], 16 // RING * (j - b) + 16)
                    pool.sem_inc(waited, 1)
                    for n in range(TOPK):
                        pool.indirect_dma_start(xs_dram, bass.IndirectOffsetOnAxis(ix[b][:, n:n + 1], 0), xr[b],
                                                None, bounds_check=SLOTS - 1, oob_is_err=False
                                                ).then_inc(sent[b], 16)

                by_rings(pool, NJ, scatter)
                for b in ring:
                    pool.wait_ge(sent[b], 16 * TOPK // RING * NJ)
                pool.sem_inc(scattered, 1)
                products(SOLO, link)
                hlink = HeadChain(pool, pl, link.n)

                def body(h, which):
                    hlink.start(h, which)
                    pool.wait_ge(weighed, h - SOLO + 1)
                    pool.wait_ge(v_in, COPIED * h + COPIED)
                    for i, s in enumerate(POOL_SUMS):
                        w = PW[:, i, :].unsqueeze(2).to_broadcast([P, NJ, DH])
                        dst = pprod[0] if i else pacc
                        hlink(*[pool.tensor_tensor(dst[:, js, :], src, w[:, js, :], ALU.mult)
                                for js, src in back(VC, V, h, OFFSETS[s])])
                        if i:
                            hlink(pool.tensor_tensor(pacc[:], pacc[:], pprod[0][:], ALU.add))
                    pool.wait_ge(summed, h - SOLO + 1)
                    hlink(pool.tensor_tensor(head(K, h), acc[:], pacc[:], ALU.add))
                    pool.sem_inc(whole, 1)
                    if which < 2:
                        products(h + 1, hlink)
                heads(pool, body)

            @block.vector
            def _(ve):
                link = Chain(ve, vl)
                ve.memset(KC[:], 0.0).then_inc(zeroed, 1)
                ve.memset(VC[:], 0.0).then_inc(zeroed, 1)

                def gated(g, b, wait):
                    ve.wait_ge(th_ready, g + 1)
                    if wait:
                        ve.wait_ge(o_ready, g - 1)
                    ve.tensor_tensor(gate[b][:], th[b][:], hp[b][:, 1, :], ALU.mult).then_inc(gate_ready, 1)

                def every(count):
                    return mx[:].unsqueeze(1).to_broadcast([P, count, NJ])

                def exponentials(h, done):
                    by_token = SC[:].rearrange("p s j -> p j s")
                    ve.wait_ge(masked, 1)
                    done(ve.tensor_tensor(SC[:], SC[:], MASK[:], ALU.add))
                    done(ve.tensor_reduce(mx[:], by_token, AX_X, ALU.max))
                    ve.tensor_tensor(SC[:], SC[:], every(len(OFFSETS)), ALU.subtract).then_inc(shifted, 1)
                    ve.wait_ge(exped, h + 1)
                    done(ve.tensor_reduce(mx[:], by_token, AX_X, ALU.add))
                    done(ve.reciprocal(mx[:], mx[:]))

                for h in range(SOLO):
                    ve.wait_ge(k_in, COPIED * h + COPIED)
                    for s, o in enumerate(OFFSETS):
                        for js, ks in back(KC, K, h, o):
                            link(ve.tensor_tensor(prod[:, js, :], head(Q, h)[:, js, :], ks, ALU.mult))
                        link(ve.tensor_reduce(SC[:, s, :], prod[:], AX_X, ALU.add))
                    exponentials(h, link)
                    link(ve.tensor_tensor(SC[:], SC[:], every(len(OFFSETS)), ALU.mult))
                    ve.wait_ge(v_in, COPIED * h + COPIED)
                    for s, o in enumerate(OFFSETS):
                        w = SC[:, s, :].unsqueeze(2).to_broadcast([P, NJ, DH])
                        for js, src in back(VC, V, h, o):
                            link(ve.tensor_tensor((prod if s else acc)[:, js, :], src, w[:, js, :], ALU.mult))
                        if s:
                            dst = head(K, h) if s == len(OFFSETS) - 1 else acc[:]
                            link(ve.tensor_tensor(dst, acc[:], prod[:], ALU.add))
                    ve.sem_inc(alone, 1)
                hlink = HeadChain(ve, vl, link.n)

                def body(h, which):
                    hlink.start(h, which)
                    ve.wait_ge(k_in, COPIED * h + COPIED)
                    n = 0
                    own = [s for s in range(len(OFFSETS)) if s not in POOL_SCORES]
                    for i, s in enumerate(own + POOL_SCORES):
                        if s in POOL_SCORES:
                            src = pprod[POOL_SCORES.index(s)]
                            ve.wait_ge(multiplied, len(POOL_SCORES) * (h - SOLO) + POOL_SCORES.index(s) + 1)
                        else:
                            src = prod
                            hlink(*[ve.tensor_tensor(prod[:, js, :], head(Q, h)[:, js, :], ks, ALU.mult)
                                    for js, ks in back(KC, K, h, OFFSETS[s])])
                        hlink(ve.tensor_reduce(SC[:, s, :], src[:], AX_X, ALU.add))
                        if i in GATES_BESIDE_SCORES:
                            gated((h - SOLO) * PER + n, n % 2, which > 0 or n > 1)
                            n += 1
                    exponentials(h, hlink)
                    first = POOL_SUMS[0]
                    hlink(ve.tensor_tensor(PW[:], SC[:, first:, :], every(len(POOL_SUMS)), ALU.mult))
                    ve.sem_inc(weighed, 1)
                    hlink(ve.tensor_tensor(SC[:, 0:first, :], SC[:, 0:first, :], every(first), ALU.mult))
                    ve.wait_ge(v_in, COPIED * h + COPIED)
                    for s in range(first):
                        w = SC[:, s, :].unsqueeze(2).to_broadcast([P, NJ, DH])
                        dst = prod if s else acc
                        hlink(*[ve.tensor_tensor(dst[:, js, :], src, w[:, js, :], ALU.mult)
                                for js, src in back(VC, V, h, OFFSETS[s])])
                        if s:
                            hlink(ve.tensor_tensor(acc[:], acc[:], prod[:], ALU.add))
                        if s in GATES_BESIDE_SUMS:
                            gated((h - SOLO) * PER + n, n % 2, True)
                            n += 1
                    ve.sem_inc(summed, 1)
                heads(ve, body)


def stage_mix1(nc, w_o, xn1_dram, x1_dram, z_dram, o_dram, conv_dram, ident, Q, K, KVB, WK, GIDX, out):
    KD = D // P
    LW = P + 4
    with Core(nc) as k:
        wo = k.sb("m_wo", [P, KD, D])
        two, ring = range(2), range(RING)
        xr = [k.sb(f"m_xn{b}", [P, D]) for b in ring]
        x1 = [k.sb(f"m_x1{b}", [P, D]) for b in ring]
        zr = [k.sb(f"m_z{b}", [P, D]) for b in ring]
        cT = [k.sb(f"m_cT{b}", [P, KD, P]) for b in ring]
        ix = [k.sb(f"m_ix{b}", [P, TOPK], U32) for b in ring]
        gt = [k.sb(f"m_gt{b}", [P, TOPK, D]) for b in ring]
        ex = [k.sb(f"m_ex{b}", [P, D]) for b in two]
        fq = [k.sb(f"m_fq{b}", [P, D]) for b in two]
        fqT = [k.sb(f"m_fqT{b}", [P, KD, P]) for b in two]
        rz = [k.sb(f"m_rz{b}", [P, KD, 4]) for b in two]
        hs = [k.sb(f"m_h{b}", [P, D]) for b in two]
        hT = [k.sb(f"m_hT{b}", [P, KD, P]) for b in two]
        s1 = [k.sb(f"m_s1{b}", [P, D]) for b in two]
        th = [k.sb(f"m_th{b}", [P, D]) for b in two]
        res = [k.sb(f"m_res{b}", [P, D]) for b in two]
        qp = [k.ps(f"m_qp{b}", [P, KD, P]) for b in two]
        lp = [k.ps(f"m_lp{b}", [P, KD, LW]) for b in two]
        hp = [k.ps(f"m_hp{b}", [P, KD, P]) for b in two]
        ap = [k.ps(f"m_ap{b}", [P, D]) for b in two]
        wo_in, cT_in = k.sem("m_wo_in"), [k.sem(f"m_cT_in{b}") for b in ring]
        rows_in, got = [k.sem(f"m_rows_in{b}") for b in ring], [k.sem(f"m_got{b}") for b in ring]
        ix_ready, vl, stored = k.sem("m_ix_ready"), k.sem("m_vl"), [k.sem(f"m_stored{b}") for b in two]
        min_ready, ex_ready, fq_ready, qp_ready = (k.sem(f"m_{n}_ready") for n in ("min", "ex", "fq", "qp"))
        fqT_ready, lp_ready, hs_ready, hp_ready = (k.sem(f"m_{n}_ready") for n in ("fqT", "lp", "hs", "hp"))
        hT_ready, ap_ready, f_ready, th_ready = (k.sem(f"m_{n}_ready") for n in ("hT", "ap", "f", "th"))
        res_ready = k.sem("m_res_ready")
        waited = k.sem("m_waited")

        def heads(a, j):
            return a[:, :, bass.ds(j, 1), :].rearrange("p h a d -> p h (a d)")

        def steps(eng, step):
            def single(j):
                step(j, j % RING, lambda lag: 0 <= j - lag < NJ)

            for j in ring:
                single(j)
            with eng.Fori(1, NJ // RING - 1) as i:
                for r in ring:
                    step(RING * i + r, r, lambda lag: True)
            for j in range(NJ - RING, NJ + 2):
                single(j)

        def by_head(a):
            return a[:].rearrange("p (h d) -> p h d", h=NH)

        with nc.Block() as block:

            @block.sync
            def _(sp):
                sp.dma_start(wo[:], w_o.rearrange("(k p) n -> p k n", p=P)).then_inc(wo_in, 16)

                def store(j, b):
                    sp.dma_start(token_rows(out[0], j), res[b][:]).then_inc(stored[b], 16)

                def load(j, r, first):
                    if not first:
                        sp.wait_ge(res_ready, j - RING + 1)
                        store(j - RING, r % 2)
                    for dst, src in ((zr, z_dram), (xr, xn1_dram), (x1, x1_dram)):
                        sp.dma_start(dst[r][:], token_rows(src, j)).then_inc(rows_in[r], 16)
                    sp.dma_start(cT[r][:], conv_dram[:, :, bass.ds(j, 1), :].rearrange("c m a p -> c m (a p)")
                                 ).then_inc(cT_in[r], 16)
                by_rings(sp, NJ, load)
                for j in range(NJ - RING, NJ):
                    sp.wait_ge(res_ready, j + 1)
                    store(j, j % 2)
                for b in two:
                    sp.wait_ge(stored[b], 8 * NJ)

            @block.gpsimd
            def _(pool):
                def step(j, b, first):
                    if not first:
                        pool.wait_ge(got[b], 4 * TOPK * (j - b))
                        pool.sem_inc(waited, 1)
                        pool.wait_ge(f_ready, j - RING + 1)
                        pool.sem_inc(waited, 1)
                    pool.tensor_copy(ix[b][:], GIDX[:, bass.ds(j, 1), :].rearrange("p a n -> p (a n)")
                                     ).then_inc(ix_ready, 1)
                    pool.wait_ge(ix_ready, j + 1)
                    pool.sem_inc(waited, 1)
                    for n in range(TOPK):
                        pool.indirect_dma_start(gt[b][:, n, :], None, o_dram,
                                                bass.IndirectOffsetOnAxis(ix[b][:, n:n + 1], 0)).then_inc(got[b], 16)
                by_rings(pool, NJ, step)

            @block.tensor
            def _(pe):
                pe.wait_ge(wo_in, 16)

                def product(j, r, part, first):
                    b = r % 2
                    for d in range(KD):
                        last = pe.matmul(ap[b][:], part[:, d, :], wo[:, d, :], start=(first and d == 0),
                                         stop=(not first and d == KD - 1))
                    return last

                def step(j, r, has):
                    b, r1 = r % 2, (r - 1) % RING
                    if has(0):
                        pe.wait_ge(fq_ready, j + 1)
                        for d in range(KD):
                            last = pe.transpose(qp[b][:, d, :], fq[b][:, d * P:(d + 1) * P], ident[:])
                        last.then_inc(qp_ready, 1)
                    if has(1):
                        pe.wait_ge(cT_in[r1], 4 * (j - 1 - r1) + 16)
                        if has(3):
                            pe.wait_ge(res_ready, j - 2)
                        product(j - 1, r1, cT[r1], True)
                    if has(0):
                        pe.wait_ge(fqT_ready, j + 1)
                        for m in range(KD):
                            last = pe.matmul(lp[b][:, m, :], fqT[b][:, m, :], KVB[:, m, :], start=True, stop=True)
                        last.then_inc(lp_ready, 1)
                    if has(1):
                        pe.wait_ge(hs_ready, j)
                        for d in range(KD):
                            last = pe.transpose(hp[1 - b][:, d, :], hs[1 - b][:, d * P:(d + 1) * P], ident[:])
                        last.then_inc(hp_ready, 1)
                        pe.wait_ge(hT_ready, j)
                        product(j - 1, r1, hT[1 - b], False).then_inc(ap_ready, 1)

                steps(pe, step)

            @block.scalar
            def _(act):
                act.preload_act_table(ACT.Exp)

                def exp(j, b):
                    act.wait_ge(min_ready, j + 1)
                    act.activation(ex[b][:], ex[b][:], ACT.Exp).then_inc(ex_ready, 1)

                def step(j, r, has):
                    b = r % 2
                    if has(0):
                        act.wait_ge(qp_ready, j + 1)
                        act.copy(fqT[b][:], qp[b][:]).then_inc(fqT_ready, 1)
                    if has(1):
                        act.wait_ge(f_ready, j)
                        act.activation(th[1 - b][:], zr[(r - 1) % RING][:], ACT.Tanh, scale=0.5).then_inc(th_ready, 1)
                        act.wait_ge(hp_ready, j)
                        act.copy(hT[1 - b][:], hp[1 - b][:]).then_inc(hT_ready, 1)
                    if has(-1):
                        exp(j + 1, 1 - b)
                exp(0, 0)
                steps(act, step)

            @block.vector
            def _(ve):
                PER_STEP = (TOPK - 1) + 4 + 3
                place = [0, 0]

                def link(ins):
                    place[1] += 1
                    ins.then_inc(vl, 1)
                    return place[1]

                def need(n):
                    ve.wait_ge(vl, place[0] + n)

                def low(j, b):
                    ve.tensor_scalar(by_head(ex[b]), heads(Q, j), 0.0, None, ALU.min).then_inc(min_ready, 1)

                def step(j, r, has):
                    b, c, r1, r2 = r % 2, 1 - r % 2, (r - 1) % RING, (r - 2) % RING
                    if type(j) is int and j < RING:
                        place[0] += place[1]
                    else:
                        place[0] = whole_steps(j)
                    place[1] = 0
                    z, l, h = zr[r1], lp[c], hs[c]
                    h4 = h[:].rearrange("p (m h d) -> p m h d", m=KD, h=4)

                    def expert(n):
                        wn = WK[:, bass.ds(j - 1, 1), n]
                        return ve.scalar_tensor_tensor(z[:], gt[r1][:, n, :], wn, z[:], ALU.mult, ALU.add)

                    def over_normaliser(m):
                        return link(ve.tensor_tensor(h4[:, m, :, :],
                                                     l[:, m, 0:P].rearrange("p (h d) -> p h d", h=4),
                                                     rz[c][:, m, :].unsqueeze(2).to_broadcast([P, 4, DH]), ALU.mult))

                    if has(0):
                        ve.wait_ge(ex_ready, j + 1)
                        ve.scalar_tensor_tensor(by_head(fq[b]), heads(Q, j), 0.0, by_head(ex[b]), ALU.max, ALU.add
                                                ).then_inc(fq_ready, 1)
                    if has(1):
                        ve.wait_ge(lp_ready, j)
                        bias = link(ve.tensor_scalar(rz[c][:], l[:, :, P:LW], 1e-6, None, ALU.add))
                        ve.wait_ge(rows_in[r1], 12 * (j - 1 - r1) + 48)
                        ve.wait_ge(got[r1], 4 * TOPK * (j - 1 - r1) + 16 * TOPK)
                        z0 = link(expert(0))
                        need(bias)
                        recip = link(ve.reciprocal(rz[c][:], rz[c][:]))
                        need(z0)
                        z1 = link(expert(1))
                        need(recip)
                        over_normaliser(0)
                        m1 = over_normaliser(1)
                        need(z1)
                        z2 = link(expert(2))
                        need(m1)
                        ve.tensor_tensor(by_head(h), heads(K, j - 1), by_head(h), ALU.add).then_inc(hs_ready, 1)
                        need(z2)
                        expert(TOPK - 1).then_inc(f_ready, 1)
                    if has(2):
                        ve.wait_ge(th_ready, j - 1)
                        gate = link(ve.scalar_tensor_tensor(th[b][:], th[b][:], 1.0, zr[r2][:], ALU.add, ALU.mult))
                        ve.wait_ge(ap_ready, j - 1)
                        total = link(ve.tensor_tensor(s1[b][:], ap[b][:], xr[r2][:], ALU.add))
                    if has(-1):
                        low(j + 1, c)
                    if has(2):
                        need(total)
                        part = link(ve.scalar_tensor_tensor(th[b][:], th[b][:], 0.5, s1[b][:], ALU.mult, ALU.mult))
                        if has(4):
                            ve.wait_ge(stored[b], 8 * (j - 2 - b))
                        need(part)
                        ve.tensor_tensor(res[b][:], th[b][:], x1[r2][:], ALU.add).then_inc(res_ready, 1)

                def whole_steps(j):
                    return PER_STEP * j - PER_STEP - 3
                low(0, 0)
                steps(ve, step)


def gated_s4d_then_ripple_moe(nc, x, log_a_re, a_im, c_re, c_im, log_dt, d_skip, ln_w, ln_b, ffn_w, disha,
                              w_qkv, w_o, conv_w, w_gate, w1, w2, w3, ws1, ws2, ws3, out):
    v_dram = nc.dram_tensor("v_powers", (NG, P, 4 * GH * P), BF16, kind="Internal").ap()
    kp_dram = nc.dram_tensor("padded_taps", (D, 2 * P), F32, kind="Internal").ap()
    x1_dram = nc.dram_tensor("x1", (T, D), F32, kind="Internal").ap()
    xn1_dram = nc.dram_tensor("xn1", (T, D), F32, kind="Internal").ap()
    z_dram = nc.dram_tensor("shared_out", (T, D), F32, kind="Internal").ap()
    vt_dram = nc.dram_tensor("v_channels_first", (P, D // P, NJ, P), F32, kind="Internal").ap()
    conv_dram = nc.dram_tensor("convolved", (P, D // P, NJ, P), F32, kind="Internal").ap()
    xs_dram = nc.dram_tensor("slots_in", (SLOTS, D), F32, kind="Internal").ap()
    o_dram = nc.dram_tensor("slots_out", (SLOTS, D), F32, kind="Internal").ap()
    Core.used = []
    with Core(nc) as k:
        ident = k.sb("ident", [P, P])
        with Core(nc) as l0:
            anti, zero = l0.sb("anti", [P, P]), l0.sb("zero", [P, D])
            XN, G0 = l0.sb("XN", [P, NC, D]), l0.sb("G0", [P, NC, D])
            stage_norm_gate0(nc, x, ffn_w, disha, ident, anti, XN, G0, zero, xs_dram)
            with Core(nc) as s4d:
                S = s4d.sb("S", [P, NC, 2, P])
                with Core(nc) as c:
                    turns, KT = c.sb("turns", [P, P]), c.sb("KT", [P, 2, P])
                    WR, WQ = c.sb("WR", [P, 2, P]), c.sb("WQ", [P, 2, P])
                    with Core(nc) as m:
                        DP = m.sb("DP", [P, 7, P])
                        CMH, CML = (m.sb(n, [P, P, 2, 2], BF16) for n in ("CMH", "CML"))
                        MR, MRN, MI = m.sb("MR", [P, P]), m.sb("MRN", [P, P]), m.sb("MI", [P, P])
                        stage_s4d_constants(nc, log_a_re, a_im, c_re, c_im, log_dt, ident, turns, DP, CMH, CML, MR, MRN,
                                            MI, WR, WQ, zero, xs_dram)
                        stage_s4d_states(nc, turns, DP, CMH, CML, MR, MRN, MI, ident, anti, XN, KT, S, v_dram)
                    stage_s4d_scan(nc, WR, WQ, S, KT, ident, kp_dram, zero, xs_dram)
                with Core(nc) as o:
                    Y = o.sb("Y", [P, NC, D])
                    stage_s4d_outputs(nc, S, XN, anti, v_dram, kp_dram, Y)
                    stage_mix0(nc, x, d_skip, ln_w, ln_b, XN, G0, Y, x1_dram, xn1_dram)
        k.recycle()
        with Core(nc) as l1:
            WK = l1.sb("WK", [P, NJ, TOPK])
            SIDX, GIDX = l1.sb("SIDX", [P, NJ, TOPK], U32), l1.sb("GIDX", [P, NJ, TOPK], U32)
            EXP = l1.sb("EXP", [P, NGR], I32)
            KVB = l1.sb("KVB", [P, 2, P + 4])
            Q, K, V = (l1.sb(n, [P, NH, NJ, DH]) for n in "QKV")
            with Core(nc) as g:
                L = g.sb("L", [P, NJ, NE])
                stage_projections(nc, w_qkv, w_gate, ws1, ws2, ws3, xn1_dram, z_dram, vt_dram, ident, Q, K, V, L, KVB)
                stage_routing_and_convolution(nc, conv_w, vt_dram, conv_dram, ident, L, WK, SIDX, GIDX, EXP)
            stage_experts_and_attention(nc, w1, w2, w3, xn1_dram, xs_dram, o_dram, ident, SIDX, EXP, Q, K, V)
            stage_mix1(nc, w_o, xn1_dram, x1_dram, z_dram, o_dram, conv_dram, ident, Q, K, KVB, WK, GIDX,
                       out)


_INS = ['L0_attn_x', 'L0_attn_log_A_real', 'L0_attn_A_imag', 'L0_attn_C_re', 'L0_attn_C_im', 'L0_attn_log_dt',
        'L0_attn_D', 'L0_attn_ln_w', 'L0_attn_ln_b', 'L0_ffn_weight', 'L0_ffn_disha', 'L1_attn_Wqkv', 'L1_attn_Wo',
        'L1_attn_conv_w', 'L1_ffn_Wg', 'L1_ffn_W1', 'L1_ffn_W2', 'L1_ffn_W3', 'L1_ffn_Ws1', 'L1_ffn_Ws2',
        'L1_ffn_Ws3']
_OUTS = [((1, 4096, 256), 'float32')]


def kernel(**inputs):
    import numpy as _np
    import concourse.bacc as _bacc
    from concourse import mybir as _mybir
    from concourse.bass_utils import run_bass_kernel_spmd as _run

    nc = _bacc.Bacc("TRN2", target_bir_lowering=False, num_devices=1)
    arrays, args = {}, []
    for name in _INS:
        a = _np.ascontiguousarray(inputs[name])
        arrays[f"in_{name}_dram"] = a
        args.append(nc.dram_tensor(f"in_{name}_dram", a.shape, _mybir.dt.from_np(a.dtype), kind="ExternalInput").ap())
    for i, (shape, dtype) in enumerate(_OUTS):
        dt = _mybir.dt.from_np(_np.dtype(dtype))
        args.append(nc.dram_tensor(f"out_{i}_dram", shape, dt, kind="ExternalOutput").ap())
    gated_s4d_then_ripple_moe(nc, *args)
    r = _run(nc, [arrays], core_ids=[0])
    return r.results[0]["out_0_dram"]
```
